# Optimizing a Trainium2 kernel written in Bass

```python
import numpy as np
import jax
import jax.numpy as jnp

def _softmax(x, axis=-1):
    return jax.nn.softmax(x, axis=axis)

def _gelu(x):
    return jax.nn.gelu(x, approximate=True)

def _silu(x):
    return jax.nn.silu(x)

def _sigmoid(x):
    return jax.nn.sigmoid(x)

def _layernorm(x, axis=-1, eps=1e-05):
    m = jnp.mean(x, axis=axis, keepdims=True)
    v = jnp.var(x, axis=axis, keepdims=True)
    return (x - m) / jnp.sqrt(v + eps)

def _scatter_add(tgt, idx, src, axis=0):
    return tgt.at[idx].add(src)

def _segment_sum(src, seg, n):
    return jax.ops.segment_sum(src, seg, n)
kernel_name = 'mk_gnn_resnorm_d2_gnn_r8_1b2408'

def setup_inputs(seed: int=0):
    np.random.seed(seed)
    _w = jnp.asarray

    def _rec_inputs():
        import jax
        import jax.numpy as jnp
        _gk = jax.random.key(seed)
        x = -0.0003713 + 1 * jax.random.normal(jax.random.fold_in(_gk, 1), (12500, 128), jnp.float32)
        _s = jax.random.randint(jax.random.fold_in(_gk, 2), (100000,), 0, 12500, jnp.int32)
        _d = jax.random.randint(jax.random.fold_in(_gk, 3), (100000,), 0, 12500, jnp.int32)
        _loop = jnp.arange(12500, dtype=jnp.int32)
        src = jnp.concatenate([_s, _d, _loop])
        dst = jnp.concatenate([_d, _s, _loop])
        _o = jnp.argsort(dst, stable=True)
        src = src[_o]
        dst = dst[_o]
        edge_attr_8 = jax.random.uniform(jax.random.fold_in(_gk, 12), (212500, 8), jnp.float32, 0.0, 1)
        edge_weight1 = 0.00121237 + 1.00026 * jax.random.normal(jax.random.fold_in(_gk, 14), (212500, 1), jnp.float32)
        return (x, src, dst, edge_attr_8, edge_weight1)
    x, src, dst, edge_attr_8, edge_weight1 = _rec_inputs()

    def _L0_gnn_setup():
        import jax, jax.numpy as jnp
        import numpy as np
        N, E = (12500, 200000)
        NODE_DIM, EDGE_DIM, NUM_BASIS, LMAX = (128, 128, 8, 0)
        NUM_SH = (LMAX + 1) ** 2
        key = jax.random.key(seed)
        ks = jax.random.split(key, 12)
        inp = {'node_feats': jax.random.normal(ks[0], (N, NODE_DIM), dtype=jnp.float32), 'edge_index': jax.random.randint(ks[1], (2, E), 0, N, dtype=jnp.int64), 'edge_rbf': jax.random.uniform(ks[2], (E, NUM_BASIS), dtype=jnp.float32), 'edge_sh': jax.random.normal(ks[3], (E, NUM_SH), dtype=jnp.float32), 'W1': jax.random.normal(ks[4], (NUM_BASIS, EDGE_DIM), dtype=jnp.float32) / np.sqrt(NUM_BASIS), 'b1': jnp.zeros((EDGE_DIM,), dtype=jnp.float32), 'W2': jax.random.normal(ks[5], (EDGE_DIM, NODE_DIM * (LMAX + 1)), dtype=jnp.float32) / np.sqrt(EDGE_DIM), 'b2': jnp.zeros((NODE_DIM * (LMAX + 1),), dtype=jnp.float32), 'Wself': jax.random.normal(ks[6], (NODE_DIM, NODE_DIM), dtype=jnp.float32) / np.sqrt(NODE_DIM), 'bself': jnp.zeros((NODE_DIM,), dtype=jnp.float32), 'Wcat': jax.random.normal(ks[7], (2 * NODE_DIM, NODE_DIM), dtype=jnp.float32) / np.sqrt(2 * NODE_DIM), 'bcat': jnp.zeros((NODE_DIM,), dtype=jnp.float32)}
        return inp
    _L0_gnn_all = _L0_gnn_setup()
    _L0_gnn_in = {k: v for k, v in _L0_gnn_all.items() if k in ('W1', 'b1', 'W2', 'b2', 'Wself', 'bself', 'Wcat', 'bcat')}
    del _L0_gnn_all

    def _L1_gnn_setup():
        import jax, jax.numpy as jnp
        import numpy as np
        NUM_STEPS = 1

        def _seg_mean(vals, idx, num_nodes):
            s = jax.ops.segment_sum(vals, idx, num_segments=num_nodes)
            cnt = jax.ops.segment_sum(jnp.ones((vals.shape[0],), vals.dtype), idx, num_segments=num_nodes)
            return s / jnp.maximum(cnt, 1.0)[:, None]

        def _gru_cell(a, h, w_ih, w_hh, b_ih, b_hh):
            gi = a @ w_ih.T + b_ih
            gh = h @ w_hh.T + b_hh
            H = h.shape[1]
            i_r, i_z, i_n = (gi[:, :H], gi[:, H:2 * H], gi[:, 2 * H:])
            h_r, h_z, h_n = (gh[:, :H], gh[:, H:2 * H], gh[:, 2 * H:])
            r = jax.nn.sigmoid(i_r + h_r)
            z = jax.nn.sigmoid(i_z + h_z)
            n = jnp.tanh(i_n + r * h_n)
            return (1.0 - z) * n + z * h
        key = jax.random.key(seed)
        ks = jax.random.split(key, 8)
        N, E, H = (12500, 80000, 128)
        sc = 1.0 / np.sqrt(H)
        feat = jax.random.normal(ks[0], (N, H), jnp.float32)
        src = jax.random.randint(ks[1], (E,), 0, N, jnp.int32)
        dst = jax.random.randint(ks[2], (E,), 0, N, jnp.int32)
        W_in = jax.random.normal(ks[3], (H, H), jnp.float32) * sc
        W_out = jax.random.normal(ks[4], (H, H), jnp.float32) * sc
        w_ih = jax.random.normal(ks[5], (3 * H, 2 * H), jnp.float32) * sc
        w_hh = jax.random.normal(ks[6], (3 * H, H), jnp.float32) * sc
        return {'feat': feat, 'src': src, 'dst': dst, 'W_in': W_in, 'b_in': jnp.zeros((H,), jnp.float32), 'W_out': W_out, 'b_out': jnp.zeros((H,), jnp.float32), 'w_ih': w_ih, 'w_hh': w_hh, 'b_ih': jnp.zeros((3 * H,), jnp.float32), 'b_hh': jnp.zeros((3 * H,), jnp.float32)}
    _L1_gnn_all = _L1_gnn_setup()
    _L1_gnn_in = {k: v for k, v in _L1_gnn_all.items() if k in ('W_in', 'b_in', 'W_out', 'b_out', 'w_ih', 'w_hh', 'b_ih', 'b_hh')}
    del _L1_gnn_all
    return {'x': x, 'src': src, 'dst': dst, 'edge_attr_8': edge_attr_8, 'edge_weight1': edge_weight1, 'L0_gnn_W1': _L0_gnn_in['W1'], 'L0_gnn_b1': _L0_gnn_in['b1'], 'L0_gnn_W2': _L0_gnn_in['W2'], 'L0_gnn_b2': _L0_gnn_in['b2'], 'L0_gnn_Wself': _L0_gnn_in['Wself'], 'L0_gnn_bself': _L0_gnn_in['bself'], 'L0_gnn_Wcat': _L0_gnn_in['Wcat'], 'L0_gnn_bcat': _L0_gnn_in['bcat'], 'L1_gnn_W_in': _L1_gnn_in['W_in'], 'L1_gnn_b_in': _L1_gnn_in['b_in'], 'L1_gnn_W_out': _L1_gnn_in['W_out'], 'L1_gnn_b_out': _L1_gnn_in['b_out'], 'L1_gnn_w_ih': _L1_gnn_in['w_ih'], 'L1_gnn_w_hh': _L1_gnn_in['w_hh'], 'L1_gnn_b_ih': _L1_gnn_in['b_ih'], 'L1_gnn_b_hh': _L1_gnn_in['b_hh']}

def reference(x, src, dst, edge_attr_8, edge_weight1, L0_gnn_W1, L0_gnn_b1, L0_gnn_W2, L0_gnn_b2, L0_gnn_Wself, L0_gnn_bself, L0_gnn_Wcat, L0_gnn_bcat, L1_gnn_W_in, L1_gnn_b_in, L1_gnn_W_out, L1_gnn_b_out, L1_gnn_w_ih, L1_gnn_w_hh, L1_gnn_b_ih, L1_gnn_b_hh):
    import jax
    import jax.numpy as jnp

    def _L0_gnn_ref(node_feats, edge_index, edge_rbf, edge_sh, W1, b1, W2, b2, Wself, bself, Wcat, bcat):
        import jax, jax.numpy as jnp
        import numpy as np
        N, E = (12500, 200000)
        NODE_DIM, EDGE_DIM, NUM_BASIS, LMAX = (128, 128, 8, 0)
        NUM_SH = (LMAX + 1) ** 2
        row, col = (edge_index[0], edge_index[1])
        n_nodes = node_feats.shape[0]
        h = jax.nn.silu(edge_rbf @ W1 + b1)
        weights = (h @ W2 + b2).reshape(-1, NODE_DIM, LMAX + 1)
        node_j = node_feats[col]
        messages = (node_j[:, :, None] * weights).sum(axis=-1)
        aggregated = jax.ops.segment_sum(messages, row, num_segments=n_nodes)
        self_out = node_feats @ Wself + bself
        combined = jnp.concatenate([self_out, aggregated], axis=-1)
        return combined @ Wcat + bcat

    def _L1_gnn_ref(feat, src, dst, W_in, b_in, W_out, b_out, w_ih, w_hh, b_ih, b_hh):
        import jax, jax.numpy as jnp
        import numpy as np
        NUM_STEPS = 1

        def _seg_mean(vals, idx, num_nodes):
            s = jax.ops.segment_sum(vals, idx, num_segments=num_nodes)
            cnt = jax.ops.segment_sum(jnp.ones((vals.shape[0],), vals.dtype), idx, num_segments=num_nodes)
            return s / jnp.maximum(cnt, 1.0)[:, None]

        def _gru_cell(a, h, w_ih, w_hh, b_ih, b_hh):
            gi = a @ w_ih.T + b_ih
            gh = h @ w_hh.T + b_hh
            H = h.shape[1]
            i_r, i_z, i_n = (gi[:, :H], gi[:, H:2 * H], gi[:, 2 * H:])
            h_r, h_z, h_n = (gh[:, :H], gh[:, H:2 * H], gh[:, 2 * H:])
            r = jax.nn.sigmoid(i_r + h_r)
            z = jax.nn.sigmoid(i_z + h_z)
            n = jnp.tanh(i_n + r * h_n)
            return (1.0 - z) * n + z * h
        N = feat.shape[0]
        h = feat
        for _ in range(NUM_STEPS):
            feat_in = h @ W_in.T + b_in
            feat_out = h @ W_out.T + b_out
            a_in = _seg_mean(feat_in[src], dst, N)
            a_out = _seg_mean(feat_out[dst], src, N)
            a = jnp.concatenate((a_in, a_out), axis=1)
            h = _gru_cell(a, h, w_ih, w_hh, b_ih, b_hh)
        return h
    edge_index = jnp.stack([src, dst])
    x = _layernorm(x + _L0_gnn_ref(x, edge_index, edge_attr_8, edge_weight1, L0_gnn_W1, L0_gnn_b1, L0_gnn_W2, L0_gnn_b2, L0_gnn_Wself, L0_gnn_bself, L0_gnn_Wcat, L0_gnn_bcat), axis=-1)
    x = _layernorm(x + _L1_gnn_ref(x, src, dst, L1_gnn_W_in, L1_gnn_b_in, L1_gnn_W_out, L1_gnn_b_out, L1_gnn_w_ih, L1_gnn_w_hh, L1_gnn_b_ih, L1_gnn_b_hh), axis=-1)
    return x

_drawn_inputs = setup_inputs


def setup_inputs(seed=0):
    import zlib

    import numpy as np

    out = dict(_drawn_inputs(seed))
    spreads = {'L0_gnn_b1': (0.0, 0.1),
     'L0_gnn_b2': (0.0, 0.1),
     'L0_gnn_bself': (0.0, 0.1),
     'L0_gnn_bcat': (0.0, 0.1),
     'L1_gnn_b_in': (0.0, 0.32),
     'L1_gnn_b_out': (0.0, 0.1),
     'L1_gnn_b_ih': (0.0, 0.1),
     'L1_gnn_b_hh': (0.0, 0.399)}
    factors = {}
    for name, (base, spread) in spreads.items():
        noise = np.random.default_rng([zlib.crc32(name.encode()), seed]).standard_normal(out[name].shape)
        drawn = base * np.exp(spread * noise) if base else spread * noise
        out[name] = jnp.asarray(drawn.astype(out[name].dtype))
    for name, factor in factors.items():
        out[name] = (out[name] * factor).astype(out[name].dtype)
    return out
```

```python
import concourse.bass as bass
from concourse import mybir
from concourse.alu_op_type import AluOpType as ALU
from contextlib import ExitStack

N, E, D, A = 12500, 212500, 128, 8
P = 128
TG = 8
GE = TG * P
NG = -(-E // GE)
NG += NG % 2
EP = NG * GE
T = NG * TG
NB = -(-N // P)
NPAD = NB * P
NBP = NB + 1
PAD = NPAD
NQ = 104
QE = EP // NQ
QG = QE // GE
RW = 136
U0, U1 = 2 * P, P
V0 = -(-(E // U0 + NB) // 8) * 8
V1 = -(-(E // U1 + NB) // 32) * 32
CW = D + 1
EPS = 1e-5
FORCE_GENERAL = 0


class Steps:

    def __init__(self, eng, sem):
        self.eng, self.sem, self.n, self.it, self.per = eng, sem, 0, None, 0

    def loop(self, it, per):
        self.it, self.per, self.first = it, per, self.n

    def end(self, trips):
        assert self.n - self.first == self.per, (self.n - self.first, self.per)
        self.n, self.it = self.first + trips * self.per, None

    def value(self):
        return self.n if self.it is None else self.it * self.per + self.n

    def wait(self):
        self.eng.wait_ge(self.sem, self.value())

    def mark(self, ins):
        ins.then_inc(self.sem, 1)
        self.n += 1

    def link(self, ins):
        self.mark(ins)
        self.wait()


def need(eng, sem, value):
    if not isinstance(value, int) or value > 0:
        eng.wait_ge(sem, value)


def hold(pool, sem, value):
    if not isinstance(value, int) or value > 0:
        pool.wait_ge(sem, value)
        pool.nop(nofuse=True)


def gnn_kernel(nc, x, src, dst, edge_attr, W1, b1, W2, b2, Wself, bself, Wcat, bcat,
               W_in, b_in, W_out, b_out, w_ih, w_hh, b_ih, b_hh, out):
    f32, i32, bf16 = mybir.dt.float32, mybir.dt.int32, mybir.dt.bfloat16
    ACT, AX = mybir.ActivationFunctionType, mybir.AxisListType

    def dram(name, shape, dt):
        return nc.dram_tensor(name, shape, dt, kind="Internal").ap()

    xwin = dram("xwin", [NPAD + EP, D], f32)
    x1d = dram("x1d", [NPAD, D], f32)
    rows3 = dram("rows3", [NG, 3, GE], bf16)
    winrow = dram("winrow", [T], i32)
    dlist = dram("dlist", [EP, 2], f32)
    dtmp = dram("dtmp", [EP, 2], f32)
    msgs = dram("msgs", [EP, RW], f32)
    vtab = dram("vtab", [6, V1], i32)

    ctx = ExitStack()
    with ctx:
        def sb(name, shape, dt=f32):
            return ctx.enter_context(nc.sbuf_tensor(name, shape, dt))

        def sem(name):
            return ctx.enter_context(nc.semaphore(name))

        acc_a = sb("acc_a", [P, NBP * CW])
        acc_b = sb("acc_b", [P, NBP * CW])
        src_key = sb("src_key", [P, T])
        dst_idx = sb("dst_idx", [P, T], i32)
        base3 = sb("base3", [NBP, T, 3], bf16)
        blk0 = sb("blk0", [P, V0])
        blk1s = sb("blk1s", [P, V1])
        blk1d = sb("blk1d", [P, V1])
        ident = sb("ident", [P, P])
        earlier = sb("earlier", [P, P])
        tri = sb("tri", [P, P])
        iota_row = sb("iota_row", [P, P])
        iota_c = sb("iota_c", [P, 1])
        iota_k = sb("iota_k", [P, NBP], bf16)
        ones = sb("ones", [P, P])
        ones_b = sb("ones_b", [P, P], bf16)
        w1pad = sb("w1pad", [TG * A, TG, D])
        w2s = sb("w2s", [P, D])
        b1c = sb("b1c", [P, 1])
        b2row = sb("b2row", [1, 4, D])
        b2parts = sb("b2parts", [1, 3, D], bf16)
        b2s = sb("b2s", [3, D], bf16)
        wcomb = sb("wcomb", [P, D])
        wbot = sb("wbot", [P, D])
        bias0 = sb("bias0", [1, D])
        m_in = sb("m_in", [P, 3 * D])
        m_out = sb("m_out", [P, 3 * D])
        whh_t = sb("whh_t", [P, 3 * D])
        auxw = sb("auxw", [3, 4 * D])
        mean_var = sb("mean_var", [P, NB, 2])
        deviation = sb("deviation", [P, NB])
        flag_f = sb("flag_f", [P, 2])
        flag_i = sb("flag_i", [P, 2], i32)

        ARENA = 11264
        arena = sb("arena", [P, ARENA])

        def cutter(whole, size):
            at = [0]

            def cut(n, dt=f32):
                words = n if dt != bf16 else -(-n // 2)
                got = whole[:, at[0]:at[0] + words]
                at[0] += words
                assert at[0] <= size, (at[0], size)
                return got if dt == f32 else got.bitcast(dt)
            return cut

        cut = cutter(arena, ARENA)
        win = cut(2 * TG * D).rearrange("p (b j d) -> p b j d", b=2, j=TG)
        rowsb = cut(2 * 2 * GE, bf16).rearrange("p (b r e) -> p b r e", b=2, r=2)
        attr = cut(2 * TG * A).rearrange("p (b c) -> p b c", b=2)
        attr_t = cut(P)
        oht = cut(2 * GE, bf16).rearrange("p (b j e) -> p b j e", b=2, j=TG)
        wsel = cut(GE).rearrange("p (j e) -> p j e", j=TG)
        ht = cut(2 * 4 * P).rearrange("p (h e) -> p h e", h=2)
        xjs = cut(2 * 4 * P).rearrange("p (h e) -> p h e", h=2)
        mrow = cut(2 * TG * RW).rearrange("p (b j c) -> p b j c", b=2, j=TG)
        pos = cut(2 * TG, i32).rearrange("p (b j) -> p b j", b=2)
        junk = cut(TG * P, bf16).rearrange("p (j e) -> p j e", j=TG)
        rank = cut(TG)
        digits = cut(3 * TG).rearrange("p (j c) -> p j c", c=3)
        posf = cut(2 * TG).rearrange("p (s j) -> p s j", s=2)
        drow = cut(TG * 2).rearrange("p (j c) -> p j c", c=2)
        widx = cut(TG, i32)
        cut = cutter(arena, ARENA)
        mtile = cut(8 * 2 * RW).rearrange("p (s i c) -> p s i c", s=8, i=2)
        oh0 = cut(8 * 2 * P).rearrange("p (s i n) -> p s i n", s=8, i=2)
        xblk = cut(2 * P).rearrange("p (b c) -> p b c", b=2)
        xat = cut(2 * 4 * P).rearrange("p (b c) -> p b c", b=2)
        yblk = cut(2 * P).rearrange("p (b c) -> p b c", b=2)
        x1blk = cut(2 * P).rearrange("p (b c) -> p b c", b=2)
        stats = cut(2 * 16).rearrange("p (b c) -> p b c", b=2)
        means = cut(2 * 256).rearrange("p (b c) -> p b c", b=2)
        aux = cut(2 * 4).rearrange("p (b c) -> p b c", b=2)
        rcnt = cut(2 * 4).rearrange("p (b c) -> p b c", b=2)
        gates = cut(2 * 384).rearrange("p (b c) -> p b c", b=2)
        auxt = cut(2 * P).rearrange("p (b c) -> p b c", b=2)
        cut = cutter(arena, ARENA)
        NS = 32
        grow = cut(NS * CW).rearrange("p (s c) -> p s c", s=NS)
        edge2 = cut(NS * 2).rearrange("p (s c) -> p s c", s=NS)
        oh1 = cut(TG * P).rearrange("p (s n) -> p s n", s=TG)

        cut = cutter(acc_a, NBP * CW)
        dst_n = cut(QE, i32)
        src_n = cut(QE, i32)
        next_n = cut(QE, i32)
        tmp_n = cut(QE)
        tile_p = cut(GE, i32)
        rows_n = cut(QG * 3 * GE, bf16).rearrange("p (g r e) -> p g r e", g=QG, r=3)
        cut = cutter(acc_b, NBP * CW)
        base3d = acc_b[0:NBP, 0:T * 3 // 2].bitcast(bf16).rearrange("k (t c) -> k t c", c=3)
        pair_n = cut(QE * 2).rearrange("p (e c) -> p e c", c=2)
        src_p = cut(T, i32)
        dst_p = cut(T, i32)
        hist_s = cut(T)
        hist_d = cut(T)
        brow = cut(7 * D)
        rows_w = cut(2 * 3 * D).rearrange("p (c f) -> p c f", c=2)
        cut = cutter(arena, ARENA)
        onek = cut(4 * TG * NBP, bf16).rearrange("p (s j k) -> p s j k", s=4, j=TG)
        blk_s = cut(T, bf16)
        blk_d = cut(T, bf16)
        sumt = cut(T)
        iota_i = cut(V1, i32)
        wih_n = cut(3 * 2 * D).rearrange("p (c f) -> p c f", c=3)
        whh_n = cut(3 * D).rearrange("p (c f) -> p c f", c=3)
        iota_v = cut(V1)
        wself_n, wself_t, wtop, win_n, wout_n = (cut(D) for _ in range(5))
        wih_t = cut(2 * 3 * D).rearrange("p (d f) -> p d f", d=2)
        cut = cutter(acc_a, NBP * CW)
        ge_start = cut(V1)
        ge_end = cut(V1)
        off_f = cut(V1)
        vrow = cut(2 * V1, i32).rearrange("p (c v) -> p c v", c=2)
        sumt2 = cut(T)
        cols = sb("cols", [P, 3])
        row2 = sb("row2", [1, 4 * D])
        lohi = sb("lohi", [P, 4, QG])
        viol = sb("viol", [P, 2])
        slowrow = sb("slowrow", [P, QG, TG], i32)
        lorow = sb("lorow", [P, 2, QG, TG])
        lorow_i = sb("lorow_i", [P, QG, TG], i32)
        kcol = sb("kcol", [P, 16])
        kcol_i = sb("kcol_i", [P, 2], i32)
        coef = sb("coef", [P, P])

        bank = [ctx.enter_context(nc.psum_tensor(f"bank{i}", [P, 512], f32)) for i in range(8)]

        names = """pads pool_const edges_in weights_in attr_w small_in dve_step act_step pe_weights act_weights dve_weights
        aux_in blocks_ready counted hist_ready flags_sum flag_ready prep_out start_in start_sum tables_sum tables_read
        tables_out prepared window_ready dst_sorted slow_in slow_oht slow_sums slow_rank slow_pos slow_step
        flag_pe x1_out out_done u_stats u_var u_root y_ready g_var g_root agg_sb slow_own reg_dve gru_step list_copied attr_tr attr_sb oht_ready wsel_ready h_ready silu_done sums_ready ranked base_ready pos_ready xj_ready
        xj_sb w_ready msg_ready key_ready acc_zero oh0_ready sum0_ready add0_done x_t xt_sb u_ready u_store
        x1_ready oh1_ready sum1_ready add1_done g_mean g_t g_tsb g_lin g_gate g_cand g_out g_add xcopy pool_step
        gather_own upd_step grow_ones out_final w1_in slow_pool lotab_out reg_done""".split()
        s = {n: sem(n) for n in names}
        win_in = [sem(f"win_in{i}") for i in range(2)]
        rows_in = [sem(f"rows_in{i}") for i in range(2)]
        attr_in = [sem(f"attr_in{i}") for i in range(2)]
        scattered = [sem(f"scattered{i}") for i in range(2)]
        mtile_in = [sem(f"mtile_in{i}") for i in range(8)]
        edge2_in = [sem(f"edge2_in{i}") for i in range(4)]
        gathered = [sem(f"gathered{i}") for i in range(4)]
        xblk_in = [sem(f"xblk_in{i}") for i in range(2)]
        hblk_in = [sem(f"hblk_in{i}") for i in range(2)]
        block = ctx.enter_context(nc.Block())

        LAST = E - (NG - 1) * GE
        LP, LJ = LAST // TG, LAST % TG
        NLAST = E - (NQ - 1) * QE
        N_EDGES = 2 * (2 + (LJ > 0)) + 6
        PASSES = [(U0, V0, blk0, 0), (U1, V1, blk1s, 2), (U1, V1, blk1d, 4)]
        SB = 7
        IT0, IT1, ITU = V0 // 8, V1 // NS, NB // 2
        HCHUNK = 512

        def registers(eng, name, n):
            return [eng.alloc_register(f"{name}{i}") for i in range(n)]

        def load_table(eng, regs, row, v, top):
            eng.load(regs, vtab[row:row + 1, bass.ds(v, len(regs))])
            return [eng.snap(r, min_val=0, max_val=top) for r in regs]

        @block.sync
        def _(sp):
            sp.wait_ge(s["pads"], 5)
            for to, of in ((src_p, src), (dst_p, dst)):
                v = to.rearrange("p (g j) -> p g j", j=TG)
                sp.dma_start(v[:, 0:NG - 1, :], of[0:(NG - 1) * GE].rearrange("(g p j) -> p g j", p=P, j=TG)).then_inc(s["edges_in"], 16)
                sp.dma_start(v[0:LP, NG - 1, :], of[(NG - 1) * GE:(NG - 1) * GE + LP * TG].rearrange("(p j) -> p j", j=TG)).then_inc(s["edges_in"], 16)
                if LJ:
                    sp.dma_start(v[LP:LP + 1, NG - 1, 0:LJ], of[E - LJ:E].rearrange("(p j) -> p j", p=1)).then_inc(s["edges_in"], 16)
            for to, of, shift in ((src_n, src, 0), (dst_n, dst, 0), (next_n, dst, 1)):
                sp.dma_start(to[0:NQ - 1, :], of[shift:shift + (NQ - 1) * QE].rearrange("(q e) -> q e", e=QE)).then_inc(s["edges_in"], 16)
                sp.dma_start(to[NQ - 1:NQ, 0:NLAST - shift], of[(NQ - 1) * QE + shift:E].rearrange("(q e) -> q e", q=1)).then_inc(s["edges_in"], 16)
            sp.dma_start(xwin[0:N, :].rearrange("(a b) d -> a (b d)", a=100), x.rearrange("(a b) d -> a (b d)", a=100)).then_inc(s["xcopy"], 16)
            sp.wait_ge(s["pool_const"], 1)
            sp.dma_start(xwin[N:NPAD, :], coef[0:NPAD - N, :]).then_inc(s["xcopy"], 16)
            sp.wait_ge(s["dve_weights"], 1)
            for j in range(TG):
                sp.dma_start(w1pad[j * A:(j + 1) * A, j, :], W1).then_inc(s["w1_in"], 16)
            sp.wait_ge(s["dve_weights"], 2)
            for c in range(3):
                sp.dma_start(b2s[c:c + 1, :], b2parts[0:1, c, :]).then_inc(s["aux_in"], 16)
            sp.wait_ge(s["dve_weights"], 3)
            sp.wait_ge(s["act_weights"], 8)
            sp.dma_start(auxw[0:1, 0:3 * D], rows_w[0:1, 0, :]).then_inc(s["aux_in"], 16)
            sp.dma_start(auxw[1:2, 0:3 * D], rows_w[0:1, 1, :]).then_inc(s["aux_in"], 16)
            sp.dma_start(auxw[2:3, :], row2[0:1, :]).then_inc(s["aux_in"], 16)
            sp.wait_ge(s["prep_out"], 1)
            sp.dma_start(rows3.rearrange("(q g) r e -> q (g r e)", g=QG), rows_n[0:NQ].rearrange("q g r e -> q (g r e)")).then_inc(s["lotab_out"], 16)
            sp.dma_start(winrow.rearrange("(q c) -> q c", c=QG * TG), lorow_i[0:NQ].rearrange("q g j -> q (g j)")).then_inc(s["lotab_out"], 16)
            sp.dma_start(dlist.rearrange("(q e) c -> q (e c)", e=QE), pair_n[0:NQ].rearrange("q e c -> q (e c)")).then_inc(s["lotab_out"], 16)
            for i, (U, V, _, row) in enumerate(PASSES):
                sp.wait_ge(s["tables_read"], i + 1)
                sp.dma_start(vtab[row:row + 2, 0:V].rearrange("(o c) v -> o c v", o=1), vrow[0:1, :, 0:V]).then_inc(s["tables_out"], 16)
            sp.wait_ge(s["lotab_out"], 48)
            sp.wait_ge(s["xcopy"], 32)

            sp.wait_ge(s["flag_ready"], 1)
            unsorted = sp.value_load(flag_i[0:1, 1:2], min_val=0, max_val=1)
            with sp.If(unsorted):
                with sp.Fori(0, NG) as g:
                    sp.wait_ge(s["slow_pool"], g + 1)
                    sp.dma_start(rowsb[:, 0, 0, :], rows3[bass.ds(g, 1), 2, :].to_broadcast([P, GE])).then_inc(s["slow_in"], 16)
                    sp.dma_start(drow, dlist[bass.ds(g * GE, GE), :].rearrange("(p j) c -> p j c", j=TG)).then_inc(s["slow_in"], 16)

            regs = registers(sp, "sp_win", TG)
            sp.wait_ge(s["window_ready"], 1)
            sp.wait_ge(s["prepared"], 1)

            def edge_loads(it, last=False):
                for b in range(2):
                    g = 2 * it + b
                    sp.load(regs, winrow[bass.ds(g * TG, TG)].rearrange("(o t) -> o t", o=1))
                    need(sp, s["wsel_ready"], g - 1)
                    sp.dma_start(rowsb[:, b, :, :], rows3[bass.ds(g, 1), 0:2, :].to_broadcast([P, 2, GE])).then_inc(rows_in[b], 16)
                    need(sp, s["attr_tr"], g - 1)
                    if last and b == 1:
                        av = attr[:, b, :].rearrange("p (j a) -> p j a", a=A)
                        e0 = (NG - 1) * GE
                        sp.dma_start(attr[0:LP, b, :], edge_attr[e0:e0 + LP * TG, :].rearrange("(p j) a -> p (j a)", j=TG)).then_inc(attr_in[b], 16)
                        k = 16
                        if LJ:
                            sp.dma_start(av[LP:LP + 1, 0:LJ, :], edge_attr[E - LJ:E, :].rearrange("(p j) a -> p j a", p=1)).then_inc(attr_in[b], 16)
                            sp.dma_start(av[LP:LP + 1, LJ:TG, :], edge_attr[0:TG - LJ, :].rearrange("(p j) a -> p j a", p=1)).then_inc(attr_in[b], 16)
                            k += 32
                        r = LP + (LJ > 0)
                        sp.dma_start(attr[r:P, b, :], edge_attr[0:(P - r) * TG, :].rearrange("(p j) a -> p (j a)", j=TG)).then_inc(attr_in[b], 16)
                    else:
                        sp.dma_start(attr[:, b, :], edge_attr[bass.ds(g * GE, GE), :].rearrange("(p j) a -> p (j a)", j=TG)).then_inc(attr_in[b], 16)
                    need(sp, s["xj_ready"], 2 * g - 2)
                    for j in range(TG):
                        r = sp.snap(regs[j], min_val=0, max_val=NPAD + EP - P)
                        sp.dma_start(win[:, b, j, :], xwin[bass.ds(r, P), :]).then_inc(win_in[b], 16)

            edge_loads(0)
            with sp.Fori(1, NG // 2 - 1) as it:
                edge_loads(it)
            edge_loads(NG // 2 - 1, last=True)

            sp.wait_ge(scattered[0], 16 * TG * (NG // 2))
            sp.wait_ge(scattered[1], 16 * TG * (NG // 2))
            sp.wait_ge(s["msg_ready"], 2 * NG)
            regs0 = registers(sp, "sp_row", 8)
            sp.wait_ge(s["tables_out"], 48)

            def row_loads(it):
                offs = load_table(sp, regs0, 0, it * 8, EP - U0)
                for k in range(0, 8, 2):
                    need(sp, s["sum0_ready"], it * 8 + k - 7)
                    sp.dma_start(mtile[:, k, :, :], msgs[bass.ds(offs[k], U0), :].rearrange("(p i) c -> p i c", i=2)).then_inc(mtile_in[k], 16)

            row_loads(0)
            with sp.Fori(1, IT0) as it:
                row_loads(it)

            def update_in(it):
                for b in range(2):
                    nb = 2 * it + b
                    need(sp, s["u_stats"], nb - 1)
                    sp.dma_start(xblk[:, b, :], xwin[bass.ds(nb * P, P), :]).then_inc(xblk_in[b], 16)

            sp.wait_ge(s["add0_done"], V0)
            update_in(0)
            with sp.Fori(1, ITU) as it:
                update_in(it)
            acc_rows = acc_a[:, 0:NB * D].rearrange("p (n d) -> p n d", d=D)
            with sp.Fori(0, NB // SB) as c:
                sp.wait_ge(s["u_store"], c * SB + SB)
                sp.dma_start(x1d[bass.ds(c * (SB * P), SB * P), :].rearrange("(n p) d -> p n d", p=P),
                             acc_rows[:, bass.ds(c * SB, SB), :]).then_inc(s["x1_out"], 16)
            sp.wait_ge(s["x1_out"], 16 * (NB // SB))

            regs1 = registers(sp, "sp_edge", TG)
            sp.wait_ge(s["dst_sorted"], 1)
            for half, row in ((0, 2), (1, 4)):
                first = half * V1 // TG

                def edge2_loads(it):
                    for q in range(4):
                        offs = load_table(sp, regs1, row, it * NS + q * TG, EP - U1)
                        need(sp, s["sum1_ready"], first + it * 4 + q - 3)
                        for k in range(TG):
                            of = msgs[bass.ds(offs[k], U1), D:D + 2] if half == 0 else dlist[bass.ds(offs[k], U1), :]
                            sp.dma_start(edge2[:, q * TG + k, :], of).then_inc(edge2_in[q], 16)

                edge2_loads(0)
                with sp.Fori(1, IT1) as it:
                    edge2_loads(it)

            def gru_in(it):
                for b in range(2):
                    nb = 2 * it + b
                    need(sp, s["g_out"], nb - 1)
                    sp.dma_start(xblk[:, b, :], x1d[bass.ds(nb * P, P), :]).then_inc(hblk_in[b], 16)

            sp.wait_ge(s["add1_done"], 2 * V1)
            gru_in(0)
            with sp.Fori(1, ITU) as it:
                gru_in(it)
            y_rows = acc_b[:, 0:NB * CW].rearrange("p (n c) -> p n c", c=CW)
            with sp.Fori(0, NB // SB - 1) as c:
                sp.wait_ge(s["y_ready"], c * SB + SB)
                sp.dma_start(out[bass.ds(c * (SB * P), SB * P), :].rearrange("(n p) d -> p n d", p=P),
                             y_rows[:, bass.ds(c * SB, SB), 0:D]).then_inc(s["out_done"], 16)
            sp.wait_ge(s["y_ready"], NB)
            at, full = NB - SB, N // P
            sp.dma_start(out[at * P:full * P, :].rearrange("(n p) d -> p n d", p=P), y_rows[:, at:full, 0:D]).then_inc(s["out_done"], 16)
            sp.dma_start(out[full * P:N, :], y_rows[0:N - full * P, full, 0:D]).then_inc(s["out_done"], 16)
            sp.wait_ge(s["out_done"], 16 * (NB // SB + 1))

        @block.gpsimd
        def _(pool):
            st = Steps(pool, s["pool_step"])
            loads = [(w2s[:, :], W2), (wself_n[:, :], Wself), (wtop[:, :], Wcat[0:D, :]), (wbot[:, :], Wcat[D:2 * D, :]),
                     (win_n[:, :], W_in), (wout_n[:, :], W_out), (wih_n, w_ih.rearrange("(c p) f -> p c f", p=P)),
                     (whh_n, w_hh.rearrange("(c p) f -> p c f", p=P)), (b1c[:, :], b1.rearrange("(p o) -> p o", o=1)),
                     (cols[:, 0:1], bself.rearrange("(p o) -> p o", o=1)), (cols[:, 1:2], b_in.rearrange("(p o) -> p o", o=1)),
                     (cols[:, 2:3], b_out.rearrange("(p o) -> p o", o=1)), (b2row[0:1, 0, :], b2.rearrange("(o f) -> o f", o=1)),
                     (brow[0:1, 0:D], bcat.rearrange("(o f) -> o f", o=1)), (brow[0:1, D:4 * D], b_ih.rearrange("(o f) -> o f", o=1)),
                     (brow[0:1, 4 * D:7 * D], b_hh.rearrange("(o f) -> o f", o=1))]
            st.link(pool.memset(coef[:, :], 0.0))
            pool.memset(ones[:, :], 1.0).then_inc(s["pool_const"], 1)
            pool.memset(ones_b[:, :], 1.0).then_inc(s["pool_const"], 1)
            for m, fill, start, op, cm, step in ((ident, 1.0, 0.0, ALU.not_equal, 1, -1), (earlier, 0.0, 1.0, ALU.is_gt, 1, -1),
                                                 (tri, 0.0, 1.0, ALU.is_gt, -1, 1)):
                st.link(pool.memset(m[:, :], start))
                pool.affine_select(out=m[:, :], in_=m[:, :], compare_op=op, fill=fill, base=0, pattern=[[step, P]],
                                   channel_multiplier=cm).then_inc(s["pool_const"], 1)
            pool.iota(iota_i, pattern=[[1, V1]], base=0, channel_multiplier=0).then_inc(s["pool_const"], 1)
            pool.iota(kcol_i[:, 0:1], pattern=[[0, 1]], base=0, channel_multiplier=1).then_inc(s["pool_const"], 1)
            pool.iota(slowrow[0:NQ].rearrange("q g j -> q (g j)"), pattern=[[P, QG * TG]], base=NPAD,
                      channel_multiplier=QG * TG * P).then_inc(s["pool_const"], 1)
            pool.iota(tile_p, pattern=[[1, P], [0, TG]], base=0, channel_multiplier=0).then_inc(s["pool_const"], 1)
            for to, of in loads:
                pool.dma_start(to, of).then_inc(s["weights_in"], 16)

            pool.wait_ge(s["flag_ready"], 1)
            wide = pool.value_load(flag_i[0:1, 0:1], min_val=0, max_val=1)
            with pool.If(wide):
                with pool.Fori(0, NG) as g:
                    pool.tensor_copy(widx, dst_idx[:, bass.ds(g * TG, TG)]).then_inc(s["gather_own"], 1)
                    hold(pool, s["gather_own"], g + 1)
                    for j in range(TG):
                        pool.indirect_dma_start(win[:, 0, j, :], None, x, bass.IndirectOffsetOnAxis(ap=widx[:, j:j + 1], axis=0)).then_inc(s["slow_step"], 16)
                    hold(pool, s["slow_step"], g * (16 * (TG + 1)) + 16 * TG)
                    pool.dma_start(xwin[bass.ds(g * GE + NPAD, GE), :].rearrange("(j p) d -> p j d", p=P), win[:, 0, :, :]).then_inc(s["slow_step"], 16)
                    hold(pool, s["slow_step"], g * (16 * (TG + 1)) + 16 * (TG + 1))
            unsorted = pool.value_load(flag_i[0:1, 1:2], min_val=0, max_val=1)
            with pool.If(unsorted):
                with pool.Fori(0, NG) as g:
                    hold(pool, s["slow_pos"], g + 1)
                    hold(pool, s["slow_in"], g * 32 + 32)
                    for j in range(TG):
                        pool.indirect_dma_start(dtmp, bass.IndirectOffsetOnAxis(ap=pos[:, 0, j:j + 1], axis=0), drow[:, j, :], None).then_inc(s["reg_done"], 16)
                    hold(pool, s["reg_done"], g * (16 * TG) + 16 * TG)
                    pool.sem_inc(s["slow_pool"], 1)
                pool.dma_start(dlist.rearrange("(q e) c -> q (e c)", e=QE), dtmp.rearrange("(q e) c -> q (e c)", e=QE)).then_inc(s["list_copied"], 16)
                hold(pool, s["list_copied"], 16)
            pool.sem_inc(s["window_ready"], 1)
            pool.sem_inc(s["dst_sorted"], 1)

            def scatters(it):
                for b in range(2):
                    g = 2 * it + b
                    hold(pool, s["pos_ready"], g + 1)
                    hold(pool, s["key_ready"], 2 * g + 2)
                    hold(pool, s["msg_ready"], 2 * g + 2)
                    for j in range(TG):
                        pool.indirect_dma_start(msgs, bass.IndirectOffsetOnAxis(ap=pos[:, b, j:j + 1], axis=0), mrow[:, b, j, :], None).then_inc(scattered[b], 16)

            with pool.Fori(0, NG // 2) as it:
                scatters(it)

            pool.wait_ge(s["x1_out"], 16 * (NB // SB))
            hold(pool, s["grow_ones"], 1)
            for half in range(2):
                with pool.Fori(0, IT1) as it:
                    for q in range(4):
                        hold(pool, edge2_in[q], 16 * TG * (it + half * IT1 + 1))
                        for k in range(TG):
                            sl = q * TG + k
                            pool.indirect_dma_start(grow[:, sl, 0:D], None, x1d, bass.IndirectOffsetOnAxis(ap=edge2[:, sl, 1:2].bitcast(i32), axis=0)).then_inc(gathered[q], 16)

        @block.scalar
        def _(act):
            def copy_out(i, to, of):
                act.wait_ge(s["pe_weights"], i)
                nc.scalar.activation(to, of, ACT.Copy).then_inc(s["act_weights"], 1)

            copy_out(1, wself_t[:, :], bank[0][:, 0:D])
            for d in range(2):
                copy_out(2 + d, wih_t[:, d, :], bank[2 + d][:, 0:3 * D])
            copy_out(4, whh_t[:, :], bank[4][:, 0:3 * D])
            copy_out(5, wcomb[:, :], bank[1][:, 0:D])
            copy_out(6, m_in[:, :], bank[5][:, 0:3 * D])
            copy_out(7, m_out[:, :], bank[6][:, 0:3 * D])
            act.wait_ge(s["pe_weights"], 9)
            nc.scalar.activation(rows_w[0:1, 0, :], bank[7][0:1, 0:3 * D], ACT.Copy)
            nc.scalar.activation(rows_w[0:1, 1, :], bank[0][0:1, 0:3 * D], ACT.Copy).then_inc(s["act_weights"], 1)
            for i, hist in enumerate((hist_s, hist_d)):
                act.wait_ge(s["counted"], 2 * NG)
                for c in range(0, T, HCHUNK):
                    w = min(HCHUNK, T - c)
                    last = nc.scalar.activation(hist[0:NBP, c:c + w], bank[4 * i + c // HCHUNK][0:NBP, 0:w], ACT.Copy)
                    last.then_inc(s["hist_ready"], 1)

            def edge_group(it):
                for b in range(2):
                    g = 2 * it + b
                    need(act, scattered[b], it * 16 * TG)
                    act.nop(nofuse=True)
                    nc.scalar.activation(mrow[:, b, :, D:D + 1].rearrange("p j c -> p (j c)"), src_key[:, bass.ds(g * TG, TG)], ACT.Copy).then_inc(s["key_ready"], 1)
                    nc.scalar.activation(mrow[:, b, :, D + 1:D + 2].rearrange("p j c -> p (j c)").bitcast(i32), dst_idx[:, bass.ds(g * TG, TG)], ACT.Copy).then_inc(s["key_ready"], 1)
                    act.wait_ge(s["attr_tr"], g + 1)
                    need(act, s["h_ready"], 2 * g)
                    nc.scalar.activation(attr_t[0:TG * A, :], bank[7][0:TG * A, 0:P], ACT.Copy).then_inc(s["attr_sb"], 1)
                    for h in range(2):
                        act.wait_ge(s["h_ready"], 2 * g + h + 1)
                        need(act, s["w_ready"], 2 * g + h - 1)
                        nc.scalar.activation(ht[:, h, :], bank[h][:, :], ACT.Silu, bias=b1c[:, 0:1]).then_inc(s["silu_done"], 1)
                    for h in range(2):
                        act.wait_ge(s["xj_ready"], 2 * g + h + 1)
                        need(act, s["msg_ready"], 2 * g + h - 1)
                        nc.scalar.activation(xjs[:, h, :], bank[4 + h][:, :], ACT.Copy).then_inc(s["xj_sb"], 1)

            act.wait_ge(s["prepared"], 1)
            edge_group(0)
            with act.Fori(1, NG // 2) as it:
                edge_group(it)

            regs0 = registers(act, "act_row", 8)
            act.wait_ge(s["tables_out"], 48)
            for b in range(2):
                act.wait_ge(scattered[b], 16 * TG * (NG // 2))
            act.wait_ge(s["msg_ready"], 2 * NG)

            def row_loads(it):
                offs = load_table(act, regs0, 0, it * 8, EP - U0)
                for k in range(1, 8, 2):
                    need(act, s["sum0_ready"], it * 8 + k - 7)
                    act.dma_start(mtile[:, k, :, :], msgs[bass.ds(offs[k], U0), :].rearrange("(p i) c -> p i c", i=2)).then_inc(mtile_in[k], 16)

            row_loads(0)
            with act.Fori(1, IT0) as it:
                row_loads(it)

            act.wait_ge(s["add0_done"], V0)

            def update(it):
                for b in range(2):
                    nb = 2 * it + b
                    need(act, s["x_t"], nb - 1)
                    act.nop(nofuse=True)
                    nc.scalar.activation(gates[:, b, 0:D], acc_a[:, bass.ds(nb * D, D)], ACT.Copy).then_inc(s["agg_sb"], 1)
                for b in range(2):
                    nb = 2 * it + b
                    act.wait_ge(s["x_t"], nb + 1)
                    need(act, s["u_ready"], nb - 1)
                    nc.scalar.activation(xat[:, b, 0:2 * P], bank[b][:, 0:2 * P], ACT.Copy).then_inc(s["xt_sb"], 1)

            update(0)
            with act.Fori(1, ITU) as it:
                update(it)

            def root(ready, done):
                act.wait_ge(ready, 1)
                nc.scalar.activation(deviation[:, :], deviation[:, :], ACT.Sqrt).then_inc(done, 1)

            root(s["u_var"], s["u_root"])

            def gru(it):
                for b in range(2):
                    nb = 2 * it + b
                    act.wait_ge(s["g_t"], nb + 1)
                    need(act, s["g_lin"], nb - 1)
                    nc.scalar.activation(xat[:, b, 0:3 * P], bank[b][:, 0:3 * P], ACT.Copy)
                    nc.scalar.activation(auxt[0:3, b, :], bank[b][0:3, 3 * P:4 * P], ACT.Copy).then_inc(s["g_tsb"], 1)
                for b in range(2):
                    nb = 2 * it + b
                    act.wait_ge(s["g_lin"], nb + 1)
                    need(act, s["g_out"], nb - 1)
                    nc.scalar.activation(gates[:, b, 0:2 * D], bank[2 + b][:, D:3 * D], ACT.Sigmoid).then_inc(s["g_gate"], 1)
                for b in range(2):
                    nb = 2 * it + b
                    act.wait_ge(s["g_cand"], nb + 1)
                    nc.scalar.activation(gates[:, b, 2 * D:3 * D], gates[:, b, 2 * D:3 * D], ACT.Tanh).then_inc(s["g_add"], 1)

            gru(0)
            with act.Fori(1, ITU) as it:
                gru(it)
            root(s["g_var"], s["g_root"])

        @block.vector
        def _(dve):
            v = nc.vector
            st = Steps(dve, s["dve_step"])
            v.memset(src_p[:, T - TG:T], PAD).then_inc(s["pads"], 1)
            v.memset(dst_p[:, T - TG:T], PAD).then_inc(s["pads"], 1)
            for t in (src_n, dst_n, next_n):
                v.memset(t[96:NQ, :], PAD).then_inc(s["pads"], 1)
            v.memset(w1pad[:, :, :], 0.0).then_inc(s["dve_weights"], 1)
            dve.wait_ge(s["pool_const"], 9)
            st.mark(v.tensor_copy(iota_row[:, :], iota_i[:, 0:P]))
            st.mark(v.tensor_copy(iota_v[:, :], iota_i))
            st.link(v.tensor_copy(iota_c[:, :], kcol_i[:, 0:1]))
            st.link(v.tensor_copy(iota_k[:, :], iota_v[:, 0:NBP]))
            dve.wait_ge(s["weights_in"], 16 * 16)
            for c in range(3):
                st.link(v.tensor_copy(b2parts[0:1, c, :], b2row[0:1, c, :]))
                if c < 2:
                    st.link(v.tensor_tensor(b2row[0:1, c + 1, :], b2row[0:1, c, :], b2parts[0:1, c, :], ALU.subtract))
            dve.sem_inc(s["dve_weights"], 1)
            v.memset(auxw[:, :], 0.0)
            v.tensor_copy(row2[0:1, 0:D], brow[0:1, 3 * D:4 * D])
            v.tensor_tensor(row2[0:1, D:3 * D], brow[0:1, D:3 * D], brow[0:1, 4 * D:6 * D], ALU.add)
            st.link(v.tensor_copy(row2[0:1, 3 * D:4 * D], brow[0:1, 6 * D:7 * D]))
            dve.wait_ge(s["pe_weights"], 8)
            st.link(v.tensor_tensor(bias0[0:1, :], bank[2][0:1, 3 * D:4 * D], brow[0:1, 0:D], ALU.add))
            dve.sem_inc(s["dve_weights"], 1)

            dve.wait_ge(s["edges_in"], 16 * N_EDGES)
            st.mark(v.tensor_copy(src_key[:, :], src_p))
            st.link(v.tensor_scalar(dst_idx[:, :], dst_p, float(N - 1), None, ALU.min))
            st.mark(v.tensor_scalar(src_p, src_p, 7, None, ALU.logical_shift_right))
            st.link(v.tensor_scalar(dst_p, dst_p, 7, None, ALU.logical_shift_right))
            st.mark(v.tensor_copy(blk_s, src_p))
            st.link(v.tensor_copy(blk_d, dst_p))
            def onehots(it):
                for b in range(2):
                    g = 2 * it + b
                    for i, blk in enumerate((blk_s, blk_d)):
                        need(dve, s["counted"], 2 * g + i - 3)
                        v.tensor_tensor(onek[:, 2 * b + i, :, :], blk[:, bass.ds(g * TG, TG)].rearrange("p (j o) -> p j o", o=1).to_broadcast([P, TG, NBP]),
                                        iota_k[:, :].rearrange("p (o k) -> p o k", o=1).to_broadcast([P, TG, NBP]), ALU.is_equal).then_inc(s["blocks_ready"], 1)

            onehots(0)
            with dve.Fori(1, NG // 2) as it:
                onehots(it)

            Q = slice(0, NQ)
            pair_i = pair_n.bitcast(i32)
            st.mark(v.tensor_copy(pair_n[Q, :, 0], dst_n[Q, :]))
            st.mark(v.tensor_scalar(pair_i[Q, :, 1], src_n[Q, :], float(N - 1), None, ALU.min))
            st.link(v.tensor_tensor(tmp_n[Q, :], next_n[Q, :], dst_n[Q, :], ALU.is_lt))
            st.link(v.tensor_reduce(viol[Q, 1:2], tmp_n[Q, :], AX.X, ALU.add))
            dw = tmp_n.rearrange("p (g e) -> p g e", g=QG)
            st.link(v.tensor_scalar(tmp_n[Q, :], dst_n[Q, :], float(N - 1), None, ALU.min))
            st.mark(v.tensor_reduce(lohi[Q, 0, :], dw[Q], AX.X, ALU.min))
            st.link(v.tensor_reduce(lohi[Q, 1, :], dw[Q], AX.X, ALU.max))
            st.link(v.tensor_scalar(lohi[Q, 0, :], lohi[Q, 0, :], float(N - P), None, ALU.min))
            st.link(v.tensor_tensor(lohi[Q, 2, :], lohi[Q, 1, :], lohi[Q, 0, :], ALU.subtract))
            st.link(v.tensor_scalar(lohi[Q, 3, :], lohi[Q, 2, :], float(P), None, ALU.is_ge))
            st.link(v.tensor_reduce(viol[Q, 0:1], lohi[Q, 3, :], AX.X, ALU.add))
            dve.sem_inc(s["flags_sum"], 1)
            st.mark(v.tensor_scalar(src_n[Q, :], src_n[Q, :], 7, None, ALU.logical_shift_right))
            st.link(v.tensor_scalar(dst_n[Q, :], dst_n[Q, :], 7, None, ALU.logical_shift_right))
            st.mark(v.tensor_copy(rows_n[Q, :, 0, :], src_n[Q, :].rearrange("p (g e) -> p g e", g=QG)))
            st.mark(v.tensor_copy(rows_n[Q, :, 2, :], dst_n[Q, :].rearrange("p (g e) -> p g e", g=QG)))
            lo_b = lohi[Q, 0, :].rearrange("p (g o) -> p g o", o=1)
            st.link(v.tensor_tensor(dw[Q], dw[Q], lo_b.to_broadcast([NQ, QG, GE]), ALU.subtract))
            dve.wait_ge(s["flag_pe"], 1)
            st.link(v.tensor_scalar(flag_f[:, :], bank[1][:, 0:2], -1.0 if FORCE_GENERAL else 0.5, None, ALU.is_gt))
            st.link(v.tensor_copy(flag_i[:, :], flag_f[:, :]))
            dve.sem_inc(s["flag_ready"], 1)
            nx = next_n.bitcast(f32).rearrange("p (g e) -> p g e", g=QG)
            for g in range(QG):
                st.link(v.tensor_tensor(nx[Q, g, :], tile_p[Q, :], dw[Q, g, :], ALU.subtract))
                st.link(v.scalar_tensor_tensor(rows_n[Q, g, 1, :], nx[Q, g, :], flag_f[Q, 0:1], dw[Q, g, :], ALU.mult, ALU.add))
            lo_t = lo_b.to_broadcast([NQ, QG, TG])
            st.link(v.tensor_tensor(lorow[Q, 0], slowrow[Q], lo_t, ALU.subtract))
            st.link(v.tensor_copy(lorow[Q, 1], lo_t))
            st.link(v.scalar_tensor_tensor(lorow_i[Q], lorow[Q, 0], flag_f[Q, 0:1], lorow[Q, 1], ALU.mult, ALU.add))
            dve.sem_inc(s["prep_out"], 1)

            def running(stp, hist, a, b):
                cur, other = hist[0:NBP, :], a
                d = 1
                while d < T:
                    stp.mark(v.tensor_copy(other[:, 0:d], cur[:, 0:d]))
                    stp.link(v.tensor_tensor(other[:, d:T], cur[:, d:T], cur[:, 0:T - d], ALU.add))
                    cur, other = other, (b if other is a else a)
                    d *= 2
                return cur, other

            def first_places(stp, hist, total, spare, start, to):
                stp.link(v.tensor_tensor(spare, total, hist[0:NBP, :], ALU.subtract))
                whole = total.bitcast(i32)
                stp.link(v.tensor_scalar(whole, spare, start, None, ALU.add))
                digit = spare.bitcast(i32)
                for c in range(3):
                    stp.link(v.tensor_scalar(digit, whole, 7 * c, 127, ALU.logical_shift_right, ALU.bitwise_and))
                    stp.link(v.tensor_copy(to[:, :, c], digit))

            dve.wait_ge(s["hist_ready"], 2 * -(-T // HCHUNK))
            dve.wait_ge(s["lotab_out"], 48)
            dve.wait_ge(s["xcopy"], 32)
            sa, sb_ = sumt[0:NBP, :], sumt2[0:NBP, :]
            total, spare = running(st, hist_s, sa, sb_)
            st.mark(v.tensor_copy(kcol[0:NBP, 0:1], total[:, T - 1:T]))
            st.link(v.tensor_reduce(kcol[0:NBP, 1:2], hist_d[0:NBP, :], AX.X, ALU.add))
            dve.sem_inc(s["start_in"], 1)
            dve.wait_ge(s["start_sum"], 1)
            st.link(v.tensor_copy(kcol[0:NBP, 2:4], bank[0][0:NBP, 0:2]))
            first_places(st, hist_s, total, spare, kcol[0:NBP, 2:3], base3)
            for i, (U, V, blk, row) in enumerate(PASSES):
                k = 1 if row == 4 else 0
                cnt, start = kcol[0:NB, k:k + 1], kcol[0:NB, 2 + k:3 + k]
                nv, vfirst, vend, co = (kcol[0:NB, c:c + 1] for c in (4, 5, 6, 7))
                st.link(v.tensor_scalar(kcol_i[0:NB, 0:1], cnt, float(U - 1), None, ALU.add))
                st.link(v.tensor_scalar(kcol_i[0:NB, 1:2], kcol_i[0:NB, 0:1], U.bit_length() - 1, None, ALU.logical_shift_right))
                st.link(v.tensor_copy(nv, kcol_i[0:NB, 1:2]))
                dve.sem_inc(s["start_in"], 1)
                dve.wait_ge(s["start_sum"], 2 + i)
                st.link(v.tensor_copy(vfirst, bank[0][0:NB, 2:3]))
                st.link(v.tensor_tensor(vend, vfirst, nv, ALU.add))
                st.link(v.scalar_tensor_tensor(co, vfirst, -float(U), start, ALU.mult, ALU.add))
                st.link(v.tensor_scalar(coef[0:NB, :], ones[0:NB, :], co, None, ALU.mult))
                st.mark(v.tensor_scalar(ge_end[0:NB, 0:V], iota_v[0:NB, 0:V], vend, None, ALU.is_ge))
                st.link(v.tensor_scalar(ge_start[0:NB, 0:V], iota_v[0:NB, 0:V], vfirst, None, ALU.is_ge))
                st.link(v.tensor_tensor(ge_start[0:NB, 0:V], ge_start[0:NB, 0:V], ge_end[0:NB, 0:V], ALU.subtract))
                dve.sem_inc(s["start_in"], 1)
                for c in range(0, V, HCHUNK):
                    w = min(HCHUNK, V - c)
                    dve.wait_ge(s["tables_sum"], sum(-(-p[1] // HCHUNK) for p in PASSES[:i]) + c // HCHUNK + 1)
                    st.mark(v.tensor_scalar(blk[:, c:c + w], bank[c // HCHUNK][:, 0:w], float(P), None, ALU.mult))
                    if i and c == 0:
                        dve.wait_ge(s["tables_out"], 16 * i)
                    scale = float(D if row == 0 else CW)
                    st.mark(v.tensor_scalar(vrow[:, 1, c:c + w], bank[c // HCHUNK][:, 0:w], scale, None, ALU.mult))
                    st.link(v.scalar_tensor_tensor(off_f[:, c:c + w], iota_v[:, c:c + w], float(U), bank[4 + c // HCHUNK][:, 0:w], ALU.mult, ALU.add))
                    st.link(v.tensor_scalar(vrow[:, 0, c:c + w], off_f[:, c:c + w], float(EP - U), None, ALU.min))
                dve.sem_inc(s["tables_read"], 1)

            unsorted = dve.value_load(flag_i[0:1, 1:2], min_val=0, max_val=1)

            def places(stp, g, b, oht_b, bas, sums_sem, sums_at, base_sem, base_at, done_sem):
                for h in range(2):
                    dve.wait_ge(sums_sem, sums_at + h)
                    for k in range(4):
                        j = 4 * h + k
                        last = v.tensor_tensor_reduce(out=junk[:, j, :], in0=bank[6][:, k * P:(k + 1) * P], in1=earlier[:, :], scale=1.0,
                                                      scalar=0.0, op0=ALU.mult, op1=ALU.add, accum_out=rank[:, j:j + 1])
                    last.then_inc(done_sem, 1)
                dve.wait_ge(base_sem, base_at)
                dve.wait_ge(done_sem, sums_at + 1)
                stp.link(v.tensor_copy(digits.rearrange("p j c -> p (j c)"), bank[7][:, P:P + 3 * TG]))
                stp.link(v.scalar_tensor_tensor(posf[:, 0, :], digits[:, :, 1], float(P), digits[:, :, 0], ALU.mult, ALU.add))
                stp.link(v.scalar_tensor_tensor(posf[:, 1, :], digits[:, :, 2], float(P * P), posf[:, 0, :], ALU.mult, ALU.add))
                return v.tensor_tensor(pos[:, b, :], posf[:, 1, :], rank, ALU.add)

            with dve.If(unsorted):
                ss = Steps(dve, s["slow_rank"])
                tot, spr = running(ss, hist_d, sa, sb_)
                first_places(ss, hist_d, tot, spr, kcol[0:NBP, 3:4], base3d)
                dve.sem_inc(s["slow_pool"], 1)
                per = 4
                with dve.Fori(0, NG) as g:
                    ss.loop(g, per)
                    dve.wait_ge(s["slow_in"], g * 32 + 32)
                    v.tensor_scalar(oht[:, 0, :, :], rowsb[:, 0, 0, :].rearrange("p (e j) -> p j e", j=TG), iota_c[:, :], None, ALU.is_equal).then_inc(s["slow_oht"], 1)
                    ss.mark(places(ss, g, 0, None, None, s["slow_sums"], g * 2 + 1, s["slow_sums"], g * 2 + 2, s["slow_own"]))
                    ss.wait()
                    dve.sem_inc(s["slow_pos"], 1)
                    ss.end(NG)
                    ss.it = None

            dve.wait_ge(s["tables_out"], 48)
            st.mark(v.memset(acc_a[:, :], 0.0))
            dve.wait_ge(s["aux_in"], 16 * 6)
            st.mark(v.memset(acc_b[:, :], 0.0))
            dve.wait_ge(s["window_ready"], 1)
            st.link(v.memset(mrow[:, :, :, :], 0.0))
            dve.sem_inc(s["prepared"], 1)

            ls = Steps(dve, s["reg_dve"])

            def edge_group(it):
                for b in range(2):
                    g = 2 * it + b
                    dve.wait_ge(rows_in[b], it * 16 + 16)
                    need(dve, s["sums_ready"], 2 * g - 2)
                    v.tensor_scalar(oht[:, b, :, :], rowsb[:, b, 0, :].rearrange("p (e j) -> p j e", j=TG), iota_c[:, :], None, ALU.is_equal).then_inc(s["oht_ready"], 1)
                    need(dve, s["xj_ready"], 2 * g)
                    v.tensor_scalar(wsel, rowsb[:, b, 1, :].rearrange("p (e j) -> p j e", j=TG), iota_c[:, :], None, ALU.is_equal).then_inc(s["wsel_ready"], 1)
                    need(dve, scattered[b], it * 16 * TG)
                    places(ls, g, b, None, None, s["sums_ready"], 2 * g + 1, s["base_ready"], g + 1, s["ranked"]).then_inc(s["pos_ready"], 1)
                    for h in range(2):
                        dve.wait_ge(s["w_ready"], 2 * g + h + 1)
                        dve.wait_ge(s["xj_sb"], 2 * g + h + 1)
                        v.tensor_tensor(mrow[:, b, 4 * h:4 * h + 4, 0:D], bank[2 + h][:, :].rearrange("p (j d) -> p j d", j=4),
                                        xjs[:, h, :].rearrange("p (j d) -> p j d", j=4), ALU.mult).then_inc(s["msg_ready"], 1)

            ls.loop(0, 6)
            edge_group(0)
            ls.n = 0
            with dve.Fori(1, NG // 2) as it:
                ls.loop(it, 6)
                edge_group(it)
            ls.it = None

            regs0 = registers(dve, "dve_blk", 8)

            def sums0(it):
                at = load_table(dve, regs0, 1, it * 8, NB * D)
                for k in range(8):
                    dve.wait_ge(mtile_in[k], it * 16 + 16)
                    for i in range(2):
                        last = v.tensor_scalar(oh0[:, k, i, :], iota_row[:, :], blk0[:, bass.ds(it * 8 + k, 1)], mtile[:, k, i, D:D + 1], ALU.add, ALU.is_equal)
                    last.then_inc(s["oh0_ready"], 1)
                for k in range(8):
                    dve.wait_ge(s["sum0_ready"], it * 8 + k + 1)
                    need(dve, s["add0_done"], it * 8 + k)
                    a = acc_a[:, bass.ds(at[k], D)]
                    v.tensor_tensor(a, a, bank[k][:, 0:D], ALU.add).then_inc(s["add0_done"], 1)

            sums0(0)
            with dve.Fori(1, IT0) as it:
                sums0(it)

            us = Steps(dve, s["upd_step"])

            def moments(stp, b, nb, y):
                dve.nop(nofuse=True)
                stp.link(v.bn_stats(stats[:, b, 0:6], y))
                dve.nop(nofuse=True)
                stp.link(v.bn_aggr(stats[:, b, 6:8], stats[:, b, 0:6]))
                dve.nop(nofuse=True)
                return v.tensor_copy(mean_var[:, bass.ds(nb, 1), :].rearrange("p n c -> p (n c)"), stats[:, b, 6:8])

            def normalized(stp, acc, width, ready, done, out_ready):
                stp.link(v.tensor_scalar(deviation[:, :], mean_var[:, :, 1], EPS, None, ALU.add))
                dve.sem_inc(ready, 1)
                dve.wait_ge(done, 1)
                stp.link(v.reciprocal(deviation[:, :], deviation[:, :]))
                with dve.Fori(0, ITU) as it:
                    for b in range(2):
                        nb = 2 * it + b
                        y = acc[:, bass.ds(nb * width, D)]
                        v.tensor_scalar(y, y, mean_var[:, bass.ds(nb, 1), 0], deviation[:, bass.ds(nb, 1)], ALU.subtract, ALU.mult).then_inc(out_ready, 1)

            def update(it):
                for b in range(2):
                    nb = 2 * it + b
                    dve.wait_ge(s["u_ready"], nb + 1)
                    y = acc_a[:, bass.ds(nb * D, D)]
                    us.link(v.tensor_tensor(y, xblk[:, b, :], bank[2 + b][:, 0:D], ALU.add))
                    moments(us, b, nb, y).then_inc(s["u_stats"], 1)

            us.loop(0, 6)
            update(0)
            us.n = 0
            with dve.Fori(1, ITU) as it:
                us.loop(it, 6)
                update(it)
                us.end(ITU)
            dve.wait_ge(s["u_stats"], NB)
            normalized(us, acc_a, D, s["u_var"], s["u_root"], s["u_store"])
            dve.wait_ge(s["x1_out"], 16 * (NB // SB))
            dve.wait_ge(s["x_t"], NB)
            v.memset(grow[:, :, D:CW], 1.0).then_inc(s["grow_ones"], 1)
            us.link(v.memset(acc_a[:, :], 0.0))
            regs1 = registers(dve, "dve_blk1", TG)
            for half, (row, blk, acc) in enumerate(((3, blk1s, acc_b), (5, blk1d, acc_a))):
                v0 = half * V1

                def sums1(it):
                    for q in range(4):
                        at = load_table(dve, regs1, row, it * NS + q * TG, NB * CW)
                        dve.wait_ge(edge2_in[q], 16 * TG * (it + half * IT1 + 1))
                        need(dve, s["sum1_ready"], half * V1 // TG + it * 4 + q)
                        for k in range(TG):
                            last = v.tensor_scalar(oh1[:, k, :], iota_row[:, :], blk[:, bass.ds(it * NS + q * TG + k, 1)], edge2[:, q * TG + k, 0:1], ALU.add, ALU.is_equal)
                        last.then_inc(s["oh1_ready"], 1)
                        dve.wait_ge(s["sum1_ready"], half * V1 // TG + it * 4 + q + 1)
                        for k in range(TG):
                            need(dve, s["add1_done"], v0 + it * NS + q * TG + k)
                            a = acc[:, bass.ds(at[k], CW)]
                            v.tensor_tensor(a, a, bank[k // 2][:, (k % 2) * 256:(k % 2) * 256 + CW], ALU.add).then_inc(s["add1_done"], 1)

                sums1(0)
                with dve.Fori(1, IT1) as it:
                    sums1(it)

            def gru(it):
                for b in range(2):
                    nb = 2 * it + b
                    need(dve, s["g_t"], nb - 1)
                    for c, acc in ((0, acc_a), (1, acc_b)):
                        cnt = acc[:, bass.ds(nb * CW + D, 1)]
                        v.tensor_scalar(aux[:, b, c:c + 1], cnt, 1.0, None, ALU.min)
                        gs.mark(v.tensor_scalar(rcnt[:, b, c:c + 1], cnt, 1.0, None, ALU.max))
                    v.memset(aux[:, b, 2:3], 1.0)
                    gs.wait()
                    gs.link(v.reciprocal(rcnt[:, b, 2:4], rcnt[:, b, 0:2]))
                    for c, acc in ((0, acc_a), (1, acc_b)):
                        last = v.tensor_scalar(means[:, b, c * D:(c + 1) * D], acc[:, bass.ds(nb * CW, D)], rcnt[:, b, 2 + c:3 + c], None, ALU.mult)
                    last.then_inc(s["g_mean"], 1)
                for b in range(2):
                    nb = 2 * it + b
                    dve.wait_ge(s["g_gate"], nb + 1)
                    ng = gates[:, b, 2 * D:3 * D]
                    gs.link(v.tensor_tensor(ng, gates[:, b, 0:D], bank[2 + b][:, 3 * D:4 * D], ALU.mult))
                    gs.link(v.tensor_tensor(ng, ng, bank[2 + b][:, 0:D], ALU.add))
                    dve.sem_inc(s["g_cand"], 1)
                for b in range(2):
                    nb = 2 * it + b
                    dve.wait_ge(s["g_add"], nb + 1)
                    ng, h = gates[:, b, 2 * D:3 * D], xblk[:, b, :]
                    gs.link(v.tensor_tensor(yblk[:, b, :], h, ng, ALU.subtract))
                    gs.link(v.tensor_tensor(yblk[:, b, :], yblk[:, b, :], gates[:, b, D:2 * D], ALU.mult))
                    gs.link(v.tensor_tensor(yblk[:, b, :], yblk[:, b, :], ng, ALU.add))
                    y = acc_b[:, bass.ds(nb * CW, D)]
                    gs.link(v.tensor_tensor(y, yblk[:, b, :], h, ALU.add))
                    moments(gs, b, nb, y).then_inc(s["g_out"], 1)

            gs = Steps(dve, s["gru_step"])
            GSTEPS = 2 * (3 + 2 + 6)
            gs.loop(0, GSTEPS)
            gru(0)
            gs.n = 0
            with dve.Fori(1, ITU) as it:
                gs.loop(it, GSTEPS)
                gru(it)
                gs.end(ITU)
            dve.wait_ge(s["g_out"], NB)
            normalized(gs, acc_b, CW, s["g_var"], s["g_root"], s["y_ready"])

        @block.tensor
        def _(pe):
            mm, tr = nc.tensor.matmul, nc.tensor.transpose
            pe.wait_ge(s["weights_in"], 16 * 16)
            pe.wait_ge(s["pool_const"], 5)
            tr(bank[0][:, 0:D], wself_n[:, :], ident[:, :]).then_inc(s["pe_weights"], 1)
            for d in range(2):
                for c, at in ((2, 0), (0, 1), (1, 2)):
                    last = tr(bank[2 + d][:, at * D:(at + 1) * D], wih_n[:, c, d * D:(d + 1) * D], ident[:, :])
                last.then_inc(s["pe_weights"], 1)
            for c in range(3):
                last = tr(bank[4][:, c * D:(c + 1) * D], whh_n[:, c, :], ident[:, :])
            last.then_inc(s["pe_weights"], 1)
            pe.wait_ge(s["act_weights"], 3)
            mm(bank[1][:, 0:D], wself_t[:, :], wtop[:, :], start=True, stop=True).then_inc(s["pe_weights"], 1)
            mm(bank[5][:, 0:3 * D], win_n[:, :], wih_t[:, 0, :], start=True, stop=True).then_inc(s["pe_weights"], 1)
            mm(bank[6][:, 0:3 * D], wout_n[:, :], wih_t[:, 1, :], start=True, stop=True).then_inc(s["pe_weights"], 1)
            mm(bank[2][0:1, 3 * D:4 * D], cols[:, 0:1], wtop[:, :], start=True, stop=True).then_inc(s["pe_weights"], 1)
            mm(bank[7][0:1, 0:3 * D], cols[:, 1:2], wih_t[:, 0, :], start=True, stop=True)
            mm(bank[0][0:1, 0:3 * D], cols[:, 2:3], wih_t[:, 1, :], start=True, stop=True).then_inc(s["pe_weights"], 1)
            pe.wait_ge(s["act_weights"], 8)
            pe.wait_ge(s["dve_weights"], 3)

            def counts(it):
                for b in range(2):
                    g = 2 * it + b
                    for i in range(2):
                        pe.wait_ge(s["blocks_ready"], 2 * g + i + 1)
                        for j in range(TG):
                            t = g * TG + j
                            last = mm(bankrow(i, g, j), onek[:, 2 * b + i, j, :], ones_b[:, 0:1], start=True, stop=True)
                        last.then_inc(s["counted"], 1)

            gb = HCHUNK // TG // 2
            for c in range(-(-T // HCHUNK)):
                def bankrow(i, g, j, c=c):
                    col = g * TG + j - c * HCHUNK
                    return bank[4 * i + c][0:NBP, bass.ds(col, 1)]
                with pe.Fori(c * gb, min((c + 1) * gb, NG // 2)) as it:
                    counts(it)
            pe.wait_ge(s["hist_ready"], 2 * -(-T // HCHUNK))
            pe.wait_ge(s["flags_sum"], 1)
            mm(bank[1][:, 0:2], ones[0:NQ, :], viol[0:NQ, :], start=True, stop=True).then_inc(s["flag_pe"], 1)
            pe.wait_ge(s["start_in"], 1)
            mm(bank[0][0:NBP, 0:2], tri[0:NBP, 0:NBP], kcol[0:NBP, 0:2], start=True, stop=True).then_inc(s["start_sum"], 1)
            for i, (U, V, _, row) in enumerate(PASSES):
                pe.wait_ge(s["start_in"], 2 * i + 2)
                if i:
                    pe.wait_ge(s["tables_read"], i)
                mm(bank[0][0:NB, 2:3], tri[0:NB, 0:NB], kcol[0:NB, 4:5], start=True, stop=True).then_inc(s["start_sum"], 1)
                pe.wait_ge(s["start_in"], 2 * i + 3)
                for c in range(0, V, HCHUNK):
                    w = min(HCHUNK, V - c)
                    mm(bank[c // HCHUNK][:, 0:w], ones[0:NB, :], ge_end[0:NB, c:c + w], start=True, stop=True)
                    mm(bank[4 + c // HCHUNK][:, 0:w], coef[0:NB, :], ge_start[0:NB, c:c + w], start=True, stop=True).then_inc(s["tables_sum"], 1)
            pe.wait_ge(s["tables_read"], 3)

            def tile_sums(h, onehot):
                for k in range(4):
                    j = 4 * h + k
                    last = mm(bank[6][:, k * P:(k + 1) * P], onehot[0:NBP, j, :], onehot[0:NBP, j, :], start=True, stop=True)
                return last

            def first_of(onehot, base, g):
                for j in range(TG):
                    last = mm(bank[7][:, P + 3 * j:P + 3 * j + 3], onehot[0:NBP, j, :],
                              base[:, bass.ds(g * TG + j, 1), :].rearrange("k t c -> k (t c)"), start=True, stop=True)
                return last

            pe.wait_ge(s["flag_ready"], 1)
            unsorted = pe.value_load(flag_i[0:1, 1:2], min_val=0, max_val=1)
            with pe.If(unsorted):
                with pe.Fori(0, NG) as g:
                    pe.wait_ge(s["slow_oht"], g + 1)
                    first_of(oht[:, 0], base3d, g)
                    for h in range(2):
                        need(pe, s["slow_own"], 2 * g + h if h else 0)
                        tile_sums(h, oht[:, 0]).then_inc(s["slow_sums"], 1)

            def edge_group(it):
                for b in range(2):
                    g = 2 * it + b
                    pe.wait_ge(attr_in[b], it * 16 + 16)
                    need(pe, s["pos_ready"], g)
                    pe.nop(nofuse=True)
                    tr(bank[7][0:TG * A, 0:P], attr[:, b, :], ident[:, :]).then_inc(s["attr_tr"], 1)
                    pe.wait_ge(s["attr_sb"], g + 1)
                    for h in range(2):
                        need(pe, s["silu_done"], 2 * g + h - 1)
                        for k in range(4):
                            last = mm(bank[h][:, k * P:(k + 1) * P], w1pad[:, 4 * h + k, :], attr_t[0:TG * A, :], start=True, stop=True)
                        last.then_inc(s["h_ready"], 1)
                    pe.wait_ge(s["oht_ready"], g + 1)
                    first_of(oht[:, b], base3, g).then_inc(s["base_ready"], 1)
                    for h in range(2):
                        need(pe, s["ranked"], 2 * g + h)
                        tile_sums(h, oht[:, b]).then_inc(s["sums_ready"], 1)
                        pe.wait_ge(s["wsel_ready"], g + 1)
                        pe.wait_ge(win_in[b], (it + 1) * 16 * TG)
                        need(pe, s["xj_sb"], 2 * g + h - 1)
                        for k in range(4):
                            j = 4 * h + k
                            last = mm(bank[4 + h][:, k * P:(k + 1) * P], wsel[:, j, :], win[:, b, j, :], start=True, stop=True)
                        last.then_inc(s["xj_ready"], 1)
                    for h in range(2):
                        pe.wait_ge(s["silu_done"], 2 * g + h + 1)
                        need(pe, s["msg_ready"], 2 * g + h - 1)
                        for k in range(4):
                            o = bank[2 + h][:, k * P:(k + 1) * P]
                            mm(o, ht[:, h, k * P:(k + 1) * P], w2s[:, :], start=True, stop=False)
                            last = mm(o, ones_b[0:3, :], b2s[:, :], start=False, stop=True)
                        last.then_inc(s["w_ready"], 1)

            pe.wait_ge(s["prepared"], 1)
            pe.wait_ge(s["w1_in"], 16 * TG)
            pe.wait_ge(s["aux_in"], 16 * 6)
            edge_group(0)
            with pe.Fori(1, NG // 2 - 1) as it:
                edge_group(it)
            pe.wait_ge(attr_in[1], (NG // 2 - 1) * 16 + 16 * (2 + 2 * (LJ > 0)))
            edge_group(NG // 2 - 1)

            def sums0(it):
                for k in range(8):
                    pe.wait_ge(s["oh0_ready"], it * 8 + k + 1)
                    need(pe, s["add0_done"], it * 8 + k - 7)
                    for i in range(2):
                        last = mm(bank[k][:, 0:D], oh0[:, k, i, :], mtile[:, k, i, 0:D], start=(i == 0), stop=(i == 1))
                    last.then_inc(s["sum0_ready"], 1)

            pe.wait_ge(s["msg_ready"], 2 * NG)
            sums0(0)
            with pe.Fori(1, IT0) as it:
                sums0(it)

            pe.wait_ge(s["add0_done"], V0)

            def update(it):
                for b in range(2):
                    nb = 2 * it + b
                    pe.wait_ge(xblk_in[b], it * 16 + 16)
                    need(pe, s["xt_sb"], nb - 1)
                    tr(bank[b][:, 0:P], xblk[:, b, :], ident[:, :])
                    pe.wait_ge(s["agg_sb"], nb + 1)
                    tr(bank[b][:, P:2 * P], gates[:, b, 0:D], ident[:, :]).then_inc(s["x_t"], 1)
                for b in range(2):
                    nb = 2 * it + b
                    pe.wait_ge(s["xt_sb"], nb + 1)
                    need(pe, s["u_stats"], nb - 1)
                    mm(bank[2 + b][:, 0:D], xat[:, b, 0:P], wcomb[:, :], start=True, stop=False)
                    mm(bank[2 + b][:, 0:D], xat[:, b, P:2 * P], wbot[:, :], start=False, stop=False)
                    mm(bank[2 + b][:, 0:D], ones[0:1, :], bias0[0:1, :], start=False, stop=True).then_inc(s["u_ready"], 1)

            update(0)
            with pe.Fori(1, ITU) as it:
                update(it)

            pe.wait_ge(s["u_store"], NB)
            for half in range(2):
                def sums1(it):
                    for q in range(4):
                        pe.wait_ge(s["oh1_ready"], half * V1 // TG + it * 4 + q + 1)
                        pe.wait_ge(gathered[q], 16 * TG * (it + half * IT1 + 1))
                        need(pe, s["add1_done"], half * V1 + it * NS + q * TG)
                        for k in range(TG):
                            last = mm(bank[k // 2][:, (k % 2) * 256:(k % 2) * 256 + CW], oh1[:, k, :], grow[:, q * TG + k, :], start=True, stop=True)
                        last.then_inc(s["sum1_ready"], 1)

                sums1(0)
                with pe.Fori(1, IT1) as it:
                    sums1(it)

            pe.wait_ge(s["add1_done"], 2 * V1)

            def gru(it):
                for b in range(2):
                    nb = 2 * it + b
                    pe.wait_ge(hblk_in[b], it * 16 + 16)
                    pe.wait_ge(s["g_mean"], nb + 1)
                    need(pe, s["g_tsb"], nb - 1)
                    tr(bank[b][:, 0:P], means[:, b, 0:D], ident[:, :])
                    tr(bank[b][:, P:2 * P], means[:, b, D:2 * D], ident[:, :])
                    tr(bank[b][:, 2 * P:3 * P], xblk[:, b, :], ident[:, :])
                    tr(bank[b][0:3, 3 * P:4 * P], aux[:, b, 0:3], ident[:, :]).then_inc(s["g_t"], 1)
                for b in range(2):
                    nb = 2 * it + b
                    pe.wait_ge(s["g_tsb"], nb + 1)
                    need(pe, s["g_out"], nb - 1)
                    o = bank[2 + b]
                    mm(o[:, :], auxt[0:3, b, :], auxw[:, :], start=True, stop=False)
                    mm(o[:, 0:3 * D], xat[:, b, 0:P], m_in[:, :], start=False, stop=False)
                    mm(o[:, 0:3 * D], xat[:, b, P:2 * P], m_out[:, :], start=False, stop=False)
                    mm(o[:, D:4 * D], xat[:, b, 2 * P:3 * P], whh_t[:, :], start=False, stop=True).then_inc(s["g_lin"], 1)

            gru(0)
            with pe.Fori(1, ITU) as it:
                gru(it)


_INS = ['x', 'src', 'dst', 'edge_attr_8', 'L0_gnn_W1', 'L0_gnn_b1', 'L0_gnn_W2', 'L0_gnn_b2', 'L0_gnn_Wself', 'L0_gnn_bself',
        'L0_gnn_Wcat', 'L0_gnn_bcat', 'L1_gnn_W_in', 'L1_gnn_b_in', 'L1_gnn_W_out', 'L1_gnn_b_out', 'L1_gnn_w_ih', 'L1_gnn_w_hh',
        'L1_gnn_b_ih', 'L1_gnn_b_hh']


def kernel(**inputs):
    import numpy as _np
    import concourse.bacc as _bacc
    from concourse import mybir as _mybir
    from concourse.bass_utils import run_bass_kernel_spmd as _run

    nc = _bacc.Bacc("TRN2", target_bir_lowering=False, num_devices=1)
    arrays, args = {}, []
    for name in _INS:
        a = _np.ascontiguousarray(inputs[name])
        arrays[f"in_{name}_dram"] = a
        args.append(nc.dram_tensor(f"in_{name}_dram", a.shape, _mybir.dt.from_np(a.dtype), kind="ExternalInput").ap())
    out = nc.dram_tensor("out_0_dram", (N, D), _mybir.dt.float32, kind="ExternalOutput").ap()
    gnn_kernel(nc, *args, out)
    return _run(nc, [arrays], core_ids=[0]).results[0]["out_0_dram"]
```

```python
import concourse.bass as bass
from concourse import mybir
from concourse.alu_op_type import AluOpType as ALU
from contextlib import ExitStack

N, E, D, A = 12500, 212500, 128, 8
P = 128
TG = 8
GE = TG * P
NG = -(-E // GE)
NG += NG % 2
EP = NG * GE
T = NG * TG
NB = -(-N // P)
NPAD = NB * P
NBP = NB + 1
PAD = NPAD
NQ = 104
QE = EP // NQ
QG = QE // GE
RW = 136
U0, U1 = 2 * P, P
V0 = -(-(E // U0 + NB) // 8) * 8
V1 = -(-(E // U1 + NB) // 32) * 32
CW = D + 1
SB = 7
EPS = 1e-5


class Steps:

    def __init__(self, eng, sem):
        self.eng, self.sem, self.n, self.it, self.per = eng, sem, 0, None, 0

    def loop(self, it, per):
        self.it, self.per, self.first = it, per, self.n

    def end(self, trips):
        assert self.n - self.first == self.per, (self.n - self.first, self.per)
        self.n, self.it = self.first + trips * self.per, None

    def value(self):
        return self.n if self.it is None else self.it * self.per + self.n

    def wait(self):
        self.eng.wait_ge(self.sem, self.value())

    def mark(self, ins):
        ins.then_inc(self.sem, 1)
        self.n += 1

    def link(self, ins):
        self.mark(ins)
        self.wait()


def need(eng, sem, value):
    if not isinstance(value, int) or value > 0:
        eng.wait_ge(sem, value)


def hold(pool, sem, value):
    if not isinstance(value, int) or value > 0:
        pool.wait_ge(sem, value)
        pool.nop(nofuse=True)


def gnn_kernel(nc, x, src, dst, edge_attr, W1, b1, W2, b2, Wself, bself, Wcat, bcat,
               W_in, b_in, W_out, b_out, w_ih, w_hh, b_ih, b_hh, out):
    f32, i32, bf16 = mybir.dt.float32, mybir.dt.int32, mybir.dt.bfloat16
    ACT, AX = mybir.ActivationFunctionType, mybir.AxisListType

    def dram(name, shape, dt):
        return nc.dram_tensor(name, shape, dt, kind="Internal").ap()

    xwin = dram("xwin", [NPAD + EP, D], f32)
    x1d = dram("x1d", [NPAD, D], f32)
    rows3 = dram("rows3", [NG, 3, GE], bf16)
    winrow = dram("winrow", [T], i32)
    dlist = dram("dlist", [EP, 2], f32)
    dtmp = dram("dtmp", [EP, 2], f32)
    msgs = dram("msgs", [EP, RW], f32)
    vtab = dram("vtab", [6, V1], i32)

    ctx = ExitStack()
    with ctx:
        def sb(name, shape, dt=f32):
            return ctx.enter_context(nc.sbuf_tensor(name, shape, dt))

        def sem(name):
            return ctx.enter_context(nc.semaphore(name))

        acc_a = sb("acc_a", [P, NBP * CW])
        acc_b = sb("acc_b", [P, NBP * CW])
        src_key = sb("src_key", [P, T])
        dst_idx = sb("dst_idx", [P, T], i32)
        base3 = sb("base3", [NBP, T, 3], bf16)
        blk0 = sb("blk0", [P, V0])
        blk1s = sb("blk1s", [P, V1])
        blk1d = sb("blk1d", [P, V1])
        ident = sb("ident", [P, P])
        earlier = sb("earlier", [P, P])
        tri = sb("tri", [P, P])
        iota_row = sb("iota_row", [P, P])
        iota_c = sb("iota_c", [P, 1])
        iota_k = sb("iota_k", [P, NBP], bf16)
        ones = sb("ones", [P, P])
        ones_b = sb("ones_b", [P, P], bf16)
        w1pad = sb("w1pad", [TG * A, TG, D])
        w2s = sb("w2s", [P, D])
        b1c = sb("b1c", [P, 1])
        b2row = sb("b2row", [1, 4, D])
        b2parts = sb("b2parts", [1, 3, D], bf16)
        b2s = sb("b2s", [3, D], bf16)
        wcomb = sb("wcomb", [P, D])
        wbot = sb("wbot", [P, D])
        bias0 = sb("bias0", [1, D])
        m_in = sb("m_in", [P, 3 * D])
        m_out = sb("m_out", [P, 3 * D])
        whh_t = sb("whh_t", [P, 3 * D])
        auxw = sb("auxw", [3, 4 * D])
        auxw9 = sb("auxw9", [9, 4 * D], bf16)
        mean_var = sb("mean_var", [P, NB, 2])
        some_mv = sb("some_mv", [P, 2 * SB, 2])
        deviation = sb("deviation", [P, NB])
        flag_f = sb("flag_f", [P, 2])
        flag_i = sb("flag_i", [P, 2], i32)

        ARENA = 11264
        arena = sb("arena", [P, ARENA])

        def cutter(whole, size):
            at = [0]

            def cut(n, dt=f32):
                words = n if dt != bf16 else -(-n // 2)
                got = whole[:, at[0]:at[0] + words]
                at[0] += words
                assert at[0] <= size, (at[0], size)
                return got if dt == f32 else got.bitcast(dt)
            return cut

        cut = cutter(arena, ARENA)
        win = cut(2 * TG * D).rearrange("p (b j d) -> p b j d", b=2, j=TG)
        rowsb = cut(2 * 2 * GE, bf16).rearrange("p (b r e) -> p b r e", b=2, r=2)
        attr = cut(2 * TG * A).rearrange("p (b c) -> p b c", b=2)
        attr_t = cut(P)
        oht = cut(2 * GE, bf16).rearrange("p (b j e) -> p b j e", b=2, j=TG)
        wsel = cut(GE).rearrange("p (j e) -> p j e", j=TG)
        ht = cut(2 * 4 * P).rearrange("p (h e) -> p h e", h=2)
        xjs = cut(2 * 4 * P).rearrange("p (h e) -> p h e", h=2)
        mrow = cut(2 * TG * RW).rearrange("p (b j c) -> p b j c", b=2, j=TG)
        pos = cut(2 * TG, i32).rearrange("p (b j) -> p b j", b=2)
        junk = cut(TG * P, bf16).rearrange("p (j e) -> p j e", j=TG)
        rank = cut(TG)
        digits = cut(3 * TG).rearrange("p (j c) -> p j c", c=3)
        posf = cut(2 * TG).rearrange("p (s j) -> p s j", s=2)
        drow = cut(TG * 2).rearrange("p (j c) -> p j c", c=2)
        widx = cut(TG, i32)
        cut = cutter(arena, ARENA)
        mtile = cut(8 * 2 * RW).rearrange("p (s i c) -> p s i c", s=8, i=2)
        oh0 = cut(8 * 2 * P).rearrange("p (s i n) -> p s i n", s=8, i=2)
        cut = cutter(arena, ARENA)
        ustage = cut(2 * 2 * SB * D).rearrange("p (h c n d) -> p h c n d", h=2, c=2, n=SB)
        uxt = cut(2 * 2 * P).rearrange("p (b c) -> p b c", b=2)
        stats = cut(2 * SB * 6).rearrange("p (b c) -> p b c", c=6)
        auxp = cut(3 * 4 * D, bf16).rearrange("p (c f) -> p c f", c=3)
        cut = cutter(arena, ARENA)
        gstage = cut(2 * 3 * SB * D).rearrange("p (h c n d) -> p h c n d", h=2, c=3, n=SB)
        gxt = cut(2 * 3 * P).rearrange("p (b c) -> p b c", b=2)
        auxt = cut(2 * P, bf16).rearrange("p (b c) -> p b c", b=2)
        gates = cut(SB * 3 * D).rearrange("p (b c) -> p b c", b=SB)
        keep = cut(SB * D).rearrange("p (b c) -> p b c", b=SB)
        gstats = cut(2 * SB * 6).rearrange("p (b c) -> p b c", c=6)
        cut = cutter(src_key, T)
        aux9 = cut(NB * 9, bf16).rearrange("p (n c r) -> p n c r", c=3, r=3)
        ident_b = cut(P, bf16)
        rcnt = cut(NB).rearrange("p (n o) -> p n o", o=1)
        cut = cutter(arena, ARENA)
        NS = 32
        grow = cut(NS * CW).rearrange("p (s c) -> p s c", s=NS)
        edge2 = cut(NS * 2).rearrange("p (s c) -> p s c", s=NS)
        oh1 = cut(2 * TG * P).rearrange("p (b s n) -> p b s n", b=2, s=TG)

        cut = cutter(acc_a, NBP * CW)
        dst_n = cut(QE, i32)
        src_n = cut(QE, i32)
        next_n = cut(QE, i32)
        tmp_n = cut(QE)
        tile_p = cut(GE, i32)
        rows_n = cut(QG * 3 * GE, bf16).rearrange("p (g r e) -> p g r e", g=QG, r=3)
        cut = cutter(acc_b, NBP * CW)
        base3d = acc_b[0:NBP, 0:T * 3 // 2].bitcast(bf16).rearrange("k (t c) -> k t c", c=3)
        pair_n = cut(QE * 2).rearrange("p (e c) -> p e c", c=2)
        src_p = cut(T, i32)
        dst_p = cut(T, i32)
        hist_s = cut(T)
        hist_d = cut(T)
        brow = cut(7 * D)
        rows_w = cut(2 * 3 * D).rearrange("p (c f) -> p c f", c=2)
        cut = cutter(arena, ARENA)
        onek = cut(4 * TG * NBP, bf16).rearrange("p (s j k) -> p s j k", s=4, j=TG)
        blk_s = cut(T, bf16)
        blk_d = cut(T, bf16)
        sumt = cut(T)
        iota_i = cut(V1, i32)
        wih_n = cut(3 * 2 * D).rearrange("p (c f) -> p c f", c=3)
        whh_n = cut(3 * D).rearrange("p (c f) -> p c f", c=3)
        iota_v = cut(V1)
        wself_n, wself_t, wtop, win_n, wout_n = (cut(D) for _ in range(5))
        wih_t = cut(2 * 3 * D).rearrange("p (d f) -> p d f", d=2)
        cut = cutter(acc_a, NBP * CW)
        ge_start = cut(V1)
        ge_end = cut(V1)
        off_f = cut(V1)
        vrow = cut(2 * V1, i32).rearrange("p (c v) -> p c v", c=2)
        sumt2 = cut(T)
        cols = sb("cols", [P, 3])
        row2 = sb("row2", [1, 4 * D])
        lohi = sb("lohi", [P, 4, QG])
        viol = sb("viol", [P, 2])
        slowrow = sb("slowrow", [P, QG, TG], i32)
        lorow = sb("lorow", [P, 2, QG, TG])
        lorow_i = sb("lorow_i", [P, QG, TG], i32)
        kcol = sb("kcol", [P, 16])
        kcol_i = sb("kcol_i", [P, 2], i32)
        coef = sb("coef", [P, P])

        bank = [ctx.enter_context(nc.psum_tensor(f"bank{i}", [P, 512], f32)) for i in range(8)]

        names = """pads pool_const edges_in weights_in attr_w small_in dve_step act_step pe_weights act_weights dve_weights
        aux_in blocks_ready counted hist_ready flags_sum flag_ready prep_out start_in start_sum tables_sum tables_read
        tables_out prepared window_ready dst_sorted slow_in slow_oht slow_sums slow_rank slow_pos slow_step
        flag_pe x1_out out_done u_stats u_var u_root y_ready g_var g_root slow_own reg_dve gru_step list_copied attr_tr attr_sb oht_ready wsel_ready h_ready silu_done sums_ready ranked base_ready pos_ready xj_ready
        xj_sb w_ready msg_ready key_ready acc_zero oh0_ready sum0_ready add0_done x_t xt_sb u_ready u_store
        x1_ready oh1_ready sum1_ready add1_done g_mean g_t g_tsb g_lin g_gate g_mult g_kept g_cand g_tanh g_part g_out g_stats g_moments u_added u_moments u_kept g_mv aux_split xcopy pool_step
        gather_own upd_step grow_ones out_final w1_in slow_pool lotab_out reg_done wide_in digits_read""".split()
        s = {n: sem(n) for n in names}
        win_in = [sem(f"win_in{i}") for i in range(2)]
        rows_in = [sem(f"rows_in{i}") for i in range(2)]
        attr_in = [sem(f"attr_in{i}") for i in range(2)]
        scattered = [sem(f"scattered{i}") for i in range(2)]
        mtile_in = [sem(f"mtile_in{i}") for i in range(8)]
        edge2_in = [sem(f"edge2_in{i}") for i in range(4)]
        gathered = [sem(f"gathered{i}") for i in range(4)]
        x_staged = [sem(f"x_staged{i}") for i in range(2)]
        h_staged = [sem(f"h_staged{i}") for i in range(2)]
        block = ctx.enter_context(nc.Block())

        LAST = E - (NG - 1) * GE
        LP, LJ = LAST // TG, LAST % TG
        NLAST = E - (NQ - 1) * QE
        N_EDGES = 2 * (2 + (LJ > 0)) + 6
        PASSES = [(U0, V0, blk0, 0), (U1, V1, blk1s, 2), (U1, V1, blk1d, 4)]
        IT0, IT1, ITU = V0 // 8, V1 // NS, NB // (2 * SB)
        HCHUNK = 512

        def registers(eng, name, n):
            return [eng.alloc_register(f"{name}{i}") for i in range(n)]

        def load_table(eng, regs, row, v, top):
            eng.load(regs, vtab[row:row + 1, bass.ds(v, len(regs))])
            return [eng.snap(r, min_val=0, max_val=top) for r in regs]

        @block.sync
        def _(sp):
            sp.wait_ge(s["pads"], 5)
            for to, of in ((src_p, src), (dst_p, dst)):
                v = to.rearrange("p (g j) -> p g j", j=TG)
                sp.dma_start(v[:, 0:NG - 1, :], of[0:(NG - 1) * GE].rearrange("(g p j) -> p g j", p=P, j=TG)).then_inc(s["edges_in"], 16)
                sp.dma_start(v[0:LP, NG - 1, :], of[(NG - 1) * GE:(NG - 1) * GE + LP * TG].rearrange("(p j) -> p j", j=TG)).then_inc(s["edges_in"], 16)
                if LJ:
                    sp.dma_start(v[LP:LP + 1, NG - 1, 0:LJ], of[E - LJ:E].rearrange("(p j) -> p j", p=1)).then_inc(s["edges_in"], 16)
            for to, of, shift in ((src_n, src, 0), (dst_n, dst, 0), (next_n, dst, 1)):
                sp.dma_start(to[0:NQ - 1, :], of[shift:shift + (NQ - 1) * QE].rearrange("(q e) -> q e", e=QE)).then_inc(s["edges_in"], 16)
                sp.dma_start(to[NQ - 1:NQ, 0:NLAST - shift], of[(NQ - 1) * QE + shift:E].rearrange("(q e) -> q e", q=1)).then_inc(s["edges_in"], 16)
            sp.dma_start(xwin[0:N, :].rearrange("(a b) d -> a (b d)", a=100), x.rearrange("(a b) d -> a (b d)", a=100)).then_inc(s["xcopy"], 16)
            sp.wait_ge(s["pool_const"], 1)
            sp.dma_start(xwin[N:NPAD, :], coef[0:NPAD - N, :]).then_inc(s["xcopy"], 16)
            sp.wait_ge(s["dve_weights"], 1)
            for j in range(TG):
                sp.dma_start(w1pad[j * A:(j + 1) * A, j, :], W1).then_inc(s["w1_in"], 16)
            sp.wait_ge(s["dve_weights"], 2)
            for c in range(3):
                sp.dma_start(b2s[c:c + 1, :], b2parts[0:1, c, :]).then_inc(s["aux_in"], 16)
            sp.wait_ge(s["dve_weights"], 3)
            sp.wait_ge(s["act_weights"], 8)
            sp.dma_start(auxw[0:1, 0:3 * D], rows_w[0:1, 0, :]).then_inc(s["aux_in"], 16)
            sp.dma_start(auxw[1:2, 0:3 * D], rows_w[0:1, 1, :]).then_inc(s["aux_in"], 16)
            sp.dma_start(auxw[2:3, :], row2[0:1, :]).then_inc(s["aux_in"], 16)
            sp.wait_ge(s["prep_out"], 1)
            sp.dma_start(rows3.rearrange("(q g) r e -> q (g r e)", g=QG), rows_n[0:NQ].rearrange("q g r e -> q (g r e)")).then_inc(s["lotab_out"], 16)
            sp.dma_start(winrow.rearrange("(q c) -> q c", c=QG * TG), lorow_i[0:NQ].rearrange("q g j -> q (g j)")).then_inc(s["lotab_out"], 16)
            sp.dma_start(dlist.rearrange("(q e) c -> q (e c)", e=QE), pair_n[0:NQ].rearrange("q e c -> q (e c)")).then_inc(s["lotab_out"], 16)
            for i, (U, V, _, row) in enumerate(PASSES):
                sp.wait_ge(s["tables_read"], i + 1)
                sp.dma_start(vtab[row:row + 2, 0:V].rearrange("(o c) v -> o c v", o=1), vrow[0:1, :, 0:V]).then_inc(s["tables_out"], 16)
            sp.wait_ge(s["lotab_out"], 48)
            sp.wait_ge(s["xcopy"], 32)

            sp.wait_ge(s["flag_ready"], 1)
            unsorted = sp.value_load(flag_i[0:1, 1:2], min_val=0, max_val=1)
            with sp.If(unsorted):
                with sp.Fori(0, NG) as g:
                    sp.wait_ge(s["slow_pool"], g + 1)
                    sp.dma_start(rowsb[:, 0, 0, :], rows3[bass.ds(g, 1), 2, :].to_broadcast([P, GE])).then_inc(s["slow_in"], 16)
                    sp.dma_start(drow, dlist[bass.ds(g * GE, GE), :].rearrange("(p j) c -> p j c", j=TG)).then_inc(s["slow_in"], 16)

            regs = registers(sp, "sp_win", 2 * TG)
            sp.wait_ge(s["window_ready"], 1)
            wide = sp.value_load(flag_i[0:1, 0:1], min_val=0, max_val=1)
            sp.wait_ge(s["prepared"], 1)

            def edge_loads(it, last=False):
                sp.load(regs, winrow[bass.ds(it * 2 * TG, 2 * TG)].rearrange("(o t) -> o t", o=1))
                for b in range(2):
                    g = 2 * it + b
                    need(sp, s["wsel_ready"], g - 1)
                    sp.dma_start(rowsb[:, b, :, :], rows3[bass.ds(g, 1), 0:2, :].to_broadcast([P, 2, GE])).then_inc(rows_in[b], 16)
                    need(sp, s["attr_tr"], g - 1)
                    if last and b == 1:
                        av = attr[:, b, :].rearrange("p (j a) -> p j a", a=A)
                        e0 = (NG - 1) * GE
                        sp.dma_start(attr[0:LP, b, :], edge_attr[e0:e0 + LP * TG, :].rearrange("(p j) a -> p (j a)", j=TG)).then_inc(attr_in[b], 16)
                        k = 16
                        if LJ:
                            sp.dma_start(av[LP:LP + 1, 0:LJ, :], edge_attr[E - LJ:E, :].rearrange("(p j) a -> p j a", p=1)).then_inc(attr_in[b], 16)
                            sp.dma_start(av[LP:LP + 1, LJ:TG, :], edge_attr[0:TG - LJ, :].rearrange("(p j) a -> p j a", p=1)).then_inc(attr_in[b], 16)
                            k += 32
                        r = LP + (LJ > 0)
                        sp.dma_start(attr[r:P, b, :], edge_attr[0:(P - r) * TG, :].rearrange("(p j) a -> p (j a)", j=TG)).then_inc(attr_in[b], 16)
                    else:
                        sp.dma_start(attr[:, b, :], edge_attr[bass.ds(g * GE, GE), :].rearrange("(p j) a -> p (j a)", j=TG)).then_inc(attr_in[b], 16)
                    need(sp, s["xj_ready"], 2 * g - 2)

                    def window(j, done):
                        r = sp.snap(regs[b * TG + j], min_val=0, max_val=NPAD + EP - P)
                        sp.dma_start(win[:, b, j, :], xwin[bass.ds(r, P), :]).then_inc(done, 16)

                    sp.nop(nofuse=True)
                    with sp.If(wide):
                        for j in range(1, TG):
                            window(j, s["wide_in"])
                        sp.wait_ge(s["wide_in"], g * (16 * (TG - 1)) + 16 * (TG - 1))
                        sp.nop(nofuse=True)
                    window(0, win_in[b])

            edge_loads(0)
            with sp.Fori(1, NG // 2 - 1) as it:
                edge_loads(it)
            edge_loads(NG // 2 - 1, last=True)

            sp.wait_ge(scattered[0], 16 * TG * (NG // 2))
            sp.wait_ge(scattered[1], 16 * TG * (NG // 2))
            sp.wait_ge(s["msg_ready"], 2 * NG)
            regs0 = registers(sp, "sp_row", 8)
            sp.wait_ge(s["tables_out"], 48)

            def row_loads(it):
                offs = load_table(sp, regs0, 0, it * 8, EP - U0)
                for k in range(0, 8, 2):
                    need(sp, s["sum0_ready"], it * 8 + k - 7)
                    sp.dma_start(mtile[:, k, :, :], msgs[bass.ds(offs[k], U0), :].rearrange("(p i) c -> p i c", i=2)).then_inc(mtile_in[k], 16)

            row_loads(0)
            with sp.Fori(1, IT0) as it:
                row_loads(it)

            sum_rows = acc_a[:, 0:NB * D].rearrange("p (n d) -> p n d", d=D)

            def update_in(it):
                for h in range(2):
                    c = 2 * it + h
                    need(sp, s["u_added"], (c - 1) * SB)
                    sp.dma_start(ustage[:, h, 0], xwin[bass.ds(c * (SB * P), SB * P), :].rearrange("(n p) d -> p n d", p=P)).then_inc(x_staged[h], 16)
                    sp.dma_start(ustage[:, h, 1], sum_rows[:, bass.ds(c * SB, SB), :]).then_inc(x_staged[h], 16)

            sp.wait_ge(s["add0_done"], V0)
            update_in(0)
            with sp.Fori(1, ITU) as it:
                update_in(it)
            with sp.Fori(0, NB // SB) as c:
                sp.wait_ge(s["u_store"], c * SB + SB)
                sp.dma_start(x1d[bass.ds(c * (SB * P), SB * P), :].rearrange("(n p) d -> p n d", p=P),
                             sum_rows[:, bass.ds(c * SB, SB), :]).then_inc(s["x1_out"], 16)
            sp.wait_ge(s["x1_out"], 16 * (NB // SB))
            sp.wait_ge(s["aux_split"], 1)
            for c in range(3):
                sp.dma_start(auxw9[3 * c:3 * c + 3, :], auxp[0:3, c, :]).then_inc(s["aux_in"], 16)
            sp.wait_ge(s["aux_in"], 16 * 9)

            regs1 = registers(sp, "sp_edge", NS)
            sp.wait_ge(s["dst_sorted"], 1)
            for half, row in ((0, 2), (1, 4)):
                first = half * V1 // TG

                def edge2_loads(it):
                    offs = load_table(sp, regs1, row, it * NS, EP - U1)
                    for q in range(4):
                        need(sp, s["sum1_ready"], first + it * 4 + q - 3)
                        for k in range(TG):
                            of = msgs[bass.ds(offs[q * TG + k], U1), D:D + 2] if half == 0 else dlist[bass.ds(offs[q * TG + k], U1), :]
                            sp.dma_start(edge2[:, q * TG + k, :], of).then_inc(edge2_in[q], 16)

                edge2_loads(0)
                with sp.Fori(1, IT1) as it:
                    edge2_loads(it)

            mean_rows = [a[:, 0:NB * CW].rearrange("p (n c) -> p n c", c=CW) for a in (acc_a, acc_b)]

            def gru_in(it):
                for h in range(2):
                    c = 2 * it + h
                    need(sp, s["g_out"], (c - 1) * SB)
                    for k in range(2):
                        sp.dma_start(gstage[:, h, k], mean_rows[k][:, bass.ds(c * SB, SB), 0:D]).then_inc(h_staged[h], 16)
                    sp.dma_start(gstage[:, h, 2], x1d[bass.ds(c * (SB * P), SB * P), :].rearrange("(n p) d -> p n d", p=P)).then_inc(h_staged[h], 16)

            sp.wait_ge(s["g_mean"], 2)
            gru_in(0)
            with sp.Fori(1, ITU) as it:
                gru_in(it)
            y_rows = acc_b[:, 0:NB * CW].rearrange("p (n c) -> p n c", c=CW)
            with sp.Fori(0, NB // SB - 1) as c:
                sp.wait_ge(s["y_ready"], c * SB + SB)
                sp.dma_start(out[bass.ds(c * (SB * P), SB * P), :].rearrange("(n p) d -> p n d", p=P),
                             y_rows[:, bass.ds(c * SB, SB), 0:D]).then_inc(s["out_done"], 16)
            sp.wait_ge(s["y_ready"], NB)
            at, full = NB - SB, N // P
            sp.dma_start(out[at * P:full * P, :].rearrange("(n p) d -> p n d", p=P), y_rows[:, at:full, 0:D]).then_inc(s["out_done"], 16)
            sp.dma_start(out[full * P:N, :], y_rows[0:N - full * P, full, 0:D]).then_inc(s["out_done"], 16)
            sp.wait_ge(s["out_done"], 16 * (NB // SB + 1))

        @block.gpsimd
        def _(pool):
            st = Steps(pool, s["pool_step"])
            loads = [(w2s[:, :], W2), (wself_n[:, :], Wself), (wtop[:, :], Wcat[0:D, :]), (wbot[:, :], Wcat[D:2 * D, :]),
                     (win_n[:, :], W_in), (wout_n[:, :], W_out), (wih_n, w_ih.rearrange("(c p) f -> p c f", p=P)),
                     (whh_n, w_hh.rearrange("(c p) f -> p c f", p=P)), (b1c[:, :], b1.rearrange("(p o) -> p o", o=1)),
                     (cols[:, 0:1], bself.rearrange("(p o) -> p o", o=1)), (cols[:, 1:2], b_in.rearrange("(p o) -> p o", o=1)),
                     (cols[:, 2:3], b_out.rearrange("(p o) -> p o", o=1)), (b2row[0:1, 0, :], b2.rearrange("(o f) -> o f", o=1)),
                     (brow[0:1, 0:D], bcat.rearrange("(o f) -> o f", o=1)), (brow[0:1, D:4 * D], b_ih.rearrange("(o f) -> o f", o=1)),
                     (brow[0:1, 4 * D:7 * D], b_hh.rearrange("(o f) -> o f", o=1))]
            st.link(pool.memset(coef[:, :], 0.0))
            pool.memset(ones[:, :], 1.0).then_inc(s["pool_const"], 1)
            pool.memset(ones_b[:, :], 1.0).then_inc(s["pool_const"], 1)
            for m, fill, start, op, cm, step in ((ident, 1.0, 0.0, ALU.not_equal, 1, -1), (earlier, 0.0, 1.0, ALU.is_gt, 1, -1),
                                                 (tri, 0.0, 1.0, ALU.is_gt, -1, 1)):
                st.link(pool.memset(m[:, :], start))
                pool.affine_select(out=m[:, :], in_=m[:, :], compare_op=op, fill=fill, base=0, pattern=[[step, P]],
                                   channel_multiplier=cm).then_inc(s["pool_const"], 1)
            pool.iota(iota_i, pattern=[[1, V1]], base=0, channel_multiplier=0).then_inc(s["pool_const"], 1)
            pool.iota(kcol_i[:, 0:1], pattern=[[0, 1]], base=0, channel_multiplier=1).then_inc(s["pool_const"], 1)
            pool.iota(slowrow[0:NQ].rearrange("q g j -> q (g j)"), pattern=[[P, QG * TG]], base=NPAD,
                      channel_multiplier=QG * TG * P).then_inc(s["pool_const"], 1)
            pool.iota(tile_p, pattern=[[1, P], [0, TG]], base=0, channel_multiplier=0).then_inc(s["pool_const"], 1)
            for to, of in loads:
                pool.dma_start(to, of).then_inc(s["weights_in"], 16)

            pool.wait_ge(s["flag_ready"], 1)
            wide = pool.value_load(flag_i[0:1, 0:1], min_val=0, max_val=1)
            with pool.If(wide):
                with pool.Fori(0, NG) as g:
                    pool.tensor_copy(widx, dst_idx[:, bass.ds(g * TG, TG)]).then_inc(s["gather_own"], 1)
                    hold(pool, s["gather_own"], g + 1)
                    for j in range(TG):
                        pool.indirect_dma_start(win[:, 0, j, :], None, x, bass.IndirectOffsetOnAxis(ap=widx[:, j:j + 1], axis=0)).then_inc(s["slow_step"], 16)
                    hold(pool, s["slow_step"], g * (16 * (TG + 1)) + 16 * TG)
                    pool.dma_start(xwin[bass.ds(g * GE + NPAD, GE), :].rearrange("(j p) d -> p j d", p=P), win[:, 0, :, :]).then_inc(s["slow_step"], 16)
                    hold(pool, s["slow_step"], g * (16 * (TG + 1)) + 16 * (TG + 1))
            unsorted = pool.value_load(flag_i[0:1, 1:2], min_val=0, max_val=1)
            with pool.If(unsorted):
                with pool.Fori(0, NG) as g:
                    hold(pool, s["slow_pos"], g + 1)
                    hold(pool, s["slow_in"], g * 32 + 32)
                    for j in range(TG):
                        pool.indirect_dma_start(dtmp, bass.IndirectOffsetOnAxis(ap=pos[:, 0, j:j + 1], axis=0), drow[:, j, :], None).then_inc(s["reg_done"], 16)
                    hold(pool, s["reg_done"], g * (16 * TG) + 16 * TG)
                    pool.sem_inc(s["slow_pool"], 1)
                pool.dma_start(dlist.rearrange("(q e) c -> q (e c)", e=QE), dtmp.rearrange("(q e) c -> q (e c)", e=QE)).then_inc(s["list_copied"], 16)
                hold(pool, s["list_copied"], 16)
            pool.sem_inc(s["window_ready"], 1)
            pool.sem_inc(s["dst_sorted"], 1)

            def scatters(it):
                for b in range(2):
                    g = 2 * it + b
                    hold(pool, s["pos_ready"], g + 1)
                    hold(pool, s["key_ready"], 2 * g + 2)
                    hold(pool, s["msg_ready"], 2 * g + 2)
                    for j in range(TG):
                        pool.indirect_dma_start(msgs, bass.IndirectOffsetOnAxis(ap=pos[:, b, j:j + 1], axis=0), mrow[:, b, j, :], None).then_inc(scattered[b], 16)

            with pool.Fori(0, NG // 2) as it:
                scatters(it)

            pool.wait_ge(s["x1_out"], 16 * (NB // SB))
            hold(pool, s["grow_ones"], 1)
            for half in range(2):
                with pool.Fori(0, IT1) as it:
                    for q in range(4):
                        hold(pool, edge2_in[q], 16 * TG * (it + half * IT1 + 1))
                        for k in range(TG):
                            sl = q * TG + k
                            pool.indirect_dma_start(grow[:, sl, 0:D], None, x1d, bass.IndirectOffsetOnAxis(ap=edge2[:, sl, 1:2].bitcast(i32), axis=0)).then_inc(gathered[q], 16)

        @block.scalar
        def _(act):
            def copy_out(i, to, of):
                act.wait_ge(s["pe_weights"], i)
                nc.scalar.activation(to, of, ACT.Copy).then_inc(s["act_weights"], 1)

            copy_out(1, wself_t[:, :], bank[0][:, 0:D])
            for d in range(2):
                copy_out(2 + d, wih_t[:, d, :], bank[2 + d][:, 0:3 * D])
            copy_out(4, whh_t[:, :], bank[4][:, 0:3 * D])
            copy_out(5, wcomb[:, :], bank[1][:, 0:D])
            copy_out(6, m_in[:, :], bank[5][:, 0:3 * D])
            copy_out(7, m_out[:, :], bank[6][:, 0:3 * D])
            act.wait_ge(s["pe_weights"], 9)
            nc.scalar.activation(rows_w[0:1, 0, :], bank[7][0:1, 0:3 * D], ACT.Copy)
            nc.scalar.activation(rows_w[0:1, 1, :], bank[0][0:1, 0:3 * D], ACT.Copy).then_inc(s["act_weights"], 1)
            for i, hist in enumerate((hist_s, hist_d)):
                act.wait_ge(s["counted"], 2 * NG)
                for c in range(0, T, HCHUNK):
                    w = min(HCHUNK, T - c)
                    last = nc.scalar.activation(hist[0:NBP, c:c + w], bank[4 * i + c // HCHUNK][0:NBP, 0:w], ACT.Copy)
                    last.then_inc(s["hist_ready"], 1)

            def hidden(g):
                act.wait_ge(s["attr_tr"], g + 1)
                need(act, s["h_ready"], 2 * g)
                nc.scalar.activation(attr_t[0:TG * A, :], bank[7][0:TG * A, 0:P], ACT.Copy).then_inc(s["attr_sb"], 1)
                for h in range(2):
                    act.wait_ge(s["h_ready"], 2 * g + h + 1)
                    need(act, s["w_ready"], 2 * g + h - 1)
                    nc.scalar.activation(ht[:, h, :], bank[h][:, :], ACT.Silu, bias=b1c[:, 0:1]).then_inc(s["silu_done"], 1)

            def edge_group(it, last=False):
                for b in range(2):
                    g = 2 * it + b
                    for h in range(2):
                        act.wait_ge(s["xj_ready"], 2 * g + h + 1)
                        need(act, s["msg_ready"], 2 * g + h - 1)
                        nc.scalar.activation(xjs[:, h, :], bank[4 + h][:, :], ACT.Copy).then_inc(s["xj_sb"], 1)
                    need(act, scattered[b], it * 16 * TG)
                    act.nop(nofuse=True)
                    nc.scalar.activation(mrow[:, b, :, D:D + 1].rearrange("p j c -> p (j c)"), src_key[:, bass.ds(g * TG, TG)], ACT.Copy).then_inc(s["key_ready"], 1)
                    nc.scalar.activation(mrow[:, b, :, D + 1:D + 2].rearrange("p j c -> p (j c)").bitcast(i32), dst_idx[:, bass.ds(g * TG, TG)], ACT.Copy).then_inc(s["key_ready"], 1)
                    if not (last and b):
                        hidden(g + 1)

            act.wait_ge(s["prepared"], 1)
            hidden(0)
            edge_group(0)
            with act.Fori(1, NG // 2 - 1) as it:
                edge_group(it)
            edge_group(NG // 2 - 1, last=True)

            regs0 = registers(act, "act_row", 8)
            act.wait_ge(s["tables_out"], 48)
            for b in range(2):
                act.wait_ge(scattered[b], 16 * TG * (NG // 2))
            act.wait_ge(s["msg_ready"], 2 * NG)

            def row_loads(it):
                offs = load_table(act, regs0, 0, it * 8, EP - U0)
                for k in range(1, 8, 2):
                    need(act, s["sum0_ready"], it * 8 + k - 7)
                    act.dma_start(mtile[:, k, :, :], msgs[bass.ds(offs[k], U0), :].rearrange("(p i) c -> p i c", i=2)).then_inc(mtile_in[k], 16)

            row_loads(0)
            with act.Fori(1, IT0) as it:
                row_loads(it)

            def update(it):
                for i in range(2 * SB):
                    nb = 2 * SB * it + i
                    act.wait_ge(s["x_t"], nb + 1)
                    need(act, s["u_ready"], nb - 1)
                    nc.scalar.activation(uxt[:, i % 2, :], bank[i % 2][:, 0:2 * P], ACT.Copy).then_inc(s["xt_sb"], 1)

            update(0)
            with act.Fori(1, ITU) as it:
                update(it)

            def root(ready, done):
                act.wait_ge(ready, 1)
                nc.scalar.activation(deviation[:, :], deviation[:, :], ACT.Sqrt).then_inc(done, 1)

            root(s["u_var"], s["u_root"])

            def gru(it):
                for i in range(2 * SB + 2):
                    if i < 2 * SB:
                        nb = 2 * SB * it + i
                        act.wait_ge(s["g_t"], nb + 1)
                        need(act, s["g_lin"], nb - 1)
                        nc.scalar.activation(gxt[:, i % 2, :], bank[0][:, 0:3 * P], ACT.Copy)
                        nc.scalar.activation(auxt[0:9, i % 2, :], bank[0][0:9, 3 * P:4 * P], ACT.Copy).then_inc(s["g_tsb"], 1)
                    if 1 <= i < 2 * SB + 1:
                        nb, k = 2 * SB * it + i - 1, (i - 1) % SB
                        act.wait_ge(s["g_lin"], nb + 1)
                        need(act, s["g_out"], nb - SB + 1)
                        nc.scalar.activation(gates[:, k, 0:2 * D], bank[1 + k][:, D:3 * D], ACT.Sigmoid).then_inc(s["g_gate"], 1)
                    if i >= 2:
                        nb, k = 2 * SB * it + i - 2, (i - 2) % SB
                        act.wait_ge(s["g_cand"], nb + 1)
                        nc.scalar.activation(gates[:, k, 2 * D:3 * D], gates[:, k, 2 * D:3 * D], ACT.Tanh).then_inc(s["g_tanh"], 1)

            gru(0)
            with act.Fori(1, ITU) as it:
                gru(it)
            root(s["g_var"], s["g_root"])

        @block.vector
        def _(dve):
            v = nc.vector
            st = Steps(dve, s["dve_step"])
            v.memset(src_p[:, T - TG:T], PAD).then_inc(s["pads"], 1)
            v.memset(dst_p[:, T - TG:T], PAD).then_inc(s["pads"], 1)
            for t in (src_n, dst_n, next_n):
                v.memset(t[96:NQ, :], PAD).then_inc(s["pads"], 1)
            v.memset(w1pad[:, :, :], 0.0).then_inc(s["dve_weights"], 1)
            dve.wait_ge(s["pool_const"], 9)
            st.mark(v.tensor_copy(iota_row[:, :], iota_i[:, 0:P]))
            st.mark(v.tensor_copy(iota_v[:, :], iota_i))
            st.link(v.tensor_copy(iota_c[:, :], kcol_i[:, 0:1]))
            st.link(v.tensor_copy(iota_k[:, :], iota_v[:, 0:NBP]))
            dve.wait_ge(s["weights_in"], 16 * 16)
            for c in range(3):
                st.link(v.tensor_copy(b2parts[0:1, c, :], b2row[0:1, c, :]))
                if c < 2:
                    st.link(v.tensor_tensor(b2row[0:1, c + 1, :], b2row[0:1, c, :], b2parts[0:1, c, :], ALU.subtract))
            dve.sem_inc(s["dve_weights"], 1)
            v.memset(auxw[:, :], 0.0)
            v.tensor_copy(row2[0:1, 0:D], brow[0:1, 3 * D:4 * D])
            v.tensor_tensor(row2[0:1, D:3 * D], brow[0:1, D:3 * D], brow[0:1, 4 * D:6 * D], ALU.add)
            st.link(v.tensor_copy(row2[0:1, 3 * D:4 * D], brow[0:1, 6 * D:7 * D]))
            dve.wait_ge(s["pe_weights"], 8)
            st.link(v.tensor_tensor(bias0[0:1, :], bank[2][0:1, 3 * D:4 * D], brow[0:1, 0:D], ALU.add))
            dve.sem_inc(s["dve_weights"], 1)

            dve.wait_ge(s["edges_in"], 16 * N_EDGES)
            st.mark(v.tensor_copy(src_key[:, :], src_p))
            st.link(v.tensor_scalar(dst_idx[:, :], dst_p, float(N - 1), None, ALU.min))
            st.mark(v.tensor_scalar(src_p, src_p, 7, None, ALU.logical_shift_right))
            st.link(v.tensor_scalar(dst_p, dst_p, 7, None, ALU.logical_shift_right))
            st.mark(v.tensor_copy(blk_s, src_p))
            st.link(v.tensor_copy(blk_d, dst_p))
            def onehots(it):
                for b in range(2):
                    g = 2 * it + b
                    for i, blk in enumerate((blk_s, blk_d)):
                        need(dve, s["counted"], 2 * g + i - 3)
                        v.tensor_tensor(onek[:, 2 * b + i, :, :], blk[:, bass.ds(g * TG, TG)].rearrange("p (j o) -> p j o", o=1).to_broadcast([P, TG, NBP]),
                                        iota_k[:, :].rearrange("p (o k) -> p o k", o=1).to_broadcast([P, TG, NBP]), ALU.is_equal).then_inc(s["blocks_ready"], 1)

            onehots(0)
            with dve.Fori(1, NG // 2) as it:
                onehots(it)

            Q = slice(0, NQ)
            pair_i = pair_n.bitcast(i32)
            st.mark(v.tensor_copy(pair_n[Q, :, 0], dst_n[Q, :]))
            st.mark(v.tensor_scalar(pair_i[Q, :, 1], src_n[Q, :], float(N - 1), None, ALU.min))
            st.link(v.tensor_tensor(tmp_n[Q, :], next_n[Q, :], dst_n[Q, :], ALU.is_lt))
            st.link(v.tensor_reduce(viol[Q, 1:2], tmp_n[Q, :], AX.X, ALU.add))
            dw = tmp_n.rearrange("p (g e) -> p g e", g=QG)
            st.link(v.tensor_scalar(tmp_n[Q, :], dst_n[Q, :], float(N - 1), None, ALU.min))
            st.mark(v.tensor_reduce(lohi[Q, 0, :], dw[Q], AX.X, ALU.min))
            st.link(v.tensor_reduce(lohi[Q, 1, :], dw[Q], AX.X, ALU.max))
            st.link(v.tensor_scalar(lohi[Q, 0, :], lohi[Q, 0, :], float(N - P), None, ALU.min))
            st.link(v.tensor_tensor(lohi[Q, 2, :], lohi[Q, 1, :], lohi[Q, 0, :], ALU.subtract))
            st.link(v.tensor_scalar(lohi[Q, 3, :], lohi[Q, 2, :], float(P), None, ALU.is_ge))
            st.link(v.tensor_reduce(viol[Q, 0:1], lohi[Q, 3, :], AX.X, ALU.add))
            dve.sem_inc(s["flags_sum"], 1)
            st.mark(v.tensor_scalar(src_n[Q, :], src_n[Q, :], 7, None, ALU.logical_shift_right))
            st.link(v.tensor_scalar(dst_n[Q, :], dst_n[Q, :], 7, None, ALU.logical_shift_right))
            st.mark(v.tensor_copy(rows_n[Q, :, 0, :], src_n[Q, :].rearrange("p (g e) -> p g e", g=QG)))
            st.mark(v.tensor_copy(rows_n[Q, :, 2, :], dst_n[Q, :].rearrange("p (g e) -> p g e", g=QG)))
            lo_b = lohi[Q, 0, :].rearrange("p (g o) -> p g o", o=1)
            st.link(v.tensor_tensor(dw[Q], dw[Q], lo_b.to_broadcast([NQ, QG, GE]), ALU.subtract))
            dve.wait_ge(s["flag_pe"], 1)
            st.link(v.tensor_scalar(flag_f[:, :], bank[1][:, 0:2], 0.5, None, ALU.is_gt))
            st.link(v.tensor_copy(flag_i[:, :], flag_f[:, :]))
            dve.sem_inc(s["flag_ready"], 1)
            nx = next_n.bitcast(f32).rearrange("p (g e) -> p g e", g=QG)
            for g in range(QG):
                st.link(v.tensor_tensor(nx[Q, g, :], tile_p[Q, :], dw[Q, g, :], ALU.subtract))
                st.link(v.scalar_tensor_tensor(rows_n[Q, g, 1, :], nx[Q, g, :], flag_f[Q, 0:1], dw[Q, g, :], ALU.mult, ALU.add))
            lo_t = lo_b.to_broadcast([NQ, QG, TG])
            st.link(v.tensor_tensor(lorow[Q, 0], slowrow[Q], lo_t, ALU.subtract))
            st.link(v.tensor_copy(lorow[Q, 1], lo_t))
            st.link(v.scalar_tensor_tensor(lorow_i[Q], lorow[Q, 0], flag_f[Q, 0:1], lorow[Q, 1], ALU.mult, ALU.add))
            dve.sem_inc(s["prep_out"], 1)

            def running(stp, hist, a, b):
                cur, other = hist[0:NBP, :], a
                d = 1
                while d < T:
                    stp.mark(v.tensor_copy(other[:, 0:d], cur[:, 0:d]))
                    stp.link(v.tensor_tensor(other[:, d:T], cur[:, d:T], cur[:, 0:T - d], ALU.add))
                    cur, other = other, (b if other is a else a)
                    d *= 2
                return cur, other

            def first_places(stp, hist, total, spare, start, to):
                stp.link(v.tensor_tensor(spare, total, hist[0:NBP, :], ALU.subtract))
                whole = total.bitcast(i32)
                stp.link(v.tensor_scalar(whole, spare, start, None, ALU.add))
                digit = spare.bitcast(i32)
                for c in range(3):
                    stp.link(v.tensor_scalar(digit, whole, 7 * c, 127, ALU.logical_shift_right, ALU.bitwise_and))
                    stp.link(v.tensor_copy(to[:, :, c], digit))

            dve.wait_ge(s["hist_ready"], 2 * -(-T // HCHUNK))
            dve.wait_ge(s["lotab_out"], 48)
            dve.wait_ge(s["xcopy"], 32)
            sa, sb_ = sumt[0:NBP, :], sumt2[0:NBP, :]
            total, spare = running(st, hist_s, sa, sb_)
            st.mark(v.tensor_copy(kcol[0:NBP, 0:1], total[:, T - 1:T]))
            st.link(v.tensor_reduce(kcol[0:NBP, 1:2], hist_d[0:NBP, :], AX.X, ALU.add))
            dve.sem_inc(s["start_in"], 1)
            dve.wait_ge(s["start_sum"], 1)
            st.link(v.tensor_copy(kcol[0:NBP, 2:4], bank[0][0:NBP, 0:2]))
            first_places(st, hist_s, total, spare, kcol[0:NBP, 2:3], base3)
            for i, (U, V, blk, row) in enumerate(PASSES):
                k = 1 if row == 4 else 0
                cnt, start = kcol[0:NB, k:k + 1], kcol[0:NB, 2 + k:3 + k]
                nv, vfirst, vend, co = (kcol[0:NB, c:c + 1] for c in (4, 5, 6, 7))
                st.link(v.tensor_scalar(kcol_i[0:NB, 0:1], cnt, float(U - 1), None, ALU.add))
                st.link(v.tensor_scalar(kcol_i[0:NB, 1:2], kcol_i[0:NB, 0:1], U.bit_length() - 1, None, ALU.logical_shift_right))
                st.link(v.tensor_copy(nv, kcol_i[0:NB, 1:2]))
                dve.sem_inc(s["start_in"], 1)
                dve.wait_ge(s["start_sum"], 2 + i)
                st.link(v.tensor_copy(vfirst, bank[0][0:NB, 2:3]))
                st.link(v.tensor_tensor(vend, vfirst, nv, ALU.add))
                st.link(v.scalar_tensor_tensor(co, vfirst, -float(U), start, ALU.mult, ALU.add))
                st.link(v.tensor_scalar(coef[0:NB, :], ones[0:NB, :], co, None, ALU.mult))
                st.mark(v.tensor_scalar(ge_end[0:NB, 0:V], iota_v[0:NB, 0:V], vend, None, ALU.is_ge))
                st.link(v.tensor_scalar(ge_start[0:NB, 0:V], iota_v[0:NB, 0:V], vfirst, None, ALU.is_ge))
                st.link(v.tensor_tensor(ge_start[0:NB, 0:V], ge_start[0:NB, 0:V], ge_end[0:NB, 0:V], ALU.subtract))
                dve.sem_inc(s["start_in"], 1)
                for c in range(0, V, HCHUNK):
                    w = min(HCHUNK, V - c)
                    dve.wait_ge(s["tables_sum"], sum(-(-p[1] // HCHUNK) for p in PASSES[:i]) + c // HCHUNK + 1)
                    st.mark(v.tensor_scalar(blk[:, c:c + w], bank[c // HCHUNK][:, 0:w], float(P), None, ALU.mult))
                    if i and c == 0:
                        dve.wait_ge(s["tables_out"], 16 * i)
                    scale = float(D if row == 0 else CW)
                    st.mark(v.tensor_scalar(vrow[:, 1, c:c + w], bank[c // HCHUNK][:, 0:w], scale, None, ALU.mult))
                    st.link(v.scalar_tensor_tensor(off_f[:, c:c + w], iota_v[:, c:c + w], float(U), bank[4 + c // HCHUNK][:, 0:w], ALU.mult, ALU.add))
                    st.link(v.tensor_scalar(vrow[:, 0, c:c + w], off_f[:, c:c + w], float(EP - U), None, ALU.min))
                dve.sem_inc(s["tables_read"], 1)

            unsorted = dve.value_load(flag_i[0:1, 1:2], min_val=0, max_val=1)

            def ranks(sums_sem, sums_at, done_sem):
                for h in range(2):
                    dve.wait_ge(sums_sem, sums_at + h)
                    for k in range(4):
                        j = 4 * h + k
                        last = v.tensor_tensor_reduce(out=junk[:, j, :], in0=bank[6][:, k * P:(k + 1) * P], in1=earlier[:, :], scale=1.0,
                                                      scalar=0.0, op0=ALU.mult, op1=ALU.add, accum_out=rank[:, j:j + 1])
                    last.then_inc(done_sem, 1)

            def places(stp, b, done_sem, done_at):
                stp.link(v.scalar_tensor_tensor(posf[:, 0, :], digits[:, :, 1], float(P), digits[:, :, 0], ALU.mult, ALU.add))
                stp.link(v.scalar_tensor_tensor(posf[:, 1, :], digits[:, :, 2], float(P * P), posf[:, 0, :], ALU.mult, ALU.add))
                dve.wait_ge(done_sem, done_at)
                return v.tensor_tensor(pos[:, b, :], posf[:, 1, :], rank, ALU.add)

            with dve.If(unsorted):
                ss = Steps(dve, s["slow_rank"])
                tot, spr = running(ss, hist_d, sa, sb_)
                first_places(ss, hist_d, tot, spr, kcol[0:NBP, 3:4], base3d)
                dve.sem_inc(s["slow_pool"], 1)
                per = 4
                with dve.Fori(0, NG) as g:
                    ss.loop(g, per)
                    dve.wait_ge(s["slow_in"], g * 32 + 32)
                    v.tensor_scalar(oht[:, 0, :, :], rowsb[:, 0, 0, :].rearrange("p (e j) -> p j e", j=TG), iota_c[:, :], None, ALU.is_equal).then_inc(s["slow_oht"], 1)
                    ranks(s["slow_sums"], g * 2 + 1, s["slow_own"])
                    ss.link(v.tensor_copy(digits.rearrange("p j c -> p (j c)"), bank[7][:, P:P + 3 * TG]))
                    ss.mark(places(ss, 0, s["slow_own"], g * 2 + 2))
                    ss.wait()
                    dve.sem_inc(s["slow_pos"], 1)
                    ss.end(NG)
                    ss.it = None

            dve.wait_ge(s["tables_out"], 48)
            st.mark(v.memset(acc_a[:, :], 0.0))
            dve.wait_ge(s["aux_in"], 16 * 6)
            st.mark(v.memset(acc_b[:, :], 0.0))
            dve.wait_ge(s["window_ready"], 1)
            st.link(v.memset(mrow[:, :, :, :], 0.0))
            dve.sem_inc(s["prepared"], 1)

            ls = Steps(dve, s["reg_dve"])

            def onehots_of(it, b):
                g = 2 * it + b
                dve.wait_ge(rows_in[b], it * 16 + 16)
                need(dve, s["sums_ready"], 2 * g - 2)
                v.tensor_scalar(oht[:, b, :, :], rowsb[:, b, 0, :].rearrange("p (e j) -> p j e", j=TG), iota_c[:, :], None, ALU.is_equal).then_inc(s["oht_ready"], 1)
                need(dve, s["xj_ready"], 2 * g)
                v.tensor_scalar(wsel, rowsb[:, b, 1, :].rearrange("p (e j) -> p j e", j=TG), iota_c[:, :], None, ALU.is_equal).then_inc(s["wsel_ready"], 1)

            def edge_group(it, last=False):
                for b in range(2):
                    g = 2 * it + b
                    dve.wait_ge(s["base_ready"], g + 1)
                    need(dve, s["pos_ready"], g)
                    v.tensor_copy(digits.rearrange("p j c -> p (j c)"), bank[7][:, P:P + 3 * TG]).then_inc(s["digits_read"], 1)
                    ranks(s["sums_ready"], 2 * g + 1, s["ranked"])
                    if not (last and b):
                        onehots_of(it + b, 1 - b)
                    need(dve, scattered[b], it * 16 * TG)
                    dve.wait_ge(s["digits_read"], g + 1)
                    places(ls, b, s["ranked"], 2 * g + 2).then_inc(s["pos_ready"], 1)
                    for h in range(2):
                        dve.wait_ge(s["w_ready"], 2 * g + h + 1)
                        dve.wait_ge(s["xj_sb"], 2 * g + h + 1)
                        v.tensor_tensor(mrow[:, b, 4 * h:4 * h + 4, 0:D], bank[2 + h][:, :].rearrange("p (j d) -> p j d", j=4),
                                        xjs[:, h, :].rearrange("p (j d) -> p j d", j=4), ALU.mult).then_inc(s["msg_ready"], 1)

            onehots_of(0, 0)
            ls.loop(0, 4)
            edge_group(0)
            ls.n = 0
            with dve.Fori(1, NG // 2 - 1) as it:
                ls.loop(it, 4)
                edge_group(it)
            ls.n = 0
            ls.loop(NG // 2 - 1, 4)
            edge_group(NG // 2 - 1, last=True)
            ls.it = None

            regs0 = registers(dve, "dve_blk", 8)

            def sums0(it):
                at = load_table(dve, regs0, 1, it * 8, NB * D)
                for k in range(8):
                    dve.wait_ge(mtile_in[k], it * 16 + 16)
                    for i in range(2):
                        last = v.tensor_scalar(oh0[:, k, i, :], iota_row[:, :], blk0[:, bass.ds(it * 8 + k, 1)], mtile[:, k, i, D:D + 1], ALU.add, ALU.is_equal)
                    last.then_inc(s["oh0_ready"], 1)
                for k in range(8):
                    dve.wait_ge(s["sum0_ready"], it * 8 + k + 1)
                    need(dve, s["add0_done"], it * 8 + k)
                    a = acc_a[:, bass.ds(at[k], D)]
                    v.tensor_tensor(a, a, bank[k][:, 0:D], ALU.add).then_inc(s["add0_done"], 1)

            sums0(0)
            with dve.Fori(1, IT0) as it:
                sums0(it)

            us = Steps(dve, s["upd_step"])

            def moments(nb, slot, y, row_ready, stat_sem):
                dve.wait_ge(row_ready, nb + 1)
                dve.nop(nofuse=True)
                v.bn_stats(slot, y).then_inc(stat_sem, 1)

            def mean_variance(it, i, slot, stat_sem, kept_sem, done_sem):
                nb = 2 * SB * it + i
                if i == 0:
                    need(dve, kept_sem, it)
                dve.wait_ge(stat_sem, nb + 1)
                dve.nop(nofuse=True)
                v.bn_aggr(some_mv[:, i, :], slot).then_inc(done_sem, 1)

            def keep_moments(it, done_sem, kept_sem):
                dve.wait_ge(done_sem, 2 * SB * it + 2 * SB)
                dve.nop(nofuse=True)
                v.tensor_copy(mean_var[:, bass.ds(2 * SB * it, 2 * SB), :], some_mv[:, :, :]).then_inc(kept_sem, 1)

            def normalized(stp, acc, width, ready, done, out_ready):
                stp.link(v.tensor_scalar(deviation[:, :], mean_var[:, :, 1], EPS, None, ALU.add))
                dve.sem_inc(ready, 1)
                dve.wait_ge(done, 1)
                stp.link(v.reciprocal(deviation[:, :], deviation[:, :]))
                with dve.Fori(0, ITU) as it:
                    for i in range(2 * SB):
                        nb = 2 * SB * it + i
                        y = acc[:, bass.ds(nb * width, D)]
                        v.tensor_scalar(y, y, mean_var[:, bass.ds(nb, 1), 0], deviation[:, bass.ds(nb, 1)], ALU.subtract, ALU.mult).then_inc(out_ready, 1)

            def update(it):
                for i in range(2 * SB + 2):
                    if i < 2 * SB:
                        nb = 2 * SB * it + i
                        dve.wait_ge(s["u_ready"], nb + 1)
                        v.tensor_tensor(acc_a[:, bass.ds(nb * D, D)], ustage[:, i // SB, 0, i % SB, :], bank[2 + i % 6][:, 0:D], ALU.add).then_inc(s["u_added"], 1)
                    if 1 <= i < 2 * SB + 1:
                        nb = 2 * SB * it + i - 1
                        moments(nb, stats[:, i - 1, :], acc_a[:, bass.ds(nb * D, D)], s["u_added"], s["u_stats"])
                    if i >= 2:
                        mean_variance(it, i - 2, stats[:, i - 2, :], s["u_stats"], s["u_kept"], s["u_moments"])
                keep_moments(it, s["u_moments"], s["u_kept"])

            update(0)
            with dve.Fori(1, ITU) as it:
                update(it)
            dve.wait_ge(s["u_kept"], ITU)
            normalized(us, acc_a, D, s["u_var"], s["u_root"], s["u_store"])
            for c in range(3):
                us.link(v.tensor_copy(auxp[0:3, c, :], auxw[:, :]))
                if c < 2:
                    us.link(v.tensor_tensor(auxw[:, :], auxw[:, :], auxp[0:3, c, :], ALU.subtract))
            dve.sem_inc(s["aux_split"], 1)
            dve.wait_ge(s["aux_in"], 16 * 9)
            dve.wait_ge(s["x1_out"], 16 * (NB // SB))
            v.memset(grow[:, :, D:CW], 1.0).then_inc(s["grow_ones"], 1)
            us.mark(v.memset(aux9[:, :, :, 2], 1.0))
            us.mark(v.tensor_copy(ident_b[:, :], ident[:, :]))
            us.link(v.memset(acc_a[:, :], 0.0))
            regs1 = registers(dve, "dve_blk1", NS)
            for half, (row, blk, acc) in enumerate(((3, blk1s, acc_b), (5, blk1d, acc_a))):
                v0 = half * V1

                def sums1(it):
                    at = load_table(dve, regs1, row, it * NS, NB * CW)
                    first = half * V1 // TG + it * 4

                    def onehots1(q):
                        dve.wait_ge(edge2_in[q], 16 * TG * (it + half * IT1 + 1))
                        need(dve, s["sum1_ready"], first + q - 1)
                        for k in range(TG):
                            last = v.tensor_scalar(oh1[:, q % 2, k, :], iota_row[:, :], blk[:, bass.ds(it * NS + q * TG + k, 1)], edge2[:, q * TG + k, 0:1], ALU.add, ALU.is_equal)
                        last.then_inc(s["oh1_ready"], 1)

                    onehots1(0)
                    for q in range(4):
                        if q < 3:
                            onehots1(q + 1)
                        dve.wait_ge(s["sum1_ready"], first + q + 1)
                        for k in range(TG):
                            need(dve, s["add1_done"], v0 + it * NS + q * TG + k)
                            a = acc[:, bass.ds(at[q * TG + k], CW)]
                            v.tensor_tensor(a, a, bank[q % 2 * 4 + k // 2][:, (k % 2) * 256:(k % 2) * 256 + CW], ALU.add).then_inc(s["add1_done"], 1)

                sums1(0)
                with dve.Fori(1, IT1) as it:
                    sums1(it)

                dve.wait_ge(s["add1_done"], (half + 1) * V1)
                sums = acc[:, 0:NB * CW].rearrange("p (n c) -> p n c", c=CW)
                any_row = 1 - half
                us.mark(v.tensor_scalar(aux9[:, :, :, any_row], sums[:, :, D:CW].to_broadcast([P, NB, 3]), 1.0, None, ALU.min))
                us.link(v.tensor_scalar(rcnt[:, :, :], sums[:, :, D:CW], 1.0, None, ALU.max))
                us.link(v.reciprocal(rcnt[:, :, :], rcnt[:, :, :]))
                us.link(v.tensor_tensor(sums[:, :, 0:D], sums[:, :, 0:D], rcnt[:, :, :].to_broadcast([P, NB, D]), ALU.mult))
                dve.sem_inc(s["g_mean"], 1)

            def gru(it):
                for i in range(2 * SB + 4):
                    if i < 2 * SB:
                        nb, k = 2 * SB * it + i, i % SB
                        dve.wait_ge(s["g_gate"], nb + 1)
                        v.tensor_tensor(gates[:, k, 2 * D:3 * D], gates[:, k, 0:D], bank[1 + k][:, 3 * D:4 * D], ALU.mult).then_inc(s["g_mult"], 1)
                        v.scalar_tensor_tensor(keep[:, k, :], gates[:, k, D:2 * D], 1.0, gstage[:, i // SB, 2, k, :], ALU.add, ALU.mult).then_inc(s["g_kept"], 1)
                        dve.wait_ge(s["g_mult"], nb + 1)
                        v.tensor_tensor(gates[:, k, 2 * D:3 * D], gates[:, k, 2 * D:3 * D], bank[1 + k][:, 0:D], ALU.add).then_inc(s["g_cand"], 1)
                    if 2 <= i < 2 * SB + 2:
                        nb, k = 2 * SB * it + i - 2, (i - 2) % SB
                        dve.wait_ge(s["g_tanh"], nb + 1)
                        v.scalar_tensor_tensor(gates[:, k, 0:D], gates[:, k, D:2 * D], 1.0, gates[:, k, 2 * D:3 * D], ALU.subtract, ALU.mult).then_inc(s["g_part"], 1)
                    if 3 <= i < 2 * SB + 3:
                        nb = 2 * SB * it + i - 3
                        moments(nb, gstats[:, i - 3, :], acc_b[:, bass.ds(nb * CW, D)], s["g_out"], s["g_stats"])
                    if 2 <= i < 2 * SB + 2:
                        nb, k = 2 * SB * it + i - 2, (i - 2) % SB
                        dve.wait_ge(s["g_kept"], nb + 1)
                        dve.wait_ge(s["g_part"], nb + 1)
                        v.tensor_tensor(acc_b[:, bass.ds(nb * CW, D)], keep[:, k, :], gates[:, k, 0:D], ALU.subtract).then_inc(s["g_out"], 1)
                    if i >= 4:
                        mean_variance(it, i - 4, gstats[:, i - 4, :], s["g_stats"], s["g_mv"], s["g_moments"])
                keep_moments(it, s["g_moments"], s["g_mv"])

            gs = Steps(dve, s["gru_step"])
            gru(0)
            with dve.Fori(1, ITU) as it:
                gru(it)
            dve.wait_ge(s["g_mv"], ITU)
            normalized(gs, acc_b, CW, s["g_var"], s["g_root"], s["y_ready"])

        @block.tensor
        def _(pe):
            mm, tr = nc.tensor.matmul, nc.tensor.transpose
            pe.wait_ge(s["weights_in"], 16 * 16)
            pe.wait_ge(s["pool_const"], 5)
            tr(bank[0][:, 0:D], wself_n[:, :], ident[:, :]).then_inc(s["pe_weights"], 1)
            for d in range(2):
                for c, at in ((2, 0), (0, 1), (1, 2)):
                    last = tr(bank[2 + d][:, at * D:(at + 1) * D], wih_n[:, c, d * D:(d + 1) * D], ident[:, :])
                last.then_inc(s["pe_weights"], 1)
            for c in range(3):
                last = tr(bank[4][:, c * D:(c + 1) * D], whh_n[:, c, :], ident[:, :])
            last.then_inc(s["pe_weights"], 1)
            pe.wait_ge(s["act_weights"], 3)
            mm(bank[1][:, 0:D], wself_t[:, :], wtop[:, :], start=True, stop=True).then_inc(s["pe_weights"], 1)
            mm(bank[5][:, 0:3 * D], win_n[:, :], wih_t[:, 0, :], start=True, stop=True).then_inc(s["pe_weights"], 1)
            mm(bank[6][:, 0:3 * D], wout_n[:, :], wih_t[:, 1, :], start=True, stop=True).then_inc(s["pe_weights"], 1)
            mm(bank[2][0:1, 3 * D:4 * D], cols[:, 0:1], wtop[:, :], start=True, stop=True).then_inc(s["pe_weights"], 1)
            mm(bank[7][0:1, 0:3 * D], cols[:, 1:2], wih_t[:, 0, :], start=True, stop=True)
            mm(bank[0][0:1, 0:3 * D], cols[:, 2:3], wih_t[:, 1, :], start=True, stop=True).then_inc(s["pe_weights"], 1)
            pe.wait_ge(s["act_weights"], 8)
            pe.wait_ge(s["dve_weights"], 3)

            def counts(it):
                for b in range(2):
                    g = 2 * it + b
                    for i in range(2):
                        pe.wait_ge(s["blocks_ready"], 2 * g + i + 1)
                        for j in range(TG):
                            t = g * TG + j
                            last = mm(bankrow(i, g, j), onek[:, 2 * b + i, j, :], ones_b[:, 0:1], start=True, stop=True)
                        last.then_inc(s["counted"], 1)

            gb = HCHUNK // TG // 2
            for c in range(-(-T // HCHUNK)):
                def bankrow(i, g, j, c=c):
                    col = g * TG + j - c * HCHUNK
                    return bank[4 * i + c][0:NBP, bass.ds(col, 1)]
                with pe.Fori(c * gb, min((c + 1) * gb, NG // 2)) as it:
                    counts(it)
            pe.wait_ge(s["hist_ready"], 2 * -(-T // HCHUNK))
            pe.wait_ge(s["flags_sum"], 1)
            mm(bank[1][:, 0:2], ones[0:NQ, :], viol[0:NQ, :], start=True, stop=True).then_inc(s["flag_pe"], 1)
            pe.wait_ge(s["start_in"], 1)
            mm(bank[0][0:NBP, 0:2], tri[0:NBP, 0:NBP], kcol[0:NBP, 0:2], start=True, stop=True).then_inc(s["start_sum"], 1)
            for i, (U, V, _, row) in enumerate(PASSES):
                pe.wait_ge(s["start_in"], 2 * i + 2)
                if i:
                    pe.wait_ge(s["tables_read"], i)
                mm(bank[0][0:NB, 2:3], tri[0:NB, 0:NB], kcol[0:NB, 4:5], start=True, stop=True).then_inc(s["start_sum"], 1)
                pe.wait_ge(s["start_in"], 2 * i + 3)
                for c in range(0, V, HCHUNK):
                    w = min(HCHUNK, V - c)
                    mm(bank[c // HCHUNK][:, 0:w], ones[0:NB, :], ge_end[0:NB, c:c + w], start=True, stop=True)
                    mm(bank[4 + c // HCHUNK][:, 0:w], coef[0:NB, :], ge_start[0:NB, c:c + w], start=True, stop=True).then_inc(s["tables_sum"], 1)
            pe.wait_ge(s["tables_read"], 3)

            def tile_sums(h, onehot):
                for k in range(4):
                    j = 4 * h + k
                    last = mm(bank[6][:, k * P:(k + 1) * P], onehot[0:NBP, j, :], onehot[0:NBP, j, :], start=True, stop=True)
                return last

            def first_of(onehot, base, g):
                for j in range(TG):
                    last = mm(bank[7][:, P + 3 * j:P + 3 * j + 3], onehot[0:NBP, j, :],
                              base[:, bass.ds(g * TG + j, 1), :].rearrange("k t c -> k (t c)"), start=True, stop=True)
                return last

            pe.wait_ge(s["flag_ready"], 1)
            unsorted = pe.value_load(flag_i[0:1, 1:2], min_val=0, max_val=1)
            with pe.If(unsorted):
                with pe.Fori(0, NG) as g:
                    pe.wait_ge(s["slow_oht"], g + 1)
                    first_of(oht[:, 0], base3d, g)
                    for h in range(2):
                        need(pe, s["slow_own"], 2 * g + h if h else 0)
                        tile_sums(h, oht[:, 0]).then_inc(s["slow_sums"], 1)

            def attributes(it, b):
                g = 2 * it + b
                pe.wait_ge(attr_in[b], it * 16 + 16)
                need(pe, s["digits_read"], g)
                pe.nop(nofuse=True)
                tr(bank[7][0:TG * A, 0:P], attr[:, b, :], ident[:, :]).then_inc(s["attr_tr"], 1)

            def hidden(g, h):
                if h == 0:
                    pe.wait_ge(s["attr_sb"], g + 1)
                need(pe, s["silu_done"], 2 * g + h - 1)
                for k in range(4):
                    last = mm(bank[h][:, k * P:(k + 1) * P], w1pad[:, 4 * h + k, :], attr_t[0:TG * A, :], start=True, stop=True)
                last.then_inc(s["h_ready"], 1)

            def weights(g, h):
                pe.wait_ge(s["silu_done"], 2 * g + h + 1)
                need(pe, s["msg_ready"], 2 * g + h - 1)
                for k in range(4):
                    o = bank[2 + h][:, k * P:(k + 1) * P]
                    mm(o, ht[:, h, k * P:(k + 1) * P], w2s[:, :], start=True, stop=False)
                    last = mm(o, ones_b[0:3, :], b2s[:, :], start=False, stop=True)
                last.then_inc(s["w_ready"], 1)

            def edge_group(it, last_one=False):
                for b in range(2):
                    g = 2 * it + b
                    pe.wait_ge(s["oht_ready"], g + 1)
                    need(pe, s["attr_sb"], g + 1)
                    first_of(oht[:, b], base3, g).then_inc(s["base_ready"], 1)
                    for h in range(2):
                        need(pe, s["ranked"], 2 * g + h)
                        tile_sums(h, oht[:, b]).then_inc(s["sums_ready"], 1)
                        if h == 0:
                            pe.wait_ge(s["wsel_ready"], g + 1)
                            pe.wait_ge(win_in[b], it * 16 + 16)
                        need(pe, s["xj_sb"], 2 * g + h - 1)
                        for k in range(4):
                            j = 4 * h + k
                            last = mm(bank[4 + h][:, k * P:(k + 1) * P], wsel[:, j, :],
                                      win[:, b, bass.ds(wide * j, 1), :].rearrange("p o d -> p (o d)"), start=True, stop=True)
                        last.then_inc(s["xj_ready"], 1)
                    more = not (last_one and b)
                    if more:
                        if last_one:
                            pe.wait_ge(attr_in[1], (NG // 2 - 1) * 16 + 16 * (2 + 2 * (LJ > 0)))
                        attributes(it + b, 1 - b)
                    for h in range(2):
                        weights(g, h)
                        if more:
                            hidden(g + 1, h)

            pe.wait_ge(s["prepared"], 1)
            pe.wait_ge(s["w1_in"], 16 * TG)
            pe.wait_ge(s["aux_in"], 16 * 6)
            wide = pe.value_load(flag_i[0:1, 0:1], min_val=0, max_val=1)
            attributes(0, 0)
            for h in range(2):
                hidden(0, h)
            edge_group(0)
            with pe.Fori(1, NG // 2 - 1) as it:
                edge_group(it)
            edge_group(NG // 2 - 1, last_one=True)

            def sums0(it):
                for k in range(8):
                    pe.wait_ge(s["oh0_ready"], it * 8 + k + 1)
                    need(pe, s["add0_done"], it * 8 + k - 7)
                    for i in range(2):
                        last = mm(bank[k][:, 0:D], oh0[:, k, i, :], mtile[:, k, i, 0:D], start=(i == 0), stop=(i == 1))
                    last.then_inc(s["sum0_ready"], 1)

            pe.wait_ge(s["msg_ready"], 2 * NG)
            sums0(0)
            with pe.Fori(1, IT0) as it:
                sums0(it)

            pe.wait_ge(s["add0_done"], V0)

            def update(it):
                for i in range(2 * SB + 1):
                    if i < 2 * SB:
                        nb, h = 2 * SB * it + i, i // SB
                        if i % SB == 0:
                            pe.wait_ge(x_staged[h], it * 32 + 32)
                        need(pe, s["xt_sb"], nb - 1)
                        for c in range(2):
                            last = tr(bank[i % 2][:, c * P:(c + 1) * P], ustage[:, h, c, i % SB, :], ident[:, :])
                        last.then_inc(s["x_t"], 1)
                    if i >= 1:
                        k = i - 1
                        nb, o = 2 * SB * it + k, bank[2 + k % 6][:, 0:D]
                        pe.wait_ge(s["xt_sb"], nb + 1)
                        need(pe, s["u_added"], nb - (5 if k >= 2 else 1))
                        mm(o, uxt[:, k % 2, 0:P], wcomb[:, :], start=True, stop=False)
                        mm(o, uxt[:, k % 2, P:2 * P], wbot[:, :], start=False, stop=False)
                        mm(o, ones[0:1, :], bias0[0:1, :], start=False, stop=True).then_inc(s["u_ready"], 1)

            update(0)
            with pe.Fori(1, ITU) as it:
                update(it)

            pe.wait_ge(s["u_store"], NB)
            for half in range(2):
                def sums1(it):
                    for q in range(4):
                        pe.wait_ge(s["oh1_ready"], half * V1 // TG + it * 4 + q + 1)
                        pe.wait_ge(gathered[q], 16 * TG * (it + half * IT1 + 1))
                        need(pe, s["add1_done"], half * V1 + it * NS + (q - 1) * TG)
                        for k in range(TG):
                            last = mm(bank[q % 2 * 4 + k // 2][:, (k % 2) * 256:(k % 2) * 256 + CW], oh1[:, q % 2, k, :], grow[:, q * TG + k, :], start=True, stop=True)
                        last.then_inc(s["sum1_ready"], 1)

                sums1(0)
                with pe.Fori(1, IT1) as it:
                    sums1(it)

            pe.wait_ge(s["g_mean"], 2)

            def gru(it):
                for i in range(2 * SB + 1):
                    if i < 2 * SB:
                        nb, h = 2 * SB * it + i, i // SB
                        if i % SB == 0:
                            pe.wait_ge(h_staged[h], it * 48 + 48)
                        need(pe, s["g_tsb"], nb)
                        for c in range(3):
                            tr(bank[0][:, c * P:(c + 1) * P], gstage[:, h, c, i % SB, :], ident[:, :])
                        mm(bank[0][0:9, 3 * P:4 * P], aux9[:, bass.ds(nb, 1), :, :].rearrange("p n c r -> p (n c r)"), ident_b[:, :], start=True, stop=True).then_inc(s["g_t"], 1)
                    if i >= 1:
                        k = i - 1
                        nb, o = 2 * SB * it + k, bank[1 + k % SB]
                        pe.wait_ge(s["g_tsb"], nb + 1)
                        need(pe, s["g_cand"], nb - SB + 1)
                        mm(o[:, :], auxt[0:9, k % 2, :], auxw9[:, :], start=True, stop=False)
                        mm(o[:, 0:3 * D], gxt[:, k % 2, 0:P], m_in[:, :], start=False, stop=False)
                        mm(o[:, 0:3 * D], gxt[:, k % 2, P:2 * P], m_out[:, :], start=False, stop=False)
                        mm(o[:, D:4 * D], gxt[:, k % 2, 2 * P:3 * P], whh_t[:, :], start=False, stop=True).then_inc(s["g_lin"], 1)

            gru(0)
            with pe.Fori(1, ITU) as it:
                gru(it)


_INS = ['x', 'src', 'dst', 'edge_attr_8', 'L0_gnn_W1', 'L0_gnn_b1', 'L0_gnn_W2', 'L0_gnn_b2', 'L0_gnn_Wself', 'L0_gnn_bself',
        'L0_gnn_Wcat', 'L0_gnn_bcat', 'L1_gnn_W_in', 'L1_gnn_b_in', 'L1_gnn_W_out', 'L1_gnn_b_out', 'L1_gnn_w_ih', 'L1_gnn_w_hh',
        'L1_gnn_b_ih', 'L1_gnn_b_hh']


def kernel(**inputs):
    import numpy as _np
    import concourse.bacc as _bacc
    from concourse import mybir as _mybir
    from concourse.bass_utils import run_bass_kernel_spmd as _run

    nc = _bacc.Bacc("TRN2", target_bir_lowering=False, num_devices=1)
    arrays, args = {}, []
    for name in _INS:
        a = _np.ascontiguousarray(inputs[name])
        arrays[f"in_{name}_dram"] = a
        args.append(nc.dram_tensor(f"in_{name}_dram", a.shape, _mybir.dt.from_np(a.dtype), kind="ExternalInput").ap())
    out = nc.dram_tensor("out_0_dram", (N, D), _mybir.dt.float32, kind="ExternalOutput").ap()
    gnn_kernel(nc, *args, out)
    return _run(nc, [arrays], core_ids=[0]).results[0]["out_0_dram"]
```

```python
import concourse.bass as bass
from concourse import mybir
from concourse.alu_op_type import AluOpType as ALU
from contextlib import ExitStack

N, E, D, A = 12500, 212500, 128, 8
P = 128
TG = 8
GE = TG * P
NG = -(-E // GE)
NG += NG % 2
EP = NG * GE
T = NG * TG
NB = -(-N // P)
NPAD = NB * P
NBP = NB + 1
PAD = NPAD
NQ = 104
QE = EP // NQ
QG = QE // GE
RW = 136
U0, U1 = 2 * P, P
NS = 32
V0 = -(-(E // U0 + NB) // NS) * NS
V1 = -(-(E // U1 + NB) // NS) * NS
CW = D + 1
SB = 7
EPS = 1e-5


class Steps:

    def __init__(self, eng, sem):
        self.eng, self.sem, self.n, self.it, self.per = eng, sem, 0, None, 0

    def loop(self, it, per):
        self.it, self.per, self.first = it, per, self.n

    def end(self, trips):
        assert self.n - self.first == self.per, (self.n - self.first, self.per)
        self.n, self.it = self.first + trips * self.per, None

    def value(self):
        return self.n if self.it is None else self.it * self.per + self.n

    def wait(self):
        self.eng.wait_ge(self.sem, self.value())

    def mark(self, ins):
        ins.then_inc(self.sem, 1)
        self.n += 1

    def link(self, ins):
        self.mark(ins)
        self.wait()


def need(eng, sem, value):
    if not isinstance(value, int) or value > 0:
        eng.wait_ge(sem, value)


def hold(pool, sem, value):
    if not isinstance(value, int) or value > 0:
        pool.wait_ge(sem, value)
        pool.nop(nofuse=True)


def gnn_kernel(nc, x, src, dst, edge_attr, W1, b1, W2, b2, Wself, bself, Wcat, bcat,
               W_in, b_in, W_out, b_out, w_ih, w_hh, b_ih, b_hh, out):
    f32, i32, bf16 = mybir.dt.float32, mybir.dt.int32, mybir.dt.bfloat16
    ACT, AX = mybir.ActivationFunctionType, mybir.AxisListType

    def dram(name, shape, dt):
        return nc.dram_tensor(name, shape, dt, kind="Internal").ap()

    xwin = dram("xwin", [NPAD + EP, D], f32)
    x1d = dram("x1d", [NPAD, D], f32)
    rows3 = dram("rows3", [NG, 3, GE], bf16)
    winrow = dram("winrow", [T], i32)
    dlist = dram("dlist", [EP, 2], f32)
    dtmp = dram("dtmp", [EP, 2], f32)
    msgs = dram("msgs", [EP, RW], f32)
    vtab = dram("vtab", [6, V1], i32)

    ctx = ExitStack()
    with ctx:
        def sb(name, shape, dt=f32):
            return ctx.enter_context(nc.sbuf_tensor(name, shape, dt))

        def sem(name):
            return ctx.enter_context(nc.semaphore(name))

        acc_a = sb("acc_a", [P, NBP * CW])
        acc_b = sb("acc_b", [P, NBP * CW])
        src_key = sb("src_key", [P, T])
        dst_idx = sb("dst_idx", [P, T], i32)
        base3 = sb("base3", [NBP, T, 3], bf16)
        blk0 = sb("blk0", [P, V0], i32)
        blk1s = sb("blk1s", [P, V1])
        blk1d = sb("blk1d", [P, V1])
        ident = sb("ident", [P, P])
        earlier = sb("earlier", [P, P])
        tri = sb("tri", [P, P])
        iota_row = sb("iota_row", [P, P])
        iota_c = sb("iota_c", [P, 1])
        iota_k = sb("iota_k", [P, NBP + 1], bf16)
        ones = sb("ones", [P, P])
        ones_b = sb("ones_b", [P, P], bf16)
        w1pad = sb("w1pad", [TG * A, TG, D])
        w2s = sb("w2s", [P, D])
        b1c = sb("b1c", [P, 1])
        b2row = sb("b2row", [1, 4, D])
        b2parts = sb("b2parts", [1, 3, D], bf16)
        b2s = sb("b2s", [3, D], bf16)
        wcomb = sb("wcomb", [P, D])
        wbot = sb("wbot", [P, D])
        bias0 = sb("bias0", [1, D])
        m_in = sb("m_in", [P, 3 * D])
        m_out = sb("m_out", [P, 3 * D])
        whh_t = sb("whh_t", [P, 3 * D])
        auxw = sb("auxw", [3, 4 * D])
        auxw9 = sb("auxw9", [9, 4 * D], bf16)
        some_mv = sb("some_mv", [P, 2 * SB, 2])
        prior = sb("prior", [P, 2, 2 * SB])
        flag_f = sb("flag_f", [P, 2])
        flag_i = sb("flag_i", [P, 2], i32)

        ARENA = 11264
        arena = sb("arena", [P, ARENA])

        def cutter(whole, size):
            at = [0]

            def cut(n, dt=f32):
                words = n if dt != bf16 else -(-n // 2)
                got = whole[:, at[0]:at[0] + words]
                at[0] += words
                assert at[0] <= size, (at[0], size)
                return got if dt == f32 else got.bitcast(dt)
            return cut

        cut = cutter(arena, ARENA)
        win = cut(2 * TG * D).rearrange("p (b j d) -> p b j d", b=2, j=TG)
        rowsb = cut(2 * 2 * GE, bf16).rearrange("p (b r e) -> p b r e", b=2, r=2)
        attr = cut(2 * TG * A).rearrange("p (b c) -> p b c", b=2)
        attr_t = cut(P)
        oht = cut(2 * GE, bf16).rearrange("p (b j e) -> p b j e", b=2, j=TG)
        wsel = cut(GE).rearrange("p (j e) -> p j e", j=TG)
        ht = cut(2 * 4 * P).rearrange("p (h e) -> p h e", h=2)
        xjs = cut(2 * 4 * P).rearrange("p (h e) -> p h e", h=2)
        mrow = cut(2 * TG * RW).rearrange("p (b j c) -> p b j c", b=2, j=TG)
        pos = cut(2 * TG, i32).rearrange("p (b j) -> p b j", b=2)
        junk = cut(TG * P, bf16).rearrange("p (j e) -> p j e", j=TG)
        rank = cut(TG)
        digits = cut(3 * TG).rearrange("p (j c) -> p j c", c=3)
        posf = cut(2 * TG).rearrange("p (s j) -> p s j", s=2)
        drow = cut(TG * 2).rearrange("p (j c) -> p j c", c=2)
        widx = cut(TG, i32)
        cut = cutter(arena, ARENA)
        S0 = 16
        mtile = cut(S0 * 2 * RW).rearrange("p (s i c) -> p s i c", s=S0, i=2)
        oh0 = cut(S0 * 2 * P).rearrange("p (s i n) -> p s i n", s=S0, i=2)
        local = cut(2 * 4 * 2).rearrange("p (b s i) -> p b s i", b=2, s=4)
        cut = cutter(arena, ARENA)
        ustage = cut(2 * 2 * SB * D).rearrange("p (h c n d) -> p h c n d", h=2, c=2, n=SB)
        uxt = cut(2 * 2 * P).rearrange("p (b c) -> p b c", b=2)
        stats = cut(2 * SB * 6).rearrange("p (b c) -> p b c", c=6)
        auxp = cut(3 * 4 * D, bf16).rearrange("p (c f) -> p c f", c=3)
        cut = cutter(arena, ARENA)
        gstage = cut(2 * 3 * SB * D).rearrange("p (h c n d) -> p h c n d", h=2, c=3, n=SB)
        gxt = cut(2 * 3 * P).rearrange("p (b c) -> p b c", b=2)
        auxt = cut(2 * P, bf16).rearrange("p (b c) -> p b c", b=2)
        gates = cut(SB * 3 * D).rearrange("p (b c) -> p b c", b=SB)
        keep = cut(SB * D).rearrange("p (b c) -> p b c", b=SB)
        gstats = cut(2 * SB * 6).rearrange("p (b c) -> p b c", c=6)
        cut = cutter(src_key, T)
        aux9 = cut(NB * 9, bf16).rearrange("p (n c r) -> p n c r", c=3, r=3)
        ident_b = cut(P, bf16)
        rcnt = cut(NB).rearrange("p (n o) -> p n o", o=1)
        cut = cutter(arena, ARENA)
        grow = cut(NS * CW).rearrange("p (s c) -> p s c", s=NS)
        edge2 = cut(NS * 2).rearrange("p (s c) -> p s c", s=NS)
        oh1 = cut(2 * TG * P).rearrange("p (b s n) -> p b s n", b=2, s=TG)

        cut = cutter(acc_a, NBP * CW)
        dst_n = cut(QE, i32)
        src_n = cut(QE, i32)
        next_n = cut(QE, i32)
        tmp_n = cut(QE)
        tile_p = cut(GE, i32)
        signs = acc_a[:, 4 * QE + GE:5 * QE + GE].bitcast(bf16).rearrange("p (b e) -> p b e", b=2)
        rows_n = cut(QG * 3 * GE, bf16).rearrange("p (g r e) -> p g r e", g=QG, r=3)
        below = cut(2 * (NBP + 1))
        cut = cutter(acc_b, NBP * CW)
        base3d = acc_b[0:NBP, 0:T * 3 // 2].bitcast(bf16).rearrange("k (t c) -> k t c", c=3)
        onek_d = acc_b[:, T * 3 // 2:T * 3 // 2 + TG * NBP].bitcast(bf16).rearrange("p (s j k) -> p s j k", s=2, j=TG)
        pair_n = cut(QE * 2).rearrange("p (e c) -> p e c", c=2)
        src_p = cut(T, i32)
        blk_d = src_p[:, 0:T // 2].bitcast(bf16)
        dst_p = cut(T, i32)
        hist_s = cut(T)
        hist_d = cut(T)
        brow = cut(7 * D)
        rows_w = cut(2 * 3 * D).rearrange("p (c f) -> p c f", c=2)
        cut = cutter(arena, ARENA)
        onek = cut(4 * TG * (NBP + 1), bf16).rearrange("p (s j k) -> p s j k", s=4, j=TG)
        blk_s = cut(T)
        sumt = cut(T)
        iota_i = cut(V1, i32)
        wih_n = cut(3 * 2 * D).rearrange("p (c f) -> p c f", c=3)
        whh_n = cut(3 * D).rearrange("p (c f) -> p c f", c=3)
        iota_v = cut(V1)
        wself_n, wself_t, wtop, win_n, wout_n = (cut(D) for _ in range(5))
        wih_t = cut(2 * 3 * D).rearrange("p (d f) -> p d f", d=2)
        cut = cutter(acc_a, NBP * CW)
        ge_start = cut(V1)
        ge_end = cut(V1)
        off_f = cut(V1)
        vrow = cut(2 * V1, i32).rearrange("p (c v) -> p c v", c=2)
        sumt2 = cut(T)
        cols = sb("cols", [P, 3])
        row2 = sb("row2", [1, 4 * D])
        lohi = sb("lohi", [P, 4, QG])
        viol = sb("viol", [P, 2])
        slowrow = sb("slowrow", [P, QG, TG], i32)
        lorow = sb("lorow", [P, 2, QG, TG])
        lorow_i = sb("lorow_i", [P, QG, TG], i32)
        kcol = sb("kcol", [P, 16])
        kcol_i = sb("kcol_i", [P, 2], i32)
        coef = sb("coef", [P, P])

        bank = [ctx.enter_context(nc.psum_tensor(f"bank{i}", [P, 512], f32)) for i in range(8)]

        names = """pads pool_const edges_in weights_in attr_w small_in dve_step act_step pe_weights act_weights dve_weights
        aux_in blocks_ready counted hist_ready flags_sum flag_ready prep_out start_in start_sum tables_sum tables_read
        tables_out prepared window_ready dst_sorted slow_in slow_oht slow_sums slow_rank slow_pos slow_step
        flag_pe x1_out out_done u_stats u_var u_root y_ready g_var g_root slow_own reg_dve gru_step list_copied attr_tr attr_sb oht_ready wsel_ready h_ready silu_done sums_ready ranked base_ready pos_ready xj_ready
        xj_sb w_ready msg_ready key_ready acc_zero oh0_ready sum0_ready add0_done x_t xt_sb u_ready u_store
        x1_ready oh1_ready sum1_ready add1_done g_mean g_t g_tsb g_lin g_gate g_mult g_kept g_cand g_tanh g_part g_out g_stats g_moments u_added u_moments u_kept g_mv u_inv g_inv aux_split xcopy pool_step
        gather_own upd_step grow_ones out_final w1_in slow_pool lotab_out reg_done wide_in digits_read local_ready edges_below slow_blocks slow_counted slow_hist limits""".split()
        s = {n: sem(n) for n in names}
        win_in = [sem(f"win_in{i}") for i in range(2)]
        rows_in = [sem(f"rows_in{i}") for i in range(2)]
        attr_in = [sem(f"attr_in{i}") for i in range(2)]
        scattered = [sem(f"scattered{i}") for i in range(2)]
        mtile_in = [sem(f"mtile_in{i}") for i in range(S0 // 4)]
        edge2_in = [sem(f"edge2_in{i}") for i in range(4)]
        gathered = [sem(f"gathered{i}") for i in range(4)]
        x_staged = [sem(f"x_staged{i}") for i in range(2)]
        h_staged = [sem(f"h_staged{i}") for i in range(2)]
        block = ctx.enter_context(nc.Block())

        LAST = E - (NG - 1) * GE
        LP, LJ = LAST // TG, LAST % TG
        NLAST = E - (NQ - 1) * QE
        N_EDGES = 2 * (2 + (LJ > 0)) + 6
        PASSES = [(U0, V0, blk0, 0), (U1, V1, blk1s, 2), (U1, V1, blk1d, 4)]
        IT0, IT1, ITU = V0 // NS, V1 // NS, NB // (2 * SB)
        HCHUNK = 512

        def registers(eng, name, n):
            return [eng.alloc_register(f"{name}{i}") for i in range(n)]

        def load_table(eng, regs, row, v, top):
            eng.load(regs, vtab[row:row + 1, bass.ds(v, len(regs))])
            return [eng.snap(r, min_val=0, max_val=top) for r in regs]

        @block.sync
        def _(sp):
            sp.wait_ge(s["pads"], 5)
            for to, of in ((src_p, src), (dst_p, dst)):
                v = to.rearrange("p (g j) -> p g j", j=TG)
                sp.dma_start(v[:, 0:NG - 1, :], of[0:(NG - 1) * GE].rearrange("(g p j) -> p g j", p=P, j=TG)).then_inc(s["edges_in"], 16)
                sp.dma_start(v[0:LP, NG - 1, :], of[(NG - 1) * GE:(NG - 1) * GE + LP * TG].rearrange("(p j) -> p j", j=TG)).then_inc(s["edges_in"], 16)
                if LJ:
                    sp.dma_start(v[LP:LP + 1, NG - 1, 0:LJ], of[E - LJ:E].rearrange("(p j) -> p j", p=1)).then_inc(s["edges_in"], 16)
            for to, of, shift in ((src_n, src, 0), (dst_n, dst, 0), (next_n, dst, 1)):
                sp.dma_start(to[0:NQ - 1, :], of[shift:shift + (NQ - 1) * QE].rearrange("(q e) -> q e", e=QE)).then_inc(s["edges_in"], 16)
                sp.dma_start(to[NQ - 1:NQ, 0:NLAST - shift], of[(NQ - 1) * QE + shift:E].rearrange("(q e) -> q e", q=1)).then_inc(s["edges_in"], 16)
            sp.dma_start(xwin[0:N, :].rearrange("(a b) d -> a (b d)", a=100), x.rearrange("(a b) d -> a (b d)", a=100)).then_inc(s["xcopy"], 16)
            sp.wait_ge(s["pool_const"], 1)
            sp.dma_start(xwin[N:NPAD, :], coef[0:NPAD - N, :]).then_inc(s["xcopy"], 16)
            sp.wait_ge(s["dve_weights"], 1)
            for j in range(TG):
                sp.dma_start(w1pad[j * A:(j + 1) * A, j, :], W1).then_inc(s["w1_in"], 16)
            sp.wait_ge(s["prep_out"], 1)
            sp.dma_start(rows3.rearrange("(q g) r e -> q (g r e)", g=QG), rows_n[0:NQ].rearrange("q g r e -> q (g r e)")).then_inc(s["lotab_out"], 16)
            sp.dma_start(winrow.rearrange("(q c) -> q c", c=QG * TG), lorow_i[0:NQ].rearrange("q g j -> q (g j)")).then_inc(s["lotab_out"], 16)
            sp.dma_start(dlist.rearrange("(q e) c -> q (e c)", e=QE), pair_n[0:NQ].rearrange("q e c -> q (e c)")).then_inc(s["lotab_out"], 16)
            sp.wait_ge(s["dve_weights"], 2)
            for c in range(3):
                sp.dma_start(b2s[c:c + 1, :], b2parts[0:1, c, :]).then_inc(s["aux_in"], 16)
            sp.wait_ge(s["dve_weights"], 3)
            sp.wait_ge(s["act_weights"], 8)
            sp.dma_start(auxw[0:1, 0:3 * D], rows_w[0:1, 0, :]).then_inc(s["aux_in"], 16)
            sp.dma_start(auxw[1:2, 0:3 * D], rows_w[0:1, 1, :]).then_inc(s["aux_in"], 16)
            sp.dma_start(auxw[2:3, :], row2[0:1, :]).then_inc(s["aux_in"], 16)
            for i, (U, V, _, row) in enumerate(PASSES):
                sp.wait_ge(s["tables_read"], i + 1)
                sp.dma_start(vtab[row:row + 2, 0:V].rearrange("(o c) v -> o c v", o=1), vrow[0:1, :, 0:V]).then_inc(s["tables_out"], 16)
            sp.wait_ge(s["lotab_out"], 48)
            sp.wait_ge(s["xcopy"], 32)

            sp.wait_ge(s["flag_ready"], 1)
            unsorted = sp.value_load(flag_i[0:1, 1:2], min_val=0, max_val=1)
            with sp.If(unsorted):
                with sp.Fori(0, NG) as g:
                    sp.wait_ge(s["slow_pool"], g + 1)
                    sp.dma_start(rowsb[:, 0, 0, :], rows3[bass.ds(g, 1), 2, :].to_broadcast([P, GE])).then_inc(s["slow_in"], 16)
                    sp.dma_start(drow, dlist[bass.ds(g * GE, GE), :].rearrange("(p j) c -> p j c", j=TG)).then_inc(s["slow_in"], 16)

            regs = registers(sp, "sp_win", 2 * TG)
            sp.wait_ge(s["window_ready"], 1)
            wide = sp.value_load(flag_i[0:1, 0:1], min_val=0, max_val=1)
            sp.wait_ge(s["prepared"], 1)

            def edge_loads(it, last=False):
                sp.load(regs, winrow[bass.ds(it * 2 * TG, 2 * TG)].rearrange("(o t) -> o t", o=1))
                for b in range(2):
                    g = 2 * it + b
                    need(sp, s["wsel_ready"], g - 1)
                    sp.dma_start(rowsb[:, b, :, :], rows3[bass.ds(g, 1), 0:2, :].to_broadcast([P, 2, GE])).then_inc(rows_in[b], 16)
                    need(sp, s["attr_tr"], g - 1)
                    if last and b == 1:
                        av = attr[:, b, :].rearrange("p (j a) -> p j a", a=A)
                        e0 = (NG - 1) * GE
                        sp.dma_start(attr[0:LP, b, :], edge_attr[e0:e0 + LP * TG, :].rearrange("(p j) a -> p (j a)", j=TG)).then_inc(attr_in[b], 16)
                        k = 16
                        if LJ:
                            sp.dma_start(av[LP:LP + 1, 0:LJ, :], edge_attr[E - LJ:E, :].rearrange("(p j) a -> p j a", p=1)).then_inc(attr_in[b], 16)
                            sp.dma_start(av[LP:LP + 1, LJ:TG, :], edge_attr[0:TG - LJ, :].rearrange("(p j) a -> p j a", p=1)).then_inc(attr_in[b], 16)
                            k += 32
                        r = LP + (LJ > 0)
                        sp.dma_start(attr[r:P, b, :], edge_attr[0:(P - r) * TG, :].rearrange("(p j) a -> p (j a)", j=TG)).then_inc(attr_in[b], 16)
                    else:
                        sp.dma_start(attr[:, b, :], edge_attr[bass.ds(g * GE, GE), :].rearrange("(p j) a -> p (j a)", j=TG)).then_inc(attr_in[b], 16)
                    need(sp, s["xj_ready"], 2 * g - 2)

                    def window(j, done):
                        r = sp.snap(regs[b * TG + j], min_val=0, max_val=NPAD + EP - P)
                        sp.dma_start(win[:, b, j, :], xwin[bass.ds(r, P), :]).then_inc(done, 16)

                    sp.nop(nofuse=True)
                    with sp.If(wide):
                        for j in range(1, TG):
                            window(j, s["wide_in"])
                        sp.wait_ge(s["wide_in"], g * (16 * (TG - 1)) + 16 * (TG - 1))
                        sp.nop(nofuse=True)
                    window(0, win_in[b])

            edge_loads(0)
            with sp.Fori(1, NG // 2 - 1) as it:
                edge_loads(it)
            edge_loads(NG // 2 - 1, last=True)

            sp.wait_ge(scattered[0], 16 * TG * (NG // 2))
            sp.wait_ge(scattered[1], 16 * TG * (NG // 2))
            sp.wait_ge(s["msg_ready"], 2 * NG)
            regs0 = registers(sp, "sp_row", NS)
            sp.wait_ge(s["tables_out"], 48)

            def row_loads(it):
                offs = load_table(sp, regs0, 0, it * NS, EP - U0)
                for k in range(0, NS, 2):
                    need(sp, s["sum0_ready"], it * NS + k - S0 + 1)
                    sp.dma_start(mtile[:, k % S0, :, :], msgs[bass.ds(offs[k], U0), :].rearrange("(p i) c -> p i c", i=2)).then_inc(mtile_in[k % S0 // 4], 16)

            row_loads(0)
            with sp.Fori(1, IT0) as it:
                row_loads(it)

            sum_rows = acc_a[:, 0:NB * D].rearrange("p (n d) -> p n d", d=D)

            def update_in(it):
                for h in range(2):
                    c = 2 * it + h
                    need(sp, s["u_added"], (c - 1) * SB)
                    sp.dma_start(ustage[:, h, 0], xwin[bass.ds(c * (SB * P), SB * P), :].rearrange("(n p) d -> p n d", p=P)).then_inc(x_staged[h], 16)
                    sp.dma_start(ustage[:, h, 1], sum_rows[:, bass.ds(c * SB, SB), :]).then_inc(x_staged[h], 16)

            sp.wait_ge(s["add0_done"], V0)
            update_in(0)
            with sp.Fori(1, ITU) as it:
                update_in(it)
            sp.wait_ge(s["x1_out"], 16 * (NB // SB))
            sp.wait_ge(s["aux_split"], 1)
            for c in range(3):
                sp.dma_start(auxw9[3 * c:3 * c + 3, :], auxp[0:3, c, :]).then_inc(s["aux_in"], 16)
            sp.wait_ge(s["aux_in"], 16 * 9)

            regs1 = registers(sp, "sp_edge", NS)
            sp.wait_ge(s["dst_sorted"], 1)
            for half, row in ((0, 2), (1, 4)):
                first = half * V1 // TG

                def edge2_loads(it):
                    offs = load_table(sp, regs1, row, it * NS, EP - U1)
                    for q in range(4):
                        need(sp, s["sum1_ready"], first + it * 4 + q - 3)
                        for k in range(TG):
                            of = msgs[bass.ds(offs[q * TG + k], U1), D:D + 2] if half == 0 else dlist[bass.ds(offs[q * TG + k], U1), :]
                            sp.dma_start(edge2[:, q * TG + k, :], of).then_inc(edge2_in[q], 16)

                edge2_loads(0)
                with sp.Fori(1, IT1) as it:
                    edge2_loads(it)

            mean_rows = [a[:, 0:NB * CW].rearrange("p (n c) -> p n c", c=CW) for a in (acc_a, acc_b)]

            def gru_in(it):
                for h in range(2):
                    c = 2 * it + h
                    need(sp, s["g_out"], (c - 1) * SB)
                    for k in range(2):
                        sp.dma_start(gstage[:, h, k], mean_rows[k][:, bass.ds(c * SB, SB), 0:D]).then_inc(h_staged[h], 16)
                    sp.dma_start(gstage[:, h, 2], x1d[bass.ds(c * (SB * P), SB * P), :].rearrange("(n p) d -> p n d", p=P)).then_inc(h_staged[h], 16)

            sp.wait_ge(s["g_mean"], 2)
            gru_in(0)
            with sp.Fori(1, ITU) as it:
                gru_in(it)
            sp.wait_ge(s["out_done"], 16 * (NB // SB + 1))

        @block.gpsimd
        def _(pool):
            st = Steps(pool, s["pool_step"])
            loads = [(w2s[:, :], W2), (wself_n[:, :], Wself), (wtop[:, :], Wcat[0:D, :]), (wbot[:, :], Wcat[D:2 * D, :]),
                     (win_n[:, :], W_in), (wout_n[:, :], W_out), (wih_n, w_ih.rearrange("(c p) f -> p c f", p=P)),
                     (whh_n, w_hh.rearrange("(c p) f -> p c f", p=P)), (b1c[:, :], b1.rearrange("(p o) -> p o", o=1)),
                     (cols[:, 0:1], bself.rearrange("(p o) -> p o", o=1)), (cols[:, 1:2], b_in.rearrange("(p o) -> p o", o=1)),
                     (cols[:, 2:3], b_out.rearrange("(p o) -> p o", o=1)), (b2row[0:1, 0, :], b2.rearrange("(o f) -> o f", o=1)),
                     (brow[0:1, 0:D], bcat.rearrange("(o f) -> o f", o=1)), (brow[0:1, D:4 * D], b_ih.rearrange("(o f) -> o f", o=1)),
                     (brow[0:1, 4 * D:7 * D], b_hh.rearrange("(o f) -> o f", o=1))]
            st.link(pool.memset(coef[:, :], 0.0))
            pool.memset(ones[:, :], 1.0).then_inc(s["pool_const"], 1)
            pool.memset(ones_b[:, :], 1.0).then_inc(s["pool_const"], 1)
            for m, fill, start, op, cm, step in ((ident, 1.0, 0.0, ALU.not_equal, 1, -1), (earlier, 0.0, 1.0, ALU.is_gt, 1, -1),
                                                 (tri, 0.0, 1.0, ALU.is_gt, -1, 1)):
                st.link(pool.memset(m[:, :], start))
                pool.affine_select(out=m[:, :], in_=m[:, :], compare_op=op, fill=fill, base=0, pattern=[[step, P]],
                                   channel_multiplier=cm).then_inc(s["pool_const"], 1)
            pool.iota(iota_i, pattern=[[1, V1]], base=0, channel_multiplier=0).then_inc(s["pool_const"], 1)
            pool.iota(kcol_i[:, 0:1], pattern=[[0, 1]], base=0, channel_multiplier=1).then_inc(s["pool_const"], 1)
            pool.iota(slowrow[0:NQ].rearrange("q g j -> q (g j)"), pattern=[[P, QG * TG]], base=NPAD,
                      channel_multiplier=QG * TG * P).then_inc(s["pool_const"], 1)
            pool.iota(tile_p, pattern=[[1, P], [0, TG]], base=0, channel_multiplier=0).then_inc(s["pool_const"], 1)
            for to, of in loads:
                pool.dma_start(to, of).then_inc(s["weights_in"], 16)

            pool.wait_ge(s["flag_ready"], 1)
            wide = pool.value_load(flag_i[0:1, 0:1], min_val=0, max_val=1)
            with pool.If(wide):
                with pool.Fori(0, NG) as g:
                    pool.tensor_copy(widx, dst_idx[:, bass.ds(g * TG, TG)]).then_inc(s["gather_own"], 1)
                    hold(pool, s["gather_own"], g + 1)
                    for j in range(TG):
                        pool.indirect_dma_start(win[:, 0, j, :], None, x, bass.IndirectOffsetOnAxis(ap=widx[:, j:j + 1], axis=0)).then_inc(s["slow_step"], 16)
                    hold(pool, s["slow_step"], g * (16 * (TG + 1)) + 16 * TG)
                    pool.dma_start(xwin[bass.ds(g * GE + NPAD, GE), :].rearrange("(j p) d -> p j d", p=P), win[:, 0, :, :]).then_inc(s["slow_step"], 16)
                    hold(pool, s["slow_step"], g * (16 * (TG + 1)) + 16 * (TG + 1))
            unsorted = pool.value_load(flag_i[0:1, 1:2], min_val=0, max_val=1)
            with pool.If(unsorted):
                with pool.Fori(0, NG) as g:
                    hold(pool, s["slow_pos"], g + 1)
                    hold(pool, s["slow_in"], g * 32 + 32)
                    for j in range(TG):
                        pool.indirect_dma_start(dtmp, bass.IndirectOffsetOnAxis(ap=pos[:, 0, j:j + 1], axis=0), drow[:, j, :], None).then_inc(s["reg_done"], 16)
                    hold(pool, s["reg_done"], g * (16 * TG) + 16 * TG)
                    pool.sem_inc(s["slow_pool"], 1)
                pool.dma_start(dlist.rearrange("(q e) c -> q (e c)", e=QE), dtmp.rearrange("(q e) c -> q (e c)", e=QE)).then_inc(s["list_copied"], 16)
                hold(pool, s["list_copied"], 16)
            pool.sem_inc(s["window_ready"], 1)
            pool.sem_inc(s["dst_sorted"], 1)

            def scatters(it):
                for b in range(2):
                    g = 2 * it + b
                    hold(pool, s["pos_ready"], g + 1)
                    hold(pool, s["key_ready"], 2 * g + 2)
                    hold(pool, s["msg_ready"], 2 * g + 2)
                    for j in range(TG):
                        pool.indirect_dma_start(msgs, bass.IndirectOffsetOnAxis(ap=pos[:, b, j:j + 1], axis=0), mrow[:, b, j, :], None).then_inc(scattered[b], 16)

            with pool.Fori(0, NG // 2) as it:
                scatters(it)

            sum_rows = acc_a[:, 0:NB * D].rearrange("p (n d) -> p n d", d=D)
            with pool.Fori(0, NB // SB) as c:
                hold(pool, s["u_store"], c * SB + SB)
                pool.dma_start(x1d[bass.ds(c * (SB * P), SB * P), :].rearrange("(n p) d -> p n d", p=P),
                               sum_rows[:, bass.ds(c * SB, SB), :]).then_inc(s["x1_out"], 16)

            pool.wait_ge(s["x1_out"], 16 * (NB // SB))
            hold(pool, s["grow_ones"], 1)
            for half in range(2):
                with pool.Fori(0, IT1) as it:
                    for q in range(4):
                        hold(pool, edge2_in[q], 16 * TG * (it + half * IT1 + 1))
                        for k in range(TG):
                            sl = q * TG + k
                            pool.indirect_dma_start(grow[:, sl, 0:D], None, x1d, bass.IndirectOffsetOnAxis(ap=edge2[:, sl, 1:2].bitcast(i32), axis=0)).then_inc(gathered[q], 16)

            y_rows = acc_b[:, 0:NB * CW].rearrange("p (n c) -> p n c", c=CW)
            with pool.Fori(0, NB // SB - 1) as c:
                hold(pool, s["y_ready"], c * SB + SB)
                pool.dma_start(out[bass.ds(c * (SB * P), SB * P), :].rearrange("(n p) d -> p n d", p=P),
                               y_rows[:, bass.ds(c * SB, SB), 0:D]).then_inc(s["out_done"], 16)
            hold(pool, s["y_ready"], NB)
            at, full = NB - SB, N // P
            pool.dma_start(out[at * P:full * P, :].rearrange("(n p) d -> p n d", p=P), y_rows[:, at:full, 0:D]).then_inc(s["out_done"], 16)
            pool.dma_start(out[full * P:N, :], y_rows[0:N - full * P, full, 0:D]).then_inc(s["out_done"], 16)

        @block.scalar
        def _(act):
            act.wait_ge(s["limits"], 1)
            act.wait_ge(s["edges_in"], 16 * N_EDGES)
            act.wait_ge(s["pads"], 5)

            def edges_below(c):
                for k in range(4):
                    n = c * 4 + k
                    need(act, s["edges_below"], n - 1)
                    act.nop(nofuse=True)
                    nc.scalar.activation(signs[0:NQ, k % 2, :], dst_n[0:NQ, :], ACT.Sign, bias=below[0:NQ, bass.ds(n + (NBP + 1), 1)],
                                         accum_out=below[0:NQ, bass.ds(n, 1)]).then_inc(s["edges_below"], 1)

            edges_below(0)
            with act.Fori(1, (NBP + 1) // 4) as c:
                edges_below(c)

            def histogram(hist, first, counted, done):
                act.wait_ge(counted, NG)
                for c in range(0, T, HCHUNK):
                    w = min(HCHUNK, T - c)
                    last = nc.scalar.activation(hist[0:NBP, c:c + w], bank[first + c // HCHUNK][0:NBP, 0:w], ACT.Copy)
                    last.then_inc(done, 1)

            histogram(hist_s, 0, s["counted"], s["hist_ready"])

            def copy_out(i, to, of):
                act.wait_ge(s["pe_weights"], i)
                nc.scalar.activation(to, of, ACT.Copy).then_inc(s["act_weights"], 1)

            copy_out(1, wself_t[:, :], bank[0][:, 0:D])
            for d in range(2):
                copy_out(2 + d, wih_t[:, d, :], bank[2 + d][:, 0:3 * D])
            copy_out(4, whh_t[:, :], bank[4][:, 0:3 * D])
            copy_out(5, wcomb[:, :], bank[1][:, 0:D])
            copy_out(6, m_in[:, :], bank[5][:, 0:3 * D])
            copy_out(7, m_out[:, :], bank[6][:, 0:3 * D])
            act.wait_ge(s["pe_weights"], 9)
            nc.scalar.activation(rows_w[0:1, 0, :], bank[7][0:1, 0:3 * D], ACT.Copy)
            nc.scalar.activation(rows_w[0:1, 1, :], bank[0][0:1, 0:3 * D], ACT.Copy).then_inc(s["act_weights"], 1)

            act.wait_ge(s["flag_ready"], 1)
            unsorted = act.value_load(flag_i[0:1, 1:2], min_val=0, max_val=1)
            with act.If(unsorted):
                histogram(hist_d, 4, s["slow_counted"], s["slow_hist"])

            def hidden(g):
                act.wait_ge(s["attr_tr"], g + 1)
                need(act, s["h_ready"], 2 * g)
                nc.scalar.activation(attr_t[0:TG * A, :], bank[7][0:TG * A, 0:P], ACT.Copy).then_inc(s["attr_sb"], 1)
                for h in range(2):
                    act.wait_ge(s["h_ready"], 2 * g + h + 1)
                    need(act, s["w_ready"], 2 * g + h - 1)
                    nc.scalar.activation(ht[:, h, :], bank[h][:, :], ACT.Silu, bias=b1c[:, 0:1]).then_inc(s["silu_done"], 1)

            def edge_group(it, last=False):
                for b in range(2):
                    g = 2 * it + b
                    for h in range(2):
                        act.wait_ge(s["xj_ready"], 2 * g + h + 1)
                        need(act, s["msg_ready"], 2 * g + h - 1)
                        nc.scalar.activation(xjs[:, h, :], bank[4 + h][:, :], ACT.Copy).then_inc(s["xj_sb"], 1)
                    need(act, scattered[b], it * 16 * TG)
                    act.nop(nofuse=True)
                    nc.scalar.activation(mrow[:, b, :, D:D + 1].rearrange("p j c -> p (j c)"), src_key[:, bass.ds(g * TG, TG)], ACT.Copy).then_inc(s["key_ready"], 1)
                    nc.scalar.activation(mrow[:, b, :, D + 1:D + 2].rearrange("p j c -> p (j c)").bitcast(i32), dst_idx[:, bass.ds(g * TG, TG)], ACT.Copy).then_inc(s["key_ready"], 1)
                    if not (last and b):
                        hidden(g + 1)

            act.wait_ge(s["prepared"], 1)
            hidden(0)
            edge_group(0)
            with act.Fori(1, NG // 2 - 1) as it:
                edge_group(it)
            edge_group(NG // 2 - 1, last=True)

            regs0 = registers(act, "act_row", NS)
            act.wait_ge(s["tables_out"], 48)
            for b in range(2):
                act.wait_ge(scattered[b], 16 * TG * (NG // 2))
            act.wait_ge(s["msg_ready"], 2 * NG)

            def row_loads(it):
                offs = load_table(act, regs0, 0, it * NS, EP - U0)
                for k in range(1, NS, 2):
                    need(act, s["sum0_ready"], it * NS + k - S0 + 1)
                    act.dma_start(mtile[:, k % S0, :, :], msgs[bass.ds(offs[k], U0), :].rearrange("(p i) c -> p i c", i=2)).then_inc(mtile_in[k % S0 // 4], 16)

            row_loads(0)
            with act.Fori(1, IT0) as it:
                row_loads(it)

            def root(it, ready, done):
                act.wait_ge(ready, it + 1)
                act.nop(nofuse=True)
                nc.scalar.activation(prior[:, 1, :], prior[:, 1, :], ACT.Sqrt).then_inc(done, 1)

            def update(it, first=False):
                for i in range(2 * SB):
                    nb = 2 * SB * it + i
                    act.wait_ge(s["x_t"], nb + 1)
                    need(act, s["u_ready"], nb - 1)
                    nc.scalar.activation(uxt[:, i % 2, :], bank[i % 2][:, 0:2 * P], ACT.Copy).then_inc(s["xt_sb"], 1)
                    if i == SB - 1 and not first:
                        root(it - 1, s["u_var"], s["u_root"])

            update(0, first=True)
            with act.Fori(1, ITU) as it:
                update(it)
            root(ITU - 1, s["u_var"], s["u_root"])

            def gru(it, first=False):
                for i in range(2 * SB + 2):
                    if i == SB and not first:
                        root(it - 1, s["g_var"], s["g_root"])
                    if i < 2 * SB:
                        nb = 2 * SB * it + i
                        act.wait_ge(s["g_t"], nb + 1)
                        need(act, s["g_lin"], nb - 1)
                        nc.scalar.activation(gxt[:, i % 2, :], bank[0][:, 0:3 * P], ACT.Copy)
                        nc.scalar.activation(auxt[0:9, i % 2, :], bank[0][0:9, 3 * P:4 * P], ACT.Copy).then_inc(s["g_tsb"], 1)
                    if 1 <= i < 2 * SB + 1:
                        nb, k = 2 * SB * it + i - 1, (i - 1) % SB
                        act.wait_ge(s["g_lin"], nb + 1)
                        need(act, s["g_out"], nb - SB + 1)
                        nc.scalar.activation(gates[:, k, 0:2 * D], bank[1 + k][:, D:3 * D], ACT.Sigmoid).then_inc(s["g_gate"], 1)
                    if i >= 2:
                        nb, k = 2 * SB * it + i - 2, (i - 2) % SB
                        act.wait_ge(s["g_cand"], nb + 1)
                        nc.scalar.activation(gates[:, k, 2 * D:3 * D], gates[:, k, 2 * D:3 * D], ACT.Tanh).then_inc(s["g_tanh"], 1)

            gru(0, first=True)
            with act.Fori(1, ITU) as it:
                gru(it)
            root(ITU - 1, s["g_var"], s["g_root"])

        @block.vector
        def _(dve):
            v = nc.vector
            st = Steps(dve, s["dve_step"])
            v.memset(src_p[:, T - TG:T], PAD).then_inc(s["pads"], 1)
            v.memset(dst_p[:, T - TG:T], PAD).then_inc(s["pads"], 1)
            for t in (src_n, dst_n, next_n):
                v.memset(t[96:NQ, :], PAD).then_inc(s["pads"], 1)
            v.memset(w1pad[:, :, :], 0.0).then_inc(s["dve_weights"], 1)
            dve.wait_ge(s["pool_const"], 9)
            st.mark(v.tensor_copy(iota_row[:, :], iota_i[:, 0:P]))
            st.mark(v.tensor_copy(iota_v[:, :], iota_i))
            st.link(v.tensor_copy(iota_c[:, :], kcol_i[:, 0:1]))
            st.link(v.tensor_copy(iota_k[:, :], iota_v[:, 0:NBP + 1]))
            st.mark(v.tensor_scalar(below[:, NBP + 1:2 * (NBP + 1)], iota_v[:, 0:NBP + 1], -float(P), 0.5, ALU.mult, ALU.add))
            st.wait()
            dve.sem_inc(s["limits"], 1)

            dve.wait_ge(s["edges_in"], 16 * N_EDGES)
            st.mark(v.tensor_copy(src_key[:, :], src_p))
            st.link(v.tensor_scalar(dst_idx[:, :], dst_p, float(N - 1), None, ALU.min))
            st.mark(v.tensor_scalar(src_p, src_p, 7, None, ALU.logical_shift_right))
            st.link(v.tensor_scalar(dst_p, dst_p, 7, None, ALU.logical_shift_right))
            st.link(v.tensor_copy(blk_s, src_p))
            st.link(v.tensor_copy(blk_d, dst_p))

            def onehots(it):
                for b in range(0, 4, 2):
                    g = 4 * it + b
                    need(dve, s["counted"], g - 2)
                    v.tensor_tensor(onek[:, b:b + 2, :, 0:NBP].rearrange("p s j k -> p (s j) k"),
                                    blk_s[:, bass.ds(g * TG, 2 * TG)].rearrange("p (j o) -> p j o", o=1).to_broadcast([P, 2 * TG, NBP]),
                                    iota_k[:, 0:NBP].rearrange("p (o k) -> p o k", o=1).to_broadcast([P, 2 * TG, NBP]), ALU.is_equal).then_inc(s["blocks_ready"], 2)

            onehots(0)
            with dve.Fori(1, NG // 4) as it:
                onehots(it)

            Q = slice(0, NQ)
            pair_i = pair_n.bitcast(i32)
            st.mark(v.tensor_copy(pair_n[Q, :, 0], dst_n[Q, :]))
            st.mark(v.tensor_scalar(pair_i[Q, :, 1], src_n[Q, :], float(N - 1), None, ALU.min))
            st.link(v.tensor_tensor(tmp_n[Q, :], next_n[Q, :], dst_n[Q, :], ALU.is_lt))
            st.link(v.tensor_reduce(viol[Q, 1:2], tmp_n[Q, :], AX.X, ALU.add))
            dw = tmp_n.rearrange("p (g e) -> p g e", g=QG)
            st.link(v.tensor_scalar(tmp_n[Q, :], dst_n[Q, :], float(N - 1), None, ALU.min))
            st.mark(v.tensor_reduce(lohi[Q, 0, :], dw[Q], AX.X, ALU.min))
            st.link(v.tensor_reduce(lohi[Q, 1, :], dw[Q], AX.X, ALU.max))
            st.link(v.tensor_scalar(lohi[Q, 0, :], lohi[Q, 0, :], float(N - P), None, ALU.min))
            st.link(v.tensor_tensor(lohi[Q, 2, :], lohi[Q, 1, :], lohi[Q, 0, :], ALU.subtract))
            st.link(v.tensor_scalar(lohi[Q, 3, :], lohi[Q, 2, :], float(P), None, ALU.is_ge))
            st.link(v.tensor_reduce(viol[Q, 0:1], lohi[Q, 3, :], AX.X, ALU.add))
            dve.sem_inc(s["flags_sum"], 1)
            dve.wait_ge(s["edges_below"], NBP + 1)
            st.mark(v.tensor_scalar(src_n[Q, :], src_n[Q, :], 7, None, ALU.logical_shift_right))
            st.link(v.tensor_scalar(dst_n[Q, :], dst_n[Q, :], 7, None, ALU.logical_shift_right))
            st.mark(v.tensor_copy(rows_n[Q, :, 0, :], src_n[Q, :].rearrange("p (g e) -> p g e", g=QG)))
            st.mark(v.tensor_copy(rows_n[Q, :, 2, :], dst_n[Q, :].rearrange("p (g e) -> p g e", g=QG)))
            lo_b = lohi[Q, 0, :].rearrange("p (g o) -> p g o", o=1)
            st.link(v.tensor_tensor(dw[Q], dw[Q], lo_b.to_broadcast([NQ, QG, GE]), ALU.subtract))
            dve.wait_ge(s["flag_pe"], 1)
            st.link(v.tensor_scalar(flag_f[:, :], bank[1][:, 0:2], 0.5, None, ALU.is_gt))
            st.link(v.tensor_copy(flag_i[:, :], flag_f[:, :]))
            dve.sem_inc(s["flag_ready"], 1)
            nx = next_n.bitcast(f32).rearrange("p (g e) -> p g e", g=QG)
            for g in range(QG):
                st.link(v.tensor_tensor(nx[Q, g, :], tile_p[Q, :], dw[Q, g, :], ALU.subtract))
                st.link(v.scalar_tensor_tensor(rows_n[Q, g, 1, :], nx[Q, g, :], flag_f[Q, 0:1], dw[Q, g, :], ALU.mult, ALU.add))
            lo_t = lo_b.to_broadcast([NQ, QG, TG])
            st.link(v.tensor_tensor(lorow[Q, 0], slowrow[Q], lo_t, ALU.subtract))
            st.link(v.tensor_copy(lorow[Q, 1], lo_t))
            st.link(v.scalar_tensor_tensor(lorow_i[Q], lorow[Q, 0], flag_f[Q, 0:1], lorow[Q, 1], ALU.mult, ALU.add))
            dve.sem_inc(s["prep_out"], 1)
            dve.wait_ge(s["weights_in"], 16 * 16)
            for c in range(3):
                st.link(v.tensor_copy(b2parts[0:1, c, :], b2row[0:1, c, :]))
                if c < 2:
                    st.link(v.tensor_tensor(b2row[0:1, c + 1, :], b2row[0:1, c, :], b2parts[0:1, c, :], ALU.subtract))
            dve.sem_inc(s["dve_weights"], 1)
            v.memset(auxw[:, :], 0.0)
            v.tensor_copy(row2[0:1, 0:D], brow[0:1, 3 * D:4 * D])
            v.tensor_tensor(row2[0:1, D:3 * D], brow[0:1, D:3 * D], brow[0:1, 4 * D:6 * D], ALU.add)
            st.link(v.tensor_copy(row2[0:1, 3 * D:4 * D], brow[0:1, 6 * D:7 * D]))
            dve.wait_ge(s["pe_weights"], 8)
            st.link(v.tensor_tensor(bias0[0:1, :], bank[2][0:1, 3 * D:4 * D], brow[0:1, 0:D], ALU.add))
            dve.sem_inc(s["dve_weights"], 1)

            def running(stp, hist, a, b):
                cur, other = hist[0:NBP, :], a
                d = 1
                while d < T:
                    stp.mark(v.tensor_copy(other[:, 0:d], cur[:, 0:d]))
                    stp.link(v.tensor_tensor(other[:, d:T], cur[:, d:T], cur[:, 0:T - d], ALU.add))
                    cur, other = other, (b if other is a else a)
                    d *= 2
                return cur, other

            def first_places(stp, hist, total, spare, start, to):
                stp.link(v.tensor_tensor(spare, total, hist[0:NBP, :], ALU.subtract))
                whole = total.bitcast(i32)
                stp.link(v.tensor_scalar(whole, spare, start, None, ALU.add))
                digit = spare.bitcast(i32)
                for c in range(3):
                    stp.link(v.tensor_scalar(digit, whole, 7 * c, 127, ALU.logical_shift_right, ALU.bitwise_and))
                    stp.link(v.tensor_copy(to[:, :, c], digit))

            dve.wait_ge(s["hist_ready"], -(-T // HCHUNK))
            dve.wait_ge(s["lotab_out"], 48)
            dve.wait_ge(s["xcopy"], 32)
            sa, sb_ = sumt[0:NBP, :], sumt2[0:NBP, :]
            total, spare = running(st, hist_s, sa, sb_)
            st.link(v.tensor_copy(kcol[0:NBP, 0:1], total[:, T - 1:T]))
            dve.sem_inc(s["start_in"], 1)
            dve.wait_ge(s["start_sum"], 1)
            st.mark(v.tensor_copy(kcol[0:NBP, 2:3], bank[0][0:NBP, 0:1]))
            st.link(v.tensor_scalar(kcol[0:NBP, 8:10], bank[0][0:NBP, 3:5], -0.5, float(EP // 2), ALU.mult, ALU.add))
            st.mark(v.tensor_copy(kcol[0:NBP, 3:4], kcol[0:NBP, 8:9]))
            st.link(v.tensor_tensor(kcol[0:NBP, 1:2], kcol[0:NBP, 9:10], kcol[0:NBP, 8:9], ALU.subtract))
            first_places(st, hist_s, total, spare, kcol[0:NBP, 2:3], base3)
            for i, (U, V, blk, row) in enumerate(PASSES):
                k = 1 if row == 4 else 0
                cnt, start = kcol[0:NB, k:k + 1], kcol[0:NB, 2 + k:3 + k]
                nv, vfirst, vend, co = (kcol[0:NB, c:c + 1] for c in (4, 5, 6, 7))
                st.link(v.tensor_scalar(kcol_i[0:NB, 0:1], cnt, float(U - 1), None, ALU.add))
                st.link(v.tensor_scalar(kcol_i[0:NB, 1:2], kcol_i[0:NB, 0:1], U.bit_length() - 1, None, ALU.logical_shift_right))
                st.link(v.tensor_copy(nv, kcol_i[0:NB, 1:2]))
                dve.sem_inc(s["start_in"], 1)
                dve.wait_ge(s["start_sum"], 2 + i)
                st.link(v.tensor_copy(vfirst, bank[0][0:NB, 2:3]))
                st.link(v.tensor_tensor(vend, vfirst, nv, ALU.add))
                st.link(v.scalar_tensor_tensor(co, vfirst, -float(U), start, ALU.mult, ALU.add))
                st.link(v.tensor_scalar(coef[0:NB, :], ones[0:NB, :], co, None, ALU.mult))
                st.mark(v.tensor_scalar(ge_end[0:NB, 0:V], iota_v[0:NB, 0:V], vend, None, ALU.is_ge))
                st.link(v.tensor_scalar(ge_start[0:NB, 0:V], iota_v[0:NB, 0:V], vfirst, None, ALU.is_ge))
                st.link(v.tensor_tensor(ge_start[0:NB, 0:V], ge_start[0:NB, 0:V], ge_end[0:NB, 0:V], ALU.subtract))
                dve.sem_inc(s["start_in"], 1)
                for c in range(0, V, HCHUNK):
                    w = min(HCHUNK, V - c)
                    dve.wait_ge(s["tables_sum"], sum(-(-p[1] // HCHUNK) for p in PASSES[:i]) + c // HCHUNK + 1)
                    st.mark(v.tensor_scalar(blk[:, c:c + w], bank[c // HCHUNK][:, 0:w], float(P), None, ALU.mult))
                    if i and c == 0:
                        dve.wait_ge(s["tables_out"], 16 * i)
                    scale = float(D if row == 0 else CW)
                    st.mark(v.tensor_scalar(vrow[:, 1, c:c + w], bank[c // HCHUNK][:, 0:w], scale, None, ALU.mult))
                    st.link(v.scalar_tensor_tensor(off_f[:, c:c + w], iota_v[:, c:c + w], float(U), bank[4 + c // HCHUNK][:, 0:w], ALU.mult, ALU.add))
                    st.link(v.tensor_scalar(vrow[:, 0, c:c + w], off_f[:, c:c + w], float(EP - U), None, ALU.min))
                dve.sem_inc(s["tables_read"], 1)

            unsorted = dve.value_load(flag_i[0:1, 1:2], min_val=0, max_val=1)

            def ranks(sums_sem, sums_at, done_sem):
                for h in range(2):
                    dve.wait_ge(sums_sem, sums_at + h)
                    for k in range(4):
                        j = 4 * h + k
                        last = v.tensor_tensor_reduce(out=junk[:, j, :], in0=bank[6][:, k * P:(k + 1) * P], in1=earlier[:, :], scale=1.0,
                                                      scalar=0.0, op0=ALU.mult, op1=ALU.add, accum_out=rank[:, j:j + 1])
                    last.then_inc(done_sem, 1)

            def places(stp, b, done_sem, done_at):
                stp.link(v.scalar_tensor_tensor(posf[:, 0, :], digits[:, :, 1], float(P), digits[:, :, 0], ALU.mult, ALU.add))
                stp.link(v.scalar_tensor_tensor(posf[:, 1, :], digits[:, :, 2], float(P * P), posf[:, 0, :], ALU.mult, ALU.add))
                dve.wait_ge(done_sem, done_at)
                return v.tensor_tensor(pos[:, b, :], posf[:, 1, :], rank, ALU.add)

            with dve.If(unsorted):
                ss = Steps(dve, s["slow_rank"])

                def onehots_d(it):
                    for b in range(2):
                        g = 2 * it + b
                        need(dve, s["slow_counted"], g - 1)
                        v.tensor_tensor(onek_d[:, b, :, :], blk_d[:, bass.ds(g * TG, TG)].rearrange("p (j o) -> p j o", o=1).to_broadcast([P, TG, NBP]),
                                        iota_k[:, 0:NBP].rearrange("p (o k) -> p o k", o=1).to_broadcast([P, TG, NBP]), ALU.is_equal).then_inc(s["slow_blocks"], 1)

                onehots_d(0)
                with dve.Fori(1, NG // 2) as it:
                    onehots_d(it)
                dve.wait_ge(s["slow_hist"], -(-T // HCHUNK))
                tot, spr = running(ss, hist_d, sa, sb_)
                first_places(ss, hist_d, tot, spr, kcol[0:NBP, 3:4], base3d)
                dve.sem_inc(s["slow_pool"], 1)
                per = 4
                with dve.Fori(0, NG) as g:
                    ss.loop(g, per)
                    dve.wait_ge(s["slow_in"], g * 32 + 32)
                    v.tensor_scalar(oht[:, 0, :, :], rowsb[:, 0, 0, :].rearrange("p (e j) -> p j e", j=TG), iota_c[:, :], None, ALU.is_equal).then_inc(s["slow_oht"], 1)
                    ranks(s["slow_sums"], g * 2 + 1, s["slow_own"])
                    ss.link(v.tensor_copy(digits.rearrange("p j c -> p (j c)"), bank[7][:, P:P + 3 * TG]))
                    ss.mark(places(ss, 0, s["slow_own"], g * 2 + 2))
                    ss.wait()
                    dve.sem_inc(s["slow_pos"], 1)
                    ss.end(NG)
                    ss.it = None

            dve.wait_ge(s["tables_out"], 48)
            dve.wait_ge(s["aux_in"], 16 * 6)
            dve.wait_ge(s["window_ready"], 1)
            st.link(v.memset(mrow[:, :, :, :], 0.0))
            dve.sem_inc(s["prepared"], 1)

            ls = Steps(dve, s["reg_dve"])

            def onehots_of(it, b):
                g = 2 * it + b
                dve.wait_ge(rows_in[b], it * 16 + 16)
                need(dve, s["sums_ready"], 2 * g - 2)
                v.tensor_scalar(oht[:, b, :, :], rowsb[:, b, 0, :].rearrange("p (e j) -> p j e", j=TG), iota_c[:, :], None, ALU.is_equal).then_inc(s["oht_ready"], 1)
                need(dve, s["xj_ready"], 2 * g)
                v.tensor_scalar(wsel, rowsb[:, b, 1, :].rearrange("p (e j) -> p j e", j=TG), iota_c[:, :], None, ALU.is_equal).then_inc(s["wsel_ready"], 1)

            def edge_group(it, last=False):
                for b in range(2):
                    g = 2 * it + b
                    dve.wait_ge(s["base_ready"], g + 1)
                    need(dve, s["pos_ready"], g)
                    v.tensor_copy(digits.rearrange("p j c -> p (j c)"), bank[7][:, P:P + 3 * TG]).then_inc(s["digits_read"], 1)
                    ranks(s["sums_ready"], 2 * g + 1, s["ranked"])
                    if not (last and b):
                        onehots_of(it + b, 1 - b)
                    need(dve, scattered[b], it * 16 * TG)
                    dve.wait_ge(s["digits_read"], g + 1)
                    places(ls, b, s["ranked"], 2 * g + 2).then_inc(s["pos_ready"], 1)
                    for h in range(2):
                        dve.wait_ge(s["w_ready"], 2 * g + h + 1)
                        dve.wait_ge(s["xj_sb"], 2 * g + h + 1)
                        v.tensor_tensor(mrow[:, b, 4 * h:4 * h + 4, 0:D], bank[2 + h][:, :].rearrange("p (j d) -> p j d", j=4),
                                        xjs[:, h, :].rearrange("p (j d) -> p j d", j=4), ALU.mult).then_inc(s["msg_ready"], 1)

            onehots_of(0, 0)
            ls.loop(0, 4)
            edge_group(0)
            ls.n = 0
            with dve.Fori(1, NG // 2 - 1) as it:
                ls.loop(it, 4)
                edge_group(it)
            ls.n = 0
            ls.loop(NG // 2 - 1, 4)
            edge_group(NG // 2 - 1, last=True)
            ls.it = None

            us = Steps(dve, s["upd_step"])
            us.link(v.memset(acc_a[:, :], 0.0))
            regs = registers(dve, "dve_blk", NS)

            def keys0(it, q):
                dve.wait_ge(mtile_in[q % (S0 // 4)], (it * (NS // S0) + 4 * q // S0) * 64 + 64)
                v.tensor_tensor(local[:, q % 2], mtile[:, 4 * q % S0:4 * q % S0 + 4, :, D], blk0[:, bass.ds(it * NS + 4 * q, 4)].rearrange("p (s o) -> p s o", o=1).to_broadcast([P, 4, 2]), ALU.subtract).then_inc(s["local_ready"], 1)
                dve.wait_ge(s["local_ready"], it * (NS // 4) + q + 1)

            def onehot0(q, k):
                v.tensor_tensor(oh0[:, (4 * q + k) % S0], iota_row[:, :].rearrange("p (o n) -> p o n", o=1).to_broadcast([P, 2, P]),
                                local[:, q % 2, k, :].rearrange("p (i o) -> p i o", o=1).to_broadcast([P, 2, P]), ALU.is_equal).then_inc(s["oh0_ready"], 1)

            def sums0(it, last=False):
                dve.load(regs, blk0[0:1, bass.ds(it * NS, NS)])
                at = [dve.snap(r, min_val=0, max_val=NB * D) for r in regs]
                for q in range(NS // 4):
                    more = not (last and q == NS // 4 - 1)
                    if more:
                        keys0(it, q + 1)
                    for k in range(4):
                        if more:
                            onehot0(q + 1, k)
                        n = 4 * q + k
                        dve.wait_ge(s["sum0_ready"], it * NS + n + 1)
                        need(dve, s["add0_done"], it * NS + n)
                        a = acc_a[:, bass.ds(at[n], D)]
                        v.tensor_tensor(a, a, bank[n % 8][:, 0:D], ALU.add).then_inc(s["add0_done"], 1)

            keys0(0, 0)
            for k in range(4):
                onehot0(0, k)
            sums0(0)
            with dve.Fori(1, IT0 - 1) as it:
                sums0(it)
            sums0(IT0 - 1, last=True)

            def moments(nb, slot, y, row_ready, stat_sem):
                dve.wait_ge(row_ready, nb + 1)
                dve.nop(nofuse=True)
                v.bn_stats(slot, y).then_inc(stat_sem, 1)

            def mean_variance(it, i, slot, stat_sem, kept_sem, done_sem):
                nb = 2 * SB * it + i
                if i == 0:
                    need(dve, kept_sem, it)
                dve.wait_ge(stat_sem, nb + 1)
                dve.nop(nofuse=True)
                v.bn_aggr(some_mv[:, i, :], slot).then_inc(done_sem, 1)

            def keep_moments(it, done_sem, norm_sem, var_sem, kept_sem):
                dve.wait_ge(done_sem, 2 * SB * it + 2 * SB)
                need(dve, norm_sem, 2 * SB * it)
                v.tensor_scalar(prior[:, 1, :], some_mv[:, :, 1], EPS, None, ALU.add).then_inc(var_sem, 1)
                dve.nop(nofuse=True)
                v.tensor_copy(prior[:, 0, :], some_mv[:, :, 0]).then_inc(kept_sem, 1)

            def inverse(it, root_sem, inv_sem):
                dve.wait_ge(root_sem, it + 1)
                dve.nop(nofuse=True)
                v.reciprocal(prior[:, 1, :], prior[:, 1, :]).then_inc(inv_sem, 1)

            def normalize(it, i, acc, width, kept_sem, inv_sem, norm_sem):
                if i == 0:
                    dve.wait_ge(kept_sem, it + 1)
                    dve.wait_ge(inv_sem, it + 1)
                y = acc[:, bass.ds((2 * SB * it + i) * width, D)]
                v.tensor_scalar(y, y, prior[:, 0, i:i + 1], prior[:, 1, i:i + 1], ALU.subtract, ALU.mult).then_inc(norm_sem, 1)

            def body_before(it, i, acc, width, sems):
                root_sem, kept_sem, inv_sem, norm_sem = sems
                if i == SB:
                    inverse(it - 1, root_sem, inv_sem)
                if SB <= i < 2 * SB:
                    for k in range(2):
                        normalize(it - 1, 2 * (i - SB) + k, acc, width, kept_sem, inv_sem, norm_sem)

            def body_last(acc, width, sems):
                root_sem, kept_sem, inv_sem, norm_sem = sems
                inverse(ITU - 1, root_sem, inv_sem)
                for i in range(2 * SB):
                    normalize(ITU - 1, i, acc, width, kept_sem, inv_sem, norm_sem)

            u_sems = s["u_root"], s["u_kept"], s["u_inv"], s["u_store"]
            g_sems = s["g_root"], s["g_mv"], s["g_inv"], s["y_ready"]

            def update(it, first=False):
                for i in range(2 * SB + 2):
                    if i < 2 * SB:
                        nb = 2 * SB * it + i
                        dve.wait_ge(s["u_ready"], nb + 1)
                        v.tensor_tensor(acc_a[:, bass.ds(nb * D, D)], ustage[:, i // SB, 0, i % SB, :], bank[2 + i % 6][:, 0:D], ALU.add).then_inc(s["u_added"], 1)
                    if 1 <= i < 2 * SB + 1:
                        nb = 2 * SB * it + i - 1
                        moments(nb, stats[:, i - 1, :], acc_a[:, bass.ds(nb * D, D)], s["u_added"], s["u_stats"])
                    if not first:
                        body_before(it, i, acc_a, D, u_sems)
                    if i >= 2:
                        mean_variance(it, i - 2, stats[:, i - 2, :], s["u_stats"], s["u_kept"], s["u_moments"])
                keep_moments(it, s["u_moments"], s["u_store"], s["u_var"], s["u_kept"])

            update(0, first=True)
            with dve.Fori(1, ITU) as it:
                update(it)
            body_last(acc_a, D, u_sems)
            for c in range(3):
                us.link(v.tensor_copy(auxp[0:3, c, :], auxw[:, :]))
                if c < 2:
                    us.link(v.tensor_tensor(auxw[:, :], auxw[:, :], auxp[0:3, c, :], ALU.subtract))
            dve.sem_inc(s["aux_split"], 1)
            dve.wait_ge(s["aux_in"], 16 * 9)
            dve.wait_ge(s["x1_out"], 16 * (NB // SB))
            v.memset(grow[:, :, D:CW], 1.0).then_inc(s["grow_ones"], 1)
            us.mark(v.memset(aux9[:, :, :, 2], 1.0))
            us.mark(v.tensor_copy(ident_b[:, :], ident[:, :]))
            us.mark(v.memset(acc_b[:, :], 0.0))
            us.link(v.memset(acc_a[:, :], 0.0))
            for half, (row, blk, acc) in enumerate(((3, blk1s, acc_b), (5, blk1d, acc_a))):
                v0 = half * V1

                def sums1(it):
                    at = load_table(dve, regs, row, it * NS, NB * CW)
                    first = half * V1 // TG + it * 4

                    def onehots1(q):
                        dve.wait_ge(edge2_in[q], 16 * TG * (it + half * IT1 + 1))
                        need(dve, s["sum1_ready"], first + q - 1)
                        for k in range(TG):
                            last = v.tensor_scalar(oh1[:, q % 2, k, :], iota_row[:, :], blk[:, bass.ds(it * NS + q * TG + k, 1)], edge2[:, q * TG + k, 0:1], ALU.add, ALU.is_equal)
                        last.then_inc(s["oh1_ready"], 1)

                    onehots1(0)
                    for q in range(4):
                        if q < 3:
                            onehots1(q + 1)
                        dve.wait_ge(s["sum1_ready"], first + q + 1)
                        for k in range(TG):
                            need(dve, s["add1_done"], v0 + it * NS + q * TG + k)
                            a = acc[:, bass.ds(at[q * TG + k], CW)]
                            v.tensor_tensor(a, a, bank[q % 2 * 4 + k // 2][:, (k % 2) * 256:(k % 2) * 256 + CW], ALU.add).then_inc(s["add1_done"], 1)

                sums1(0)
                with dve.Fori(1, IT1) as it:
                    sums1(it)

                dve.wait_ge(s["add1_done"], (half + 1) * V1)
                sums = acc[:, 0:NB * CW].rearrange("p (n c) -> p n c", c=CW)
                any_row = 1 - half
                us.mark(v.tensor_scalar(aux9[:, :, :, any_row], sums[:, :, D:CW].to_broadcast([P, NB, 3]), 1.0, None, ALU.min))
                us.link(v.tensor_scalar(rcnt[:, :, :], sums[:, :, D:CW], 1.0, None, ALU.max))
                us.link(v.reciprocal(rcnt[:, :, :], rcnt[:, :, :]))
                us.link(v.tensor_tensor(sums[:, :, 0:D], sums[:, :, 0:D], rcnt[:, :, :].to_broadcast([P, NB, D]), ALU.mult))
                dve.sem_inc(s["g_mean"], 1)

            def gru(it, first=False):
                for i in range(2 * SB + 4):
                    if i < 2 * SB:
                        nb, k = 2 * SB * it + i, i % SB
                        dve.wait_ge(s["g_gate"], nb + 1)
                        v.tensor_tensor(gates[:, k, 2 * D:3 * D], gates[:, k, 0:D], bank[1 + k][:, 3 * D:4 * D], ALU.mult).then_inc(s["g_mult"], 1)
                        v.scalar_tensor_tensor(keep[:, k, :], gates[:, k, D:2 * D], 1.0, gstage[:, i // SB, 2, k, :], ALU.add, ALU.mult).then_inc(s["g_kept"], 1)
                        dve.wait_ge(s["g_mult"], nb + 1)
                        v.tensor_tensor(gates[:, k, 2 * D:3 * D], gates[:, k, 2 * D:3 * D], bank[1 + k][:, 0:D], ALU.add).then_inc(s["g_cand"], 1)
                    if 2 <= i < 2 * SB + 2:
                        nb, k = 2 * SB * it + i - 2, (i - 2) % SB
                        dve.wait_ge(s["g_tanh"], nb + 1)
                        v.scalar_tensor_tensor(gates[:, k, 0:D], gates[:, k, D:2 * D], 1.0, gates[:, k, 2 * D:3 * D], ALU.subtract, ALU.mult).then_inc(s["g_part"], 1)
                    if 3 <= i < 2 * SB + 3:
                        nb = 2 * SB * it + i - 3
                        moments(nb, gstats[:, i - 3, :], acc_b[:, bass.ds(nb * CW, D)], s["g_out"], s["g_stats"])
                    if 2 <= i < 2 * SB + 2:
                        nb, k = 2 * SB * it + i - 2, (i - 2) % SB
                        dve.wait_ge(s["g_kept"], nb + 1)
                        dve.wait_ge(s["g_part"], nb + 1)
                        v.tensor_tensor(acc_b[:, bass.ds(nb * CW, D)], keep[:, k, :], gates[:, k, 0:D], ALU.subtract).then_inc(s["g_out"], 1)
                    if not first:
                        body_before(it, i, acc_b, CW, g_sems)
                    if i >= 4:
                        mean_variance(it, i - 4, gstats[:, i - 4, :], s["g_stats"], s["g_mv"], s["g_moments"])
                keep_moments(it, s["g_moments"], s["y_ready"], s["g_var"], s["g_mv"])

            gru(0, first=True)
            with dve.Fori(1, ITU) as it:
                gru(it)
            body_last(acc_b, CW, g_sems)

        @block.tensor
        def _(pe):
            mm, tr = nc.tensor.matmul, nc.tensor.transpose
            gb = HCHUNK // TG

            def counts(first, onehot, slots, ready, done):
                for c in range(-(-T // HCHUNK)):
                    with pe.Fori(c * gb // slots, min((c + 1) * gb, NG) // slots) as it:
                        for b in range(slots):
                            g = slots * it + b
                            pe.wait_ge(ready, g + 1)
                            for j in range(TG):
                                last = mm(bank[first + c][0:NBP, bass.ds(g * TG + j - c * HCHUNK, 1)], onehot[:, b, j, 0:NBP], ones_b[:, 0:1], start=True, stop=True)
                            last.then_inc(done, 1)

            pe.wait_ge(s["pool_const"], 2)
            counts(0, onek, 4, s["blocks_ready"], s["counted"])
            pe.wait_ge(s["hist_ready"], -(-T // HCHUNK))
            pe.wait_ge(s["weights_in"], 16 * 16)
            pe.wait_ge(s["pool_const"], 5)
            tr(bank[0][:, 0:D], wself_n[:, :], ident[:, :]).then_inc(s["pe_weights"], 1)
            for d in range(2):
                for c, at in ((2, 0), (0, 1), (1, 2)):
                    last = tr(bank[2 + d][:, at * D:(at + 1) * D], wih_n[:, c, d * D:(d + 1) * D], ident[:, :])
                last.then_inc(s["pe_weights"], 1)
            for c in range(3):
                last = tr(bank[4][:, c * D:(c + 1) * D], whh_n[:, c, :], ident[:, :])
            last.then_inc(s["pe_weights"], 1)
            pe.wait_ge(s["act_weights"], 3)
            mm(bank[1][:, 0:D], wself_t[:, :], wtop[:, :], start=True, stop=True).then_inc(s["pe_weights"], 1)
            mm(bank[5][:, 0:3 * D], win_n[:, :], wih_t[:, 0, :], start=True, stop=True).then_inc(s["pe_weights"], 1)
            mm(bank[6][:, 0:3 * D], wout_n[:, :], wih_t[:, 1, :], start=True, stop=True).then_inc(s["pe_weights"], 1)
            mm(bank[2][0:1, 3 * D:4 * D], cols[:, 0:1], wtop[:, :], start=True, stop=True).then_inc(s["pe_weights"], 1)
            mm(bank[7][0:1, 0:3 * D], cols[:, 1:2], wih_t[:, 0, :], start=True, stop=True)
            mm(bank[0][0:1, 0:3 * D], cols[:, 2:3], wih_t[:, 1, :], start=True, stop=True).then_inc(s["pe_weights"], 1)
            pe.wait_ge(s["act_weights"], 8)
            pe.wait_ge(s["flags_sum"], 1)
            mm(bank[1][:, 0:2], ones[0:NQ, :], viol[0:NQ, :], start=True, stop=True).then_inc(s["flag_pe"], 1)
            pe.wait_ge(s["start_in"], 1)
            pe.wait_ge(s["edges_below"], NBP + 1)
            for k in range(2):
                mm(bank[0][0:NBP, 3 + k:4 + k], below[0:NQ, k:k + NBP], ones[0:NQ, 0:1], start=True, stop=True)
            mm(bank[0][0:NBP, 0:1], tri[0:NBP, 0:NBP], kcol[0:NBP, 0:1], start=True, stop=True).then_inc(s["start_sum"], 1)
            for i, (U, V, _, row) in enumerate(PASSES):
                pe.wait_ge(s["start_in"], 2 * i + 2)
                if i:
                    pe.wait_ge(s["tables_read"], i)
                mm(bank[0][0:NB, 2:3], tri[0:NB, 0:NB], kcol[0:NB, 4:5], start=True, stop=True).then_inc(s["start_sum"], 1)
                pe.wait_ge(s["start_in"], 2 * i + 3)
                for c in range(0, V, HCHUNK):
                    w = min(HCHUNK, V - c)
                    mm(bank[c // HCHUNK][:, 0:w], ones[0:NB, :], ge_end[0:NB, c:c + w], start=True, stop=True)
                    mm(bank[4 + c // HCHUNK][:, 0:w], coef[0:NB, :], ge_start[0:NB, c:c + w], start=True, stop=True).then_inc(s["tables_sum"], 1)
            pe.wait_ge(s["tables_read"], 3)

            def tile_sums(h, onehot):
                for k in range(4):
                    j = 4 * h + k
                    last = mm(bank[6][:, k * P:(k + 1) * P], onehot[0:NBP, j, :], onehot[0:NBP, j, :], start=True, stop=True)
                return last

            def first_of(onehot, base, g):
                for j in range(TG):
                    last = mm(bank[7][:, P + 3 * j:P + 3 * j + 3], onehot[0:NBP, j, :],
                              base[:, bass.ds(g * TG + j, 1), :].rearrange("k t c -> k (t c)"), start=True, stop=True)
                return last

            pe.wait_ge(s["flag_ready"], 1)
            unsorted = pe.value_load(flag_i[0:1, 1:2], min_val=0, max_val=1)
            with pe.If(unsorted):
                counts(4, onek_d, 2, s["slow_blocks"], s["slow_counted"])
                pe.wait_ge(s["slow_hist"], -(-T // HCHUNK))
                with pe.Fori(0, NG) as g:
                    pe.wait_ge(s["slow_oht"], g + 1)
                    first_of(oht[:, 0], base3d, g)
                    for h in range(2):
                        need(pe, s["slow_own"], 2 * g + h if h else 0)
                        tile_sums(h, oht[:, 0]).then_inc(s["slow_sums"], 1)

            def attributes(it, b):
                g = 2 * it + b
                pe.wait_ge(attr_in[b], it * 16 + 16)
                need(pe, s["digits_read"], g)
                pe.nop(nofuse=True)
                tr(bank[7][0:TG * A, 0:P], attr[:, b, :], ident[:, :]).then_inc(s["attr_tr"], 1)

            def hidden(g, h):
                if h == 0:
                    pe.wait_ge(s["attr_sb"], g + 1)
                need(pe, s["silu_done"], 2 * g + h - 1)
                for k in range(4):
                    last = mm(bank[h][:, k * P:(k + 1) * P], w1pad[:, 4 * h + k, :], attr_t[0:TG * A, :], start=True, stop=True)
                last.then_inc(s["h_ready"], 1)

            def weights(g, h):
                pe.wait_ge(s["silu_done"], 2 * g + h + 1)
                need(pe, s["msg_ready"], 2 * g + h - 1)
                for k in range(4):
                    o = bank[2 + h][:, k * P:(k + 1) * P]
                    mm(o, ht[:, h, k * P:(k + 1) * P], w2s[:, :], start=True, stop=False)
                    last = mm(o, ones_b[0:3, :], b2s[:, :], start=False, stop=True)
                last.then_inc(s["w_ready"], 1)

            def edge_group(it, last_one=False):
                for b in range(2):
                    g = 2 * it + b
                    pe.wait_ge(s["oht_ready"], g + 1)
                    need(pe, s["attr_sb"], g + 1)
                    first_of(oht[:, b], base3, g).then_inc(s["base_ready"], 1)
                    for h in range(2):
                        need(pe, s["ranked"], 2 * g + h)
                        tile_sums(h, oht[:, b]).then_inc(s["sums_ready"], 1)
                        if h == 0:
                            pe.wait_ge(s["wsel_ready"], g + 1)
                            pe.wait_ge(win_in[b], it * 16 + 16)
                        need(pe, s["xj_sb"], 2 * g + h - 1)
                        for k in range(4):
                            j = 4 * h + k
                            last = mm(bank[4 + h][:, k * P:(k + 1) * P], wsel[:, j, :],
                                      win[:, b, bass.ds(wide * j, 1), :].rearrange("p o d -> p (o d)"), start=True, stop=True)
                        last.then_inc(s["xj_ready"], 1)
                    more = not (last_one and b)
                    if more:
                        if last_one:
                            pe.wait_ge(attr_in[1], (NG // 2 - 1) * 16 + 16 * (2 + 2 * (LJ > 0)))
                        attributes(it + b, 1 - b)
                    for h in range(2):
                        weights(g, h)
                        if more:
                            hidden(g + 1, h)

            pe.wait_ge(s["prepared"], 1)
            pe.wait_ge(s["w1_in"], 16 * TG)
            pe.wait_ge(s["aux_in"], 16 * 6)
            wide = pe.value_load(flag_i[0:1, 0:1], min_val=0, max_val=1)
            attributes(0, 0)
            for h in range(2):
                hidden(0, h)
            edge_group(0)
            with pe.Fori(1, NG // 2 - 1) as it:
                edge_group(it)
            edge_group(NG // 2 - 1, last_one=True)

            def sums0(it):
                for k in range(NS):
                    pe.wait_ge(s["oh0_ready"], it * NS + k + 1)
                    need(pe, s["add0_done"], it * NS + k - 7)
                    for i in range(2):
                        last = mm(bank[k % 8][:, 0:D], oh0[:, k % S0, i, :], mtile[:, k % S0, i, 0:D], start=(i == 0), stop=(i == 1))
                    last.then_inc(s["sum0_ready"], 1)

            pe.wait_ge(s["msg_ready"], 2 * NG)
            sums0(0)
            with pe.Fori(1, IT0) as it:
                sums0(it)

            pe.wait_ge(s["add0_done"], V0)

            def update(it):
                for i in range(2 * SB + 1):
                    if i < 2 * SB:
                        nb, h = 2 * SB * it + i, i // SB
                        if i % SB == 0:
                            pe.wait_ge(x_staged[h], it * 32 + 32)
                        need(pe, s["xt_sb"], nb - 1)
                        for c in range(2):
                            last = tr(bank[i % 2][:, c * P:(c + 1) * P], ustage[:, h, c, i % SB, :], ident[:, :])
                        last.then_inc(s["x_t"], 1)
                    if i >= 1:
                        k = i - 1
                        nb, o = 2 * SB * it + k, bank[2 + k % 6][:, 0:D]
                        pe.wait_ge(s["xt_sb"], nb + 1)
                        need(pe, s["u_added"], nb - (5 if k >= 2 else 1))
                        mm(o, uxt[:, k % 2, 0:P], wcomb[:, :], start=True, stop=False)
                        mm(o, uxt[:, k % 2, P:2 * P], wbot[:, :], start=False, stop=False)
                        mm(o, ones[0:1, :], bias0[0:1, :], start=False, stop=True).then_inc(s["u_ready"], 1)

            update(0)
            with pe.Fori(1, ITU) as it:
                update(it)

            pe.wait_ge(s["u_store"], NB)
            for half in range(2):
                def sums1(it):
                    for q in range(4):
                        pe.wait_ge(s["oh1_ready"], half * V1 // TG + it * 4 + q + 1)
                        pe.wait_ge(gathered[q], 16 * TG * (it + half * IT1 + 1))
                        need(pe, s["add1_done"], half * V1 + it * NS + (q - 1) * TG)
                        for k in range(TG):
                            last = mm(bank[q % 2 * 4 + k // 2][:, (k % 2) * 256:(k % 2) * 256 + CW], oh1[:, q % 2, k, :], grow[:, q * TG + k, :], start=True, stop=True)
                        last.then_inc(s["sum1_ready"], 1)

                sums1(0)
                with pe.Fori(1, IT1) as it:
                    sums1(it)

            pe.wait_ge(s["g_mean"], 2)

            def gru(it):
                for i in range(2 * SB + 1):
                    if i < 2 * SB:
                        nb, h = 2 * SB * it + i, i // SB
                        if i % SB == 0:
                            pe.wait_ge(h_staged[h], it * 48 + 48)
                        need(pe, s["g_tsb"], nb)
                        for c in range(3):
                            tr(bank[0][:, c * P:(c + 1) * P], gstage[:, h, c, i % SB, :], ident[:, :])
                        mm(bank[0][0:9, 3 * P:4 * P], aux9[:, bass.ds(nb, 1), :, :].rearrange("p n c r -> p (n c r)"), ident_b[:, :], start=True, stop=True).then_inc(s["g_t"], 1)
                    if i >= 1:
                        k = i - 1
                        nb, o = 2 * SB * it + k, bank[1 + k % SB]
                        pe.wait_ge(s["g_tsb"], nb + 1)
                        need(pe, s["g_cand"], nb - SB + 1)
                        mm(o[:, :], auxt[0:9, k % 2, :], auxw9[:, :], start=True, stop=False)
                        mm(o[:, 0:3 * D], gxt[:, k % 2, 0:P], m_in[:, :], start=False, stop=False)
                        mm(o[:, 0:3 * D], gxt[:, k % 2, P:2 * P], m_out[:, :], start=False, stop=False)
                        mm(o[:, D:4 * D], gxt[:, k % 2, 2 * P:3 * P], whh_t[:, :], start=False, stop=True).then_inc(s["g_lin"], 1)

            gru(0)
            with pe.Fori(1, ITU) as it:
                gru(it)


_INS = ['x', 'src', 'dst', 'edge_attr_8', 'L0_gnn_W1', 'L0_gnn_b1', 'L0_gnn_W2', 'L0_gnn_b2', 'L0_gnn_Wself', 'L0_gnn_bself',
        'L0_gnn_Wcat', 'L0_gnn_bcat', 'L1_gnn_W_in', 'L1_gnn_b_in', 'L1_gnn_W_out', 'L1_gnn_b_out', 'L1_gnn_w_ih', 'L1_gnn_w_hh',
        'L1_gnn_b_ih', 'L1_gnn_b_hh']


def kernel(**inputs):
    import numpy as _np
    import concourse.bacc as _bacc
    from concourse import mybir as _mybir
    from concourse.bass_utils import run_bass_kernel_spmd as _run

    nc = _bacc.Bacc("TRN2", target_bir_lowering=False, num_devices=1)
    arrays, args = {}, []
    for name in _INS:
        a = _np.ascontiguousarray(inputs[name])
        arrays[f"in_{name}_dram"] = a
        args.append(nc.dram_tensor(f"in_{name}_dram", a.shape, _mybir.dt.from_np(a.dtype), kind="ExternalInput").ap())
    out = nc.dram_tensor("out_0_dram", (N, D), _mybir.dt.float32, kind="ExternalOutput").ap()
    gnn_kernel(nc, *args, out)
    return _run(nc, [arrays], core_ids=[0]).results[0]["out_0_dram"]
```
